# Optimizing a Trainium2 kernel written in Bass

```python
import numpy as np
import jax
import jax.numpy as jnp

def _softmax(x, axis=-1):
    return jax.nn.softmax(x, axis=axis)

def _gelu(x):
    return jax.nn.gelu(x, approximate=True)

def _silu(x):
    return jax.nn.silu(x)

def _sigmoid(x):
    return jax.nn.sigmoid(x)

def _layernorm(x, axis=-1, eps=1e-05):
    m = jnp.mean(x, axis=axis, keepdims=True)
    v = jnp.var(x, axis=axis, keepdims=True)
    return (x - m) / jnp.sqrt(v + eps)

def _scatter_add(tgt, idx, src, axis=0):
    return tgt.at[idx].add(src)

def _segment_sum(src, seg, n):
    return jax.ops.segment_sum(src, seg, n)
kernel_name = 'mk_cond_seq_d2_seqx_r2_ff6ef1'

def setup_inputs(seed: int=0):
    np.random.seed(seed)
    _w = jnp.asarray

    def _rec_inputs():
        import jax
        import jax.numpy as jnp
        _rk = jax.random.key(seed)
        x = 1.648e-05 + 1 * jax.random.normal(jax.random.fold_in(_rk, 1), (2, 2048, 576), jnp.float32)
        _lenS = 2048 - jax.random.randint(jax.random.fold_in(_rk, 7), (2,), 0, max(1, 2048 // 4) + 1, jnp.int32)
        _lenS2 = 2048 - jax.random.randint(jax.random.fold_in(_rk, 8), (2,), 0, max(1, 2048 // 4) + 1, jnp.int32)
        cond_1152 = 0.00914911 + 1.00357 * jax.random.normal(jax.random.fold_in(_rk, 11), (2, 576), jnp.float32)
        return (x, cond_1152)
    x, cond_1152 = _rec_inputs()

    def _L0_cond_setup():
        import jax, jax.numpy as jnp
        import numpy as np
        B, N, D = (8, 512, 576)
        H = 16
        HD = D // H
        HID = 4 * D
        EPS = 1e-06

        def _ln(x):
            mu = jnp.mean(x, axis=-1, keepdims=True)
            var = jnp.mean(jnp.square(x - mu), axis=-1, keepdims=True)
            return (x - mu) * jax.lax.rsqrt(var + EPS)

        def _modulate(x, shift, scale):
            return x * (1.0 + scale[:, None, :]) + shift[:, None, :]

        def _attn(x, w_qkv, b_qkv, w_proj, b_proj):
            b, n, d = x.shape
            qkv = (x @ w_qkv + b_qkv).reshape(b, n, 3, H, HD)
            q = qkv[:, :, 0].transpose(0, 2, 1, 3)
            k = qkv[:, :, 1].transpose(0, 2, 1, 3)
            v = qkv[:, :, 2].transpose(0, 2, 1, 3)
            scores = jnp.einsum('bhnd,bhmd->bhnm', q, k) * HD ** (-0.5)
            attn = jax.nn.softmax(scores, axis=-1)
            out = jnp.einsum('bhnm,bhmd->bhnd', attn, v)
            out = out.transpose(0, 2, 1, 3).reshape(b, n, d)
            return out @ w_proj + b_proj
        key = jax.random.key(seed)
        ks = jax.random.split(key, 12)
        s = 0.02
        return {'x': jax.random.normal(ks[0], (B, N, D), jnp.float32), 't_emb': jax.random.normal(ks[1], (B, D), jnp.float32), 'w_qkv': jax.random.normal(ks[2], (D, 3 * D), jnp.float32) * s, 'b_qkv': jax.random.normal(ks[3], (3 * D,), jnp.float32) * s, 'w_proj': jax.random.normal(ks[4], (D, D), jnp.float32) * s, 'b_proj': jax.random.normal(ks[5], (D,), jnp.float32) * s, 'w_fc1': jax.random.normal(ks[6], (D, HID), jnp.float32) * s, 'b_fc1': jax.random.normal(ks[7], (HID,), jnp.float32) * s, 'w_fc2': jax.random.normal(ks[8], (HID, D), jnp.float32) * s, 'b_fc2': jax.random.normal(ks[9], (D,), jnp.float32) * s, 'w_ada': jax.random.normal(ks[10], (D, 6 * D), jnp.float32) * s, 'b_ada': jax.random.normal(ks[11], (6 * D,), jnp.float32) * s}
    _L0_cond_all = _L0_cond_setup()
    _L0_cond_in = {k: v for k, v in _L0_cond_all.items() if k in ('w_qkv', 'b_qkv', 'w_proj', 'b_proj', 'w_fc1', 'b_fc1', 'w_fc2', 'b_fc2', 'w_ada', 'b_ada')}
    del _L0_cond_all

    def _L1_cond_setup():
        import jax, jax.numpy as jnp
        import numpy as np
        from jax.scipy.linalg import expm
        N, D, COND_DIM = (576, 64, 576)
        B, T = (16, 512)

        def _rotation(cond, W, b):
            v = jax.nn.silu(cond) @ W.T + b
            iu, ju = jnp.triu_indices(D, k=1)
            A = jnp.zeros((cond.shape[0], D, D), dtype=v.dtype)
            A = A.at[:, iu, ju].set(v).at[:, ju, iu].set(-v)
            return expm(A)
        key = jax.random.key(seed)
        k1, k2, k3, k4, k5 = jax.random.split(key, 5)
        x = jax.random.normal(k1, (B, T, N), dtype=jnp.float32)
        cond = jax.random.normal(k2, (B, COND_DIM), dtype=jnp.float32)
        P = jax.random.normal(k3, (N, D), dtype=jnp.float32)
        n_skew = D * (D - 1) // 2
        bound = 1.0 / np.sqrt(COND_DIM)
        W = jax.random.uniform(k4, (n_skew, COND_DIM), minval=-bound, maxval=bound, dtype=jnp.float32)
        b = jax.random.uniform(k5, (n_skew,), minval=-bound, maxval=bound, dtype=jnp.float32)
        return {'x': x, 'cond': cond, 'P': P, 'W': W, 'b': b}
    _L1_cond_all = _L1_cond_setup()
    _L1_cond_in = {k: v for k, v in _L1_cond_all.items() if k in ('P', 'W', 'b')}
    del _L1_cond_all
    return {'x': x, 'cond_1152': cond_1152, 'L0_cond_w_qkv': _L0_cond_in['w_qkv'], 'L0_cond_b_qkv': _L0_cond_in['b_qkv'], 'L0_cond_w_proj': _L0_cond_in['w_proj'], 'L0_cond_b_proj': _L0_cond_in['b_proj'], 'L0_cond_w_fc1': _L0_cond_in['w_fc1'], 'L0_cond_b_fc1': _L0_cond_in['b_fc1'], 'L0_cond_w_fc2': _L0_cond_in['w_fc2'], 'L0_cond_b_fc2': _L0_cond_in['b_fc2'], 'L0_cond_w_ada': _L0_cond_in['w_ada'], 'L0_cond_b_ada': _L0_cond_in['b_ada'], 'L1_cond_P': _L1_cond_in['P'], 'L1_cond_W': _L1_cond_in['W'], 'L1_cond_b': _L1_cond_in['b']}

def reference(x, cond_1152, L0_cond_w_qkv, L0_cond_b_qkv, L0_cond_w_proj, L0_cond_b_proj, L0_cond_w_fc1, L0_cond_b_fc1, L0_cond_w_fc2, L0_cond_b_fc2, L0_cond_w_ada, L0_cond_b_ada, L1_cond_P, L1_cond_W, L1_cond_b):
    import jax
    import jax.numpy as jnp

    def _L0_cond_ref(x, t_emb, w_qkv, b_qkv, w_proj, b_proj, w_fc1, b_fc1, w_fc2, b_fc2, w_ada, b_ada):
        import jax, jax.numpy as jnp
        import numpy as np
        B, N, D = (8, 512, 576)
        H = 16
        HD = D // H
        HID = 4 * D
        EPS = 1e-06

        def _ln(x):
            mu = jnp.mean(x, axis=-1, keepdims=True)
            var = jnp.mean(jnp.square(x - mu), axis=-1, keepdims=True)
            return (x - mu) * jax.lax.rsqrt(var + EPS)

        def _modulate(x, shift, scale):
            return x * (1.0 + scale[:, None, :]) + shift[:, None, :]

        def _attn(x, w_qkv, b_qkv, w_proj, b_proj):
            b, n, d = x.shape
            qkv = (x @ w_qkv + b_qkv).reshape(b, n, 3, H, HD)
            q = qkv[:, :, 0].transpose(0, 2, 1, 3)
            k = qkv[:, :, 1].transpose(0, 2, 1, 3)
            v = qkv[:, :, 2].transpose(0, 2, 1, 3)
            scores = jnp.einsum('bhnd,bhmd->bhnm', q, k) * HD ** (-0.5)
            attn = jax.nn.softmax(scores, axis=-1)
            out = jnp.einsum('bhnm,bhmd->bhnd', attn, v)
            out = out.transpose(0, 2, 1, 3).reshape(b, n, d)
            return out @ w_proj + b_proj
        ada = jax.nn.silu(t_emb) @ w_ada + b_ada
        shift_a, scale_a, gate_a, shift_f, scale_f, gate_f = jnp.split(ada, 6, axis=-1)
        x = x + gate_a[:, None, :] * _attn(_modulate(_ln(x), shift_a, scale_a), w_qkv, b_qkv, w_proj, b_proj)
        h = _modulate(_ln(x), shift_f, scale_f)
        h = jax.nn.gelu(h @ w_fc1 + b_fc1, approximate=True) @ w_fc2 + b_fc2
        return x + gate_f[:, None, :] * h

    def _L1_cond_ref(x, cond, P, W, b):
        import jax, jax.numpy as jnp
        import numpy as np
        from jax.scipy.linalg import expm
        N, D, COND_DIM = (576, 64, 576)
        B, T = (16, 512)

        def _rotation(cond, W, b):
            v = jax.nn.silu(cond) @ W.T + b
            iu, ju = jnp.triu_indices(D, k=1)
            A = jnp.zeros((cond.shape[0], D, D), dtype=v.dtype)
            A = A.at[:, iu, ju].set(v).at[:, ju, iu].set(-v)
            return expm(A)
        U, _ = jnp.linalg.qr(P)
        R = _rotation(cond, W, b)
        z = jnp.einsum('btn,nd->btd', x, U)
        z_rot = jnp.einsum('btd,bde->bte', z, R)
        x_rot = x + jnp.einsum('btd,nd->btn', z_rot - z, U)
        return x_rot
    x = _L0_cond_ref(x, cond_1152, L0_cond_w_qkv, L0_cond_b_qkv, L0_cond_w_proj, L0_cond_b_proj, L0_cond_w_fc1, L0_cond_b_fc1, L0_cond_w_fc2, L0_cond_b_fc2, L0_cond_w_ada, L0_cond_b_ada)
    x = _L1_cond_ref(x, cond_1152, L1_cond_P, L1_cond_W, L1_cond_b)
    return x

_drawn_inputs = setup_inputs


def setup_inputs(seed=0):
    import zlib

    import numpy as np

    out = dict(_drawn_inputs(seed))
    spreads = {}
    factors = {'L0_cond_w_qkv': 2.931,
     'L0_cond_b_qkv': 8.0,
     'L0_cond_w_proj': 3.018,
     'L0_cond_b_proj': 8.0,
     'L0_cond_b_fc1': 8.0,
     'L0_cond_b_fc2': 8.0,
     'L0_cond_b_ada': 8.0}
    for name, (base, spread) in spreads.items():
        noise = np.random.default_rng([zlib.crc32(name.encode()), seed]).standard_normal(out[name].shape)
        drawn = base * np.exp(spread * noise) if base else spread * noise
        out[name] = jnp.asarray(drawn.astype(out[name].dtype))
    for name, factor in factors.items():
        out[name] = (out[name] * factor).astype(out[name].dtype)
    return out
```

```python
from contextlib import ExitStack

import concourse.bass as bass
from concourse import mybir

F32 = mybir.dt.float32
F32R = mybir.dt.float32r
ALU = mybir.AluOpType
ACT = mybir.ActivationFunctionType
AX = mybir.AxisListType

P = 128
B, T, D = 2, 2048, 576
H, HD = 16, 36
HID = 4 * D
RD = 64
SKEW = RD * (RD - 1) // 2
BLK = 512
TPB = BLK // P
NBLK = B * T // BLK
BPB = T // BLK
KC = 5
HALF = D // 2
FT = HID // P
NH = B * H
KT = T // P
QKT = 2 * D // P
LN_EPS = 1e-6
SECTIONS = 6
SHIFT_A, SCALE_A, GATE_A, SHIFT_F, SCALE_F, GATE_F = range(SECTIONS)


def rows(c):
    return min(P, D - c * P)


class Chain:

    def __init__(self, eng, sem, base=0):
        self.eng, self.sem, self.base, self.n = eng, sem, base, 0

    def mark(self, ins):
        ins.then_inc(self.sem, 1)
        self.n += 1

    def wait(self):
        self.eng.wait_ge(self.sem, self.base + self.n)

    def do(self, ins):
        self.mark(ins)
        self.wait()


class Counts:

    def __init__(self, sem, names, credited, credit=1):
        self.sems = {n: sem(n) for n in names}
        self.credit = {n: credit * (n in credited) for n in names}

    def __getitem__(self, name):
        return self.sems[name]

    def wait(self, eng, name, count):
        eng.wait_ge(self.sems[name], count + self.credit[name])

    def give(self, eng, *names):
        for n in names:
            eng.sem_inc(self.sems[n], self.credit[n])


def load_chunked(eng, dst, src, sem):
    full = (KC - 1) * P
    eng.dma_start(dst[:, 0:KC - 1, :], src[0:full, :].rearrange("(c p) n -> p c n", p=P)).then_inc(sem, 16)
    eng.dma_start(dst[0:D - full, KC - 1, :], src[full:D, :]).then_inc(sem, 16)


def load_columns(eng, dst, src, sem):
    full = (KC - 1) * P
    eng.dma_start(dst[:, 0:KC - 1], src[0:full].rearrange("(c p) -> p c", p=P)).then_inc(sem, 16)
    eng.dma_start(dst[0:D - full, KC - 1:KC], src[full:D].rearrange("(p a) -> p a", a=1)).then_inc(sem, 16)


def row(v):
    return v.rearrange("(a n) -> a n", a=1)


def conditioning(nc, io, g):
    with ExitStack() as ctx:
        sb = lambda name, shape, dt=F32: ctx.enter_context(nc.sbuf_tensor(name, shape, dt))
        sem = lambda name: ctx.enter_context(nc.semaphore(name))
        wa = sb("w_ada_sb", [P, KC, SECTIONS * D])
        condT = sb("condT", [P, KC, B])
        siluT = sb("siluT", [P, KC, B])
        badaT = sb("badaT", [P, SECTIONS, KC])
        w2 = sb("w2_raw", [P, FT, D])
        w2h = sb("w2_hi", [P, FT // 2, D], F32R)
        w2l = sb("w2_lo", [P, FT // 2, D], F32R)
        ps = ctx.enter_context(nc.psum_tensor("ps_ada", [P, SECTIONS, KC, B], F32))
        cond_in, bada_in, w2_in = sem("cond_in"), sem("bada_in"), sem("w2_in")
        wa_in = [sem(f"wa_in{s}") for s in range(SECTIONS)]
        silu_ready, ada_ready, mod_done = sem("silu_ready"), sem("ada_ready"), sem("mod_done")
        ident_zero, ident_ready = sem("ident_zero"), sem("ident_ready")
        hi_ready, lo_ready, w2_out = sem("w2_hi_ready"), sem("w2_lo_ready"), sem("w2_out")
        modv, ident = g["modv"], g["ident"]
        block = ctx.enter_context(nc.Block())

        @block.sync
        def _(sp):
            for b in range(B):
                load_columns(sp, condT[:, :, b], io["cond_1152"][b, :], cond_in)
            full = (KC - 1) * P
            bsec = io["L0_cond_b_ada"].rearrange("(s f) -> s f", s=SECTIONS)
            for s in range(SECTIONS):
                load_columns(sp, badaT[:, s, :], bsec[s, :], bada_in)
            for s in range(SECTIONS):
                load_chunked(sp, wa[:, :, s * D:(s + 1) * D], io["L0_cond_w_ada"][:, s * D:(s + 1) * D], wa_in[s])
            sp.dma_start(w2[:, :, :], io["L0_cond_w_fc2"].rearrange("(f p) n -> p f n", p=P)).then_inc(w2_in, 16)
            half = FT // 2
            for k in range(2):
                sp.wait_ge(hi_ready, k + 1)
                sp.wait_ge(lo_ready, k + 1)
                sp.dma_start(g["w2_split"][:, k * half:(k + 1) * half, 0, :], w2h[:, :, :].bitcast(F32)).then_inc(w2_out, 16)
                sp.dma_start(g["w2_split"][:, k * half:(k + 1) * half, 1, :], w2l[:, :, :].bitcast(F32)).then_inc(w2_out, 16)
                sp.wait_ge(w2_out, 32 * (k + 1))

        @block.gpsimd
        def _(pool):
            pool.memset(ident[:, :], 0.0).then_inc(ident_zero, 1)
            pool.wait_ge(ident_zero, 1)
            pool.affine_select(out=ident[:, :], in_=ident[:, :], compare_op=ALU.not_equal, fill=1.0,
                               base=0, pattern=[[-1, P]], channel_multiplier=1).then_inc(ident_ready, 1)

        @block.scalar
        def _(act):
            act.wait_ge(cond_in, 64)
            for r, c0, c1 in ((P, 0, KC - 1), (rows(KC - 1), KC - 1, KC)):
                act.activation(siluT[0:r, c0:c1, :], condT[0:r, c0:c1, :], ACT.Silu).then_inc(silu_ready, 1)
            act.wait_ge(w2_in, 16)
            for k in range(2):
                if k:
                    act.wait_ge(w2_out, 32 * k)
                act.activation(w2h[:, :, :], w2[:, k * (FT // 2):(k + 1) * (FT // 2), :], ACT.Copy).then_inc(hi_ready, 1)

        @block.tensor
        def _(pe):
            pe.wait_ge(silu_ready, 2)
            for s in range(SECTIONS):
                pe.wait_ge(wa_in[s], 32)
                for m in range(KC):
                    for c in range(KC):
                        last = pe.matmul(ps[0:rows(m), s, m, :],
                                         wa[0:rows(c), c, s * D + m * P:s * D + m * P + rows(m)],
                                         siluT[0:rows(c), c, :], start=(c == 0), stop=(c == KC - 1))
            last.then_inc(ada_ready, 1)

        @block.vector
        def _(dve):
            dve.wait_ge(bada_in, 32 * SECTIONS)
            dve.wait_ge(ada_ready, 1)
            parts = ((P, 0, KC - 1), (rows(KC - 1), KC - 1, KC))
            for r, c0, c1 in parts:
                for b in range(B):
                    dve.tensor_tensor(modv[0:r, b, :, c0:c1], ps[0:r, :, c0:c1, b], badaT[0:r, :, c0:c1],
                                      ALU.add).then_inc(mod_done, 1)
            dve.wait_ge(mod_done, 4)
            for r, c0, c1 in parts:
                for s in (SCALE_A, SCALE_F):
                    dve.tensor_scalar(modv[0:r, :, s, c0:c1], modv[0:r, :, s, c0:c1], 1.0, None, ALU.add)
            for k in range(2):
                dve.wait_ge(hi_ready, k + 1)
                if k:
                    dve.wait_ge(w2_out, 32 * k)
                dve.tensor_tensor(w2l[:, :, :], w2[:, k * (FT // 2):(k + 1) * (FT // 2), :],
                                  w2h[:, :, :].bitcast(F32), ALU.subtract).then_inc(lo_ready, 1)


def rotation(nc, io, g):
    SQUARINGS, DEGREE = 10, 8
    VT = 16
    VP = SKEW // VT
    PAD = RD
    ML = RD + 1
    with ExitStack() as ctx:
        sb = lambda name, shape, dt=F32: ctx.enter_context(nc.sbuf_tensor(name, shape, dt))
        sem = lambda name: ctx.enter_context(nc.semaphore(name))
        psum = lambda name, shape: ctx.enter_context(nc.psum_tensor(name, shape, F32))
        ident, UT = g["ident"], g["UT"]
        Pc = sb("Pc", [P, KC, RD])
        PT = sb("PT", [RD, D])
        G = sb("gram", [RD, RD])
        M = sb("elim", [RD, ML + RD])
        step = sb("step_lhsT", [RD, P])
        stepT = sb("stepT_lhsT", [RD, P])
        tiny = sb("tiny", [1, 8])
        LiT = sb("LiT", [RD, RD])
        prod = sb("prod", [RD, RD])
        dcol = sb("dcol", [RD, 4])
        S = sb("Sinv", [RD, RD])
        ST = sb("SinvT", [RD, RD])
        U1T = sb("U1T", [RD, D])
        U1 = sb("U1", [P, KC, RD])
        U2T = sb("U2T", [RD, D])
        half_mask = sb("half_mask", [RD, RD])
        KTm = sb("KTm", [RD, RD])
        X2 = sb("lu_pair", [RD, 2, ML])
        sg = sb("signs", [1, RD])
        crow = sb("cond_rows", [B, D])
        srow = sb("silu_rows", [B, D])
        selb = sb("sel_batch", [B, B, VP])
        sbc = sb("silu_bcast", [VP, B, D])
        Wv = sb("W_skew", [VP, VT, D])
        junk = sb("junk", [VP, D])
        v = sb("v", [VP, B, VT])
        vT = sb("vT", [B * VT, VP])
        bv2 = sb("b_skew2", [B * VT, VP])
        zpad = sb("zpad", [B, PAD])
        Au = sb("A_upper", [RD, B, RD])
        X = sb("X_skew", [RD, B, RD])
        Xn = sb("X_skew_neg", [RD, B, RD])
        E = sb("E_pair", [RD, 2, B, RD])
        E2 = sb("E_pair2", [RD, 2, B, RD])
        pA = psum("pA", [P, 2, 512])
        pB = psum("pB", [P, 512])
        pC = psum("pC", [P, 512])
        p_in, w_in, c_in, b_in, v_out, a_in = (sem(x) for x in ("P_in", "W_in", "crow_in", "bskew_in", "v_out", "A_in"))
        w_ins = [sem(f"W_in{k}") for k in range(4)]
        const_s = sem("const_chain")
        pe_s, dve_s, act_s = sem("pe_step"), sem("dve_step"), sem("act_step")
        srow_ready, sbc_mm, sbc_ready, vT_mm, vT_ready, v_dve = (
            sem(x) for x in ("srow_ready", "sbc_mm", "sbc_ready", "vT_mm", "vT_ready", "v_dve"))
        row_ready, elim_mm, left_ready, right_ready = (sem(x) for x in ("row_ready", "elim_mm", "left_ready", "right_ready"))
        lrow_ready, lu_mm, lu_ready = (sem(x) for x in ("lu_row_ready", "lu_mm", "lu_ready"))
        chain_s, mask_s, sqrt_s = sem("dve_chain"), sem("mask_ready"), sem("sqrt_ready")
        vs = g["skew_scratch"]
        block = ctx.enter_context(nc.Block())

        @block.sync
        def _(sp):
            load_chunked(sp, Pc[:, :, :], io["L1_cond_P"], p_in)
            sp.dma_start(crow[:, :], io["cond_1152"]).then_inc(c_in, 16)
            for k in range(4):
                n = VT // 4
                sp.dma_start(Wv[:, k * n:(k + 1) * n, :],
                             io["L1_cond_W"].rearrange("(t p) k -> p t k", p=VP)[:, k * n:(k + 1) * n, :]).then_inc(w_ins[k], 16)
            for b in range(B):
                sp.dma_start(bv2[b * VT:(b + 1) * VT, :], io["L1_cond_b"].rearrange("(t p) -> t p", p=VP)).then_inc(b_in, 16)
            sp.wait_ge(mask_s, 1)
            sp.dma_start(vs[:, 0:PAD], zpad[:, :]).then_inc(v_out, 16)
            sp.dma_start(vs[:, PAD + SKEW:PAD + SKEW + PAD], zpad[:, :]).then_inc(v_out, 16)
            sp.wait_ge(vT_ready, 1)
            for b in range(B):
                sp.dma_start(vs[b, PAD:PAD + SKEW].rearrange("(t p) -> t p", p=VP),
                             vT[b * VT:(b + 1) * VT, :]).then_inc(v_out, 16)
            sp.wait_ge(v_out, 64)
            for i in range(RD):
                start = PAD + (RD - 2) * i - i * (i - 1) // 2 - 1
                sp.dma_start(Au[i:i + 1, :, :], vs[:, start:start + RD].rearrange("(a b) c -> a b c", a=1)).then_inc(a_in, 16)

        @block.gpsimd
        def _(pool):
            pool.memset(zpad[:, :], 0.0).then_inc(mask_s, 1)
            ch = Chain(pool, const_s)
            ch.do(pool.memset(half_mask[:, :], 1.0))
            ch.do(pool.affine_select(out=half_mask[:, :], in_=half_mask[:, :], compare_op=ALU.not_equal, fill=0.5,
                                     base=0, pattern=[[-1, RD]], channel_multiplier=1))
            ch.do(pool.affine_select(out=half_mask[:, :], in_=half_mask[:, :], compare_op=ALU.is_ge, fill=0.0,
                                     base=0, pattern=[[1, RD]], channel_multiplier=-1))
            for m in (step, stepT):
                ch.do(pool.memset(m[:, :], 0.0))
                ch.do(pool.affine_select(out=m[:, 0:RD], in_=m[:, 0:RD], compare_op=ALU.not_equal, fill=1.0,
                                         base=-1, pattern=[[-1, RD]], channel_multiplier=1))
            ch.do(pool.memset(step[0:1, RD - 1:RD], 1.0))
            ch.do(pool.memset(selb[:, :, :], 0.0))
            ch.do(pool.affine_select(out=selb[:, :, :], in_=selb[:, :, :], compare_op=ALU.not_equal, fill=1.0,
                                     base=0, pattern=[[-1, B], [0, VP]], channel_multiplier=1))
            ch.do(pool.memset(M[:, :], 0.0))
            ch.do(pool.memset(X2[:, :, :], 0.0))
            pool.memset(tiny[:, 7:8], 1.0).then_inc(mask_s, 1)
            pool.wait_ge(a_in, 16 * RD)
            pool.affine_select(out=Au[:, :, :], in_=Au[:, :, :], compare_op=ALU.is_gt, fill=0.0,
                               base=0, pattern=[[0, B], [1, RD]], channel_multiplier=-1).then_inc(mask_s, 1)

        @block.scalar
        def _(act):
            act.wait_ge(c_in, 16)
            act.activation(srow[:, :], crow[:, :], ACT.Silu).then_inc(srow_ready, 1)
            for b in range(B):
                for h in range(2):
                    act.wait_ge(sbc_mm, 2 * b + h + 1)
                    act.activation(sbc[:, b, h * HALF:(h + 1) * HALF], pA[0:VP, h, 0:HALF], ACT.Copy).then_inc(sbc_ready, 1)
            act.sem_inc(right_ready, 1)
            with act.Fori(0, RD) as i:
                act.wait_ge(elim_mm, i + 1)
                act.activation(M[:, ML:ML + RD], pC[0:RD, 0:RD], ACT.Copy).then_inc(right_ready, 1)
            act.wait_ge(sqrt_s, 1)
            act.activation(dcol[:, 1:2], dcol[:, 0:1], ACT.Sqrt).then_inc(sqrt_s, 1)

        @block.tensor
        def _(pe):
            pe.wait_ge(srow_ready, 1)
            pe.wait_ge(mask_s, 2)
            for b in range(B):
                for h in range(2):
                    if b:
                        pe.wait_ge(sbc_ready, h + 1)
                    pe.matmul(pA[0:VP, h, 0:HALF], selb[:, b, :], srow[:, h * HALF:(h + 1) * HALF],
                              start=True, stop=True).then_inc(sbc_mm, 1)
            pe.wait_ge(p_in, 32)
            for c in range(KC):
                last = pe.matmul(pB[0:RD, 0:RD], Pc[0:rows(c), c, :], Pc[0:rows(c), c, :], start=(c == 0), stop=(c == KC - 1))
            last.then_inc(pe_s, 1)
            pe.wait_ge(sbc_ready, 4)
            for c in range(KC):
                last = pe.transpose(pA[0:RD, c // 4, (c % 4) * P:(c % 4) * P + rows(c)], Pc[0:rows(c), c, :],
                                    ident[0:rows(c), 0:rows(c)])
            last.then_inc(pe_s, 1)
            pe.wait_ge(v_dve, 1)
            pe.transpose(pC[0:B * VT, 0:VP], v[:, :, :].rearrange("p b t -> p (b t)"), ident[0:VP, 0:VP]).then_inc(vT_mm, 1)
            pe.wait_ge(dve_s, 2)
            pe.wait_ge(vT_ready, 1)
            with pe.Fori(0, RD) as i:
                pe.wait_ge(row_ready, i + 1)
                pe.wait_ge(left_ready, i + 1)
                pe.wait_ge(right_ready, i + 1)
                pe.matmul(pB[:, 0:ML], step[:, :], M[:, 0:ML], start=True, stop=True)
                pe.matmul(pC[:, 0:RD], step[:, :], M[:, ML:ML + RD], start=True, stop=True).then_inc(elim_mm, 1)
            pe.wait_ge(right_ready, RD + 1)
            pe.wait_ge(left_ready, RD + 1)
            pe.transpose(pC[0:RD, 0:RD], M[:, ML:ML + RD], ident[0:RD, 0:RD]).then_inc(pe_s, 1)
            pe.wait_ge(dve_s, 3)
            pe.matmul(pB[0:RD, 0:RD], LiT[:, :], G[:, :], start=True, stop=True).then_inc(pe_s, 1)
            pe.wait_ge(dve_s, 4)
            pe.transpose(pC[0:RD, 0:RD], S[:, :], ident[0:RD, 0:RD]).then_inc(pe_s, 1)
            pe.wait_ge(dve_s, 5)
            for h in range(2):
                last = pe.matmul(pA[0:RD, h, 0:HALF], ST[:, :], PT[:, h * HALF:(h + 1) * HALF], start=True, stop=True)
            last.then_inc(pe_s, 1)
            pe.wait_ge(dve_s, 6)
            for c in range(KC):
                last = pe.transpose(pB[0:rows(c), c * RD:(c + 1) * RD], U1T[:, c * P:c * P + rows(c)], ident[0:RD, 0:RD])
            last.then_inc(pe_s, 1)
            pe.wait_ge(dve_s, 7)
            for c in range(KC):
                last = pe.matmul(pC[0:RD, 0:RD], U1[0:rows(c), c, :], U1[0:rows(c), c, :], start=(c == 0), stop=(c == KC - 1))
            last.then_inc(pe_s, 1)
            pe.wait_ge(dve_s, 8)
            for h in range(2):
                last = pe.matmul(pA[0:RD, h, 0:HALF], KTm[:, :], U1T[:, h * HALF:(h + 1) * HALF], start=True, stop=True)
            last.then_inc(pe_s, 1)
            pe.wait_ge(dve_s, 9)
            pe.transpose(pB[0:RD, 0:RD], U2T[:, 0:RD], ident[0:RD, 0:RD]).then_inc(pe_s, 1)
            with pe.Fori(0, RD) as i:
                pe.wait_ge(lrow_ready, i + 1)
                pe.matmul(pB[:, 0:ML], step[:, :], X2[:, 0, :], start=True, stop=True)
                pe.matmul(pB[:, 256:256 + ML], stepT[:, :], X2[:, 1, :], start=True, stop=True).then_inc(lu_mm, 1)
            pe.wait_ge(lu_ready, RD + 1)
            pe.matmul(pC[0:RD, 0:1], sg[0:1, :], tiny[0:1, 7:8], start=True, stop=True).then_inc(pe_s, 1)
            pe.wait_ge(mask_s, 3)
            for b in range(B):
                last = pe.transpose(pA[0:RD, 0, b * RD:(b + 1) * RD], Au[:, b, :], ident[0:RD, 0:RD])
            last.then_inc(pe_s, 1)
            pe.wait_ge(dve_s, 10)
            for k in range(DEGREE - 1):
                for b in range(B):
                    pe.matmul(pA[0:RD, 0, b * RD:(b + 1) * RD], Xn[:, b, :], E[:, 0, b, :], start=True, stop=True)
                    last = pe.matmul(pA[0:RD, 0, (B + b) * RD:(B + b + 1) * RD], X[:, b, :], E[:, 1, b, :], start=True, stop=True)
                last.then_inc(pe_s, 1)
                pe.wait_ge(dve_s, 11 + k)
            for k in range(SQUARINGS):
                src = (E, E2)[k % 2]
                for b in range(B):
                    pe.matmul(pA[0:RD, 0, b * RD:(b + 1) * RD], src[:, 1, b, :], src[:, 0, b, :], start=True, stop=True)
                    last = pe.matmul(pA[0:RD, 0, (B + b) * RD:(B + b + 1) * RD], src[:, 0, b, :], src[:, 1, b, :], start=True, stop=True)
                last.then_inc(pe_s, 1)
                pe.wait_ge(dve_s, 10 + DEGREE + k)
            for b in range(B):
                for c in range(KC):
                    last = pe.matmul((pB, pC)[b][0:rows(c), c * RD:(c + 1) * RD], UT[:, c * P:c * P + rows(c)],
                                     E[:, 0, b, :], start=True, stop=True)
            last.then_inc(pe_s, 1)

        @block.vector
        def _(dve):
            ch = Chain(dve, chain_s)
            dve.wait_ge(sbc_ready, 4)
            for t in range(VT):
                if t % (VT // 4) == 0:
                    dve.wait_ge(w_ins[t // (VT // 4)], 16)
                for b in range(B):
                    ch.do(dve.tensor_tensor_reduce(out=junk[:, :], in0=Wv[:, t, :], in1=sbc[:, b, :], scale=1.0, scalar=0.0,
                                                   op0=ALU.mult, op1=ALU.add, accum_out=v[:, b, t:t + 1]))
            dve.sem_inc(v_dve, 1)
            dve.wait_ge(pe_s, 1)
            dve.wait_ge(mask_s, 2)
            ch.do(dve.tensor_copy(G[:, :], pB[0:RD, 0:RD]))
            ch.do(dve.tensor_copy(M[:, 0:RD], G[:, :]))
            dve.tensor_copy(M[:, ML:ML + RD], ident[0:RD, 0:RD]).then_inc(dve_s, 1)
            dve.wait_ge(pe_s, 2)
            dve.tensor_copy(PT[:, :], pA[0:RD, :, :].rearrange("p a b -> p (a b)")[:, 0:D]).then_inc(dve_s, 1)
            dve.wait_ge(b_in, 32)
            dve.wait_ge(vT_mm, 1)
            dve.tensor_tensor(vT[:, :], pC[0:B * VT, 0:VP], bv2[:, :], ALU.add).then_inc(vT_ready, 1)
            dve.sem_inc(left_ready, 1)
            n0 = ch.n
            with dve.Fori(0, RD) as i:
                dve.wait_ge(left_ready, i + 1)
                dve.reciprocal(tiny[0:1, 0:1], M[0:1, 0:1]).then_inc(chain_s, 1)
                dve.wait_ge(chain_s, n0 + i + 1)
                dve.tensor_scalar(step[0:1, 0:RD - 1], M[0:1, 1:RD], tiny[0:1, 0:1], -1.0, ALU.mult, ALU.mult).then_inc(row_ready, 1)
                dve.wait_ge(elim_mm, i + 1)
                dve.tensor_copy(M[:, 0:RD], pB[0:RD, 1:ML]).then_inc(left_ready, 1)
            ch.n = n0 + RD
            dve.wait_ge(pe_s, 3)
            dve.tensor_copy(LiT[:, :], pC[0:RD, 0:RD]).then_inc(dve_s, 1)
            dve.wait_ge(pe_s, 4)
            dve.wait_ge(right_ready, RD + 1)
            ch.do(dve.tensor_tensor(prod[:, :], pB[0:RD, 0:RD], M[:, ML:ML + RD], ALU.mult))
            dve.tensor_reduce(dcol[:, 0:1], prod[:, :], op=ALU.add, axis=AX.X).then_inc(sqrt_s, 1)
            dve.wait_ge(sqrt_s, 2)
            ch.do(dve.reciprocal(dcol[:, 2:3], dcol[:, 1:2]))
            dve.tensor_scalar(S[:, :], M[:, ML:ML + RD], dcol[:, 2:3], None, ALU.mult).then_inc(dve_s, 1)
            dve.wait_ge(pe_s, 5)
            dve.tensor_copy(ST[:, :], pC[0:RD, 0:RD]).then_inc(dve_s, 1)
            dve.wait_ge(pe_s, 6)
            dve.tensor_copy(U1T[:, :].rearrange("p (a b) -> p a b", a=2), pA[0:RD, :, 0:HALF]).then_inc(dve_s, 1)
            dve.wait_ge(pe_s, 7)
            ch.do(dve.tensor_copy(U1[:, 0:KC - 1, :].rearrange("p a b -> p (a b)"), pB[:, 0:(KC - 1) * RD]))
            dve.tensor_copy(U1[0:rows(KC - 1), KC - 1, :], pB[0:rows(KC - 1), (KC - 1) * RD:KC * RD]).then_inc(dve_s, 1)
            dve.wait_ge(pe_s, 8)
            ch.do(dve.tensor_tensor(prod[:, :], pC[0:RD, 0:RD], ident[0:RD, 0:RD], ALU.subtract))
            ch.do(dve.tensor_tensor(KTm[:, :], prod[:, :], half_mask[:, :], ALU.mult))
            dve.tensor_tensor(KTm[:, :], ident[0:RD, 0:RD], KTm[:, :], ALU.subtract).then_inc(dve_s, 1)
            dve.wait_ge(pe_s, 9)
            dve.tensor_copy(U2T[:, :].rearrange("p (a b) -> p a b", a=2), pA[0:RD, :, 0:HALF]).then_inc(dve_s, 1)
            dve.wait_ge(pe_s, 10)
            ch.do(dve.tensor_copy(X2[:, 0, 0:RD], pB[0:RD, 0:RD]))
            ch.do(dve.memset(step[0:1, RD - 1:RD], 0.0))
            dve.wait_ge(dve_s, 9)
            dve.tensor_copy(X2[:, 1, 0:RD], U2T[:, 0:RD]).then_inc(lu_ready, 1)
            n1 = ch.n
            with dve.Fori(0, RD) as i:
                c = Chain(dve, chain_s, n1 + i * 4)
                dve.wait_ge(lu_ready, i + 1)
                c.do(dve.tensor_scalar(tiny[0:1, 0:1], X2[0:1, 0, 0:1], 0.0, 2.0, ALU.is_ge, ALU.mult))
                c.do(dve.tensor_scalar(sg[0:1, bass.ds(i, 1)], tiny[0:1, 0:1], -1.0, None, ALU.add))
                c.do(dve.scalar_tensor_tensor(out=tiny[0:1, 1:2], in0=tiny[0:1, 0:1], scalar=-1.0, in1=X2[0:1, 0, 0:1],
                                              op0=ALU.add, op1=ALU.add))
                c.do(dve.reciprocal(tiny[0:1, 2:3], tiny[0:1, 1:2]))
                dve.tensor_scalar(stepT[0:1, 0:RD - 1], X2[0:1, 0, 1:RD], tiny[0:1, 2:3], -1.0, ALU.mult, ALU.mult)
                dve.tensor_scalar(step[0:1, 0:RD - 1], X2[0:1, 1, 1:RD], tiny[0:1, 2:3], -1.0, ALU.mult, ALU.mult).then_inc(lrow_ready, 1)
                dve.wait_ge(lu_mm, i + 1)
                dve.tensor_copy(X2[:, :, 0:RD], pB[0:RD, :].rearrange("p (a b) -> p a b", a=2)[:, :, 1:ML]).then_inc(lu_ready, 1)
            ch.n = n1 + 4 * RD
            dve.wait_ge(pe_s, 11)
            ch.do(dve.tensor_copy(dcol[:, 3:4], pC[0:RD, 0:1]))
            ch.do(dve.tensor_scalar(UT[:, :], U2T[:, :], dcol[:, 3:4], -1.0, ALU.mult, ALU.mult))
            dve.wait_ge(pe_s, 12)
            ch.do(dve.tensor_tensor(X[:, :, :], Au[:, :, :], pA[0:RD, 0, 0:B * RD].rearrange("p (b c) -> p b c", b=B), ALU.subtract))
            ch.do(dve.tensor_scalar(Xn[:, :, :], X[:, :, :], -1.0 / 2 ** SQUARINGS, None, ALU.mult))
            ch.do(dve.tensor_scalar(X[:, :, :], X[:, :, :], 1.0 / 2 ** SQUARINGS, None, ALU.mult))
            ch.do(dve.tensor_scalar(E[:, 0, :, :], X[:, :, :], 1.0 / DEGREE, None, ALU.mult))
            dve.tensor_scalar(E[:, 1, :, :], Xn[:, :, :], 1.0 / DEGREE, None, ALU.mult).then_inc(dve_s, 1)
            pairs = pA[0:RD, 0, 0:2 * B * RD].rearrange("p (e b c) -> p e b c", e=2, b=B)
            for k in range(DEGREE - 1):
                dve.wait_ge(pe_s, 13 + k)
                ch.do(dve.tensor_tensor(E2[:, 0, :, :], pairs[:, 0], X[:, :, :], ALU.add))
                ch.do(dve.tensor_tensor(E2[:, 1, :, :], pairs[:, 1], Xn[:, :, :], ALU.add))
                dve.tensor_scalar(E[:, :, :, :], E2[:, :, :, :], 1.0 / (DEGREE - 1 - k), None, ALU.mult).then_inc(dve_s, 1)
            for k in range(SQUARINGS):
                src, dst = ((E, E2), (E2, E))[k % 2]
                dve.wait_ge(pe_s, 12 + DEGREE + k)
                dve.wait_ge(dve_s, 9 + DEGREE + k)
                dve.scalar_tensor_tensor(out=dst[:, :, :, :], in0=src[:, :, :, :], scalar=2.0, in1=pairs,
                                         op0=ALU.mult, op1=ALU.add).then_inc(dve_s, 1)
            dve.wait_ge(pe_s, 12 + DEGREE + SQUARINGS)
            for b in range(B):
                q = (pB, pC)[b]
                dve.memset(g["URI"][rows(KC - 1):P, b, KC - 1, :], 0.0)
                dve.tensor_copy(g["URI"][:, b, 0:KC - 1, :].rearrange("p a b -> p (a b)"), q[:, 0:(KC - 1) * RD])
                dve.tensor_copy(g["URI"][0:rows(KC - 1), b, KC - 1, :], q[0:rows(KC - 1), (KC - 1) * RD:KC * RD])


def qkv(nc, io, g):
    V = g["V"]
    RING = 3
    with ExitStack() as ctx:
        sb = lambda name, shape, dt=F32: ctx.enter_context(nc.sbuf_tensor(name, shape, dt))
        sem = lambda name: ctx.enter_context(nc.semaphore(name))
        psum = lambda name, shape: ctx.enter_context(nc.psum_tensor(name, shape, F32))
        ident, modv = g["ident"], g["modv"]
        stage = sb("wqk_stage", [P, 2 * D])
        wh = sb("wqk_hi", [P, KC, 2 * D], F32R)
        wl = sb("wqk_lo", [P, KC, 2 * D], F32R)
        wv = sb("wv_sb", [P, KC, D])
        bqk = sb("bqk", [P, QKT])
        ones = sb("ones_row", [1, P])
        bvr = sb("bv_row", [1, D])
        bvb = sb("bv_bcast", [P, 2, HALF])
        eps = sb("eps", [P, 1])
        x = sb("x_blk", [P, TPB, D])
        xn = sb("x_norm", [P, TPB, D])
        st = sb("ln_stats", [P, TPB, 2, 6])
        mv = sb("ln_mv", [P, TPB, 2])
        sd = sb("ln_std", [P, TPB])
        rs = sb("ln_rstd", [P, TPB])
        xm = sb("x_modT", [P, KC, BLK])
        xh = sb("x_modT_hi", [P, KC, BLK], F32R)
        xl = sb("x_modT_lo", [P, KC, BLK], F32R)
        oh = sb("qk_hi_out", [P, RING, BLK], F32R)
        ol = sb("qk_lo_out", [P, RING, BLK], F32R)
        tp = [psum(f"tp{i}", [P, BLK]) for i in range(2)]
        qk = [psum(f"qk{i}", [P, BLK]) for i in range(RING)]
        vp = [psum(f"vp{i}", [P, BLK]) for i in range(2)]
        names = ("w_in w_free wh_ready wl_ready wv_in bias_in ones_ready bvb_mm bvb_ready x_in x_used st_ready var_ready std_ready "
                 "xn_ready tr_done xm_ready xs_ready qk_done hi_ready lo_ready v_done v_ready chain")
        s = Counts(lambda n: sem("a_" + n), names.split(), ("v_done", "xs_ready", "xm_ready", "v_ready", "lo_ready", "tr_done", "qk_done"))
        rings = range(RING)
        outs = Counts(lambda n: sem("a_" + n), [f"out_{p}{i}" for p in ("hi", "lo") for i in rings],
                      [f"out_{p}{i}" for p in ("hi", "lo") for i in rings], credit=16)
        w_qkv, b_qkv = io["L0_cond_w_qkv"], io["L0_cond_b_qkv"]
        xv = io["x"].rearrange("b (k t p) d -> (b k) p t d", p=P, t=TPB)
        block = ctx.enter_context(nc.Block())

        @block.sync
        def _(sp):
            outs.give(sp, *outs.sems)
            sp.dma_start(bqk[:, :], b_qkv[0:2 * D].rearrange("(m p) -> p m", p=P)).then_inc(s["bias_in"], 16)
            sp.dma_start(bvr[:, :], row(b_qkv[2 * D:3 * D])).then_inc(s["bias_in"], 16)
            for c in range(KC):
                if c:
                    s.wait(sp, "w_free", c)
                sp.dma_start(stage[0:rows(c), :], w_qkv[c * P:c * P + rows(c), 0:2 * D]).then_inc(s["w_in"], 16)
                if c == 0:
                    sp.dma_start(x[:, :, :], xv[0]).then_inc(s["x_in"], 16)
                    load_chunked(sp, wv[:, :, :], w_qkv[:, 2 * D:3 * D], s["wv_in"])
            with sp.Fori(0, B) as b:
                with sp.Fori(0, BPB) as j:
                    it = b * BPB + j
                    for m in range(QKT):
                        if m == 1:
                            s.wait(sp, "x_used", it + 1)
                            sp.dma_start(x[:, :, :], xv[bass.ds((it + 1) % NBLK, 1)].rearrange("a p t d -> p (a t) d")
                                         ).then_inc(s["x_in"], 16)
                        for part, ready, src, out in (("q_hi", "hi_ready", oh, "out_hi"), ("q_lo", "lo_ready", ol, "out_lo")):
                            s.wait(sp, ready, it * QKT + m + 1)
                            f0 = m * P
                            nq = max(0, min(P, D - f0))
                            cols = bass.ds(j * BLK, BLK)
                            pieces = [(0, nq, part, f0)] if nq else []
                            pieces += [(nq, P, part.replace("q", "k"), f0 + nq - D)] if nq < P else []
                            for p0, p1, name, r0 in pieces:
                                sp.dma_start(g[name][bass.ds(b * D + r0, p1 - p0), cols],
                                             src[p0:p1, m % RING, :].bitcast(F32)).then_inc(outs[f"{out}{m % RING}"], 16)
            s.wait(sp, "x_in", 16 * (NBLK + 1))
            for out in ("out_hi", "out_lo"):
                for i in rings:
                    outs.wait(sp, f"{out}{i}", 16 * NBLK * (QKT // RING + (i == (QKT // 2) % RING)))

        @block.scalar
        def _(act):
            s.give(act, "xm_ready")
            for c in range(KC):
                s.wait(act, "w_in", 16 * (c + 1))
                act.activation(wh[0:rows(c), c, :], stage[0:rows(c), :], ACT.Copy).then_inc(s["wh_ready"], 1)
            s.wait(act, "bvb_mm", 1)
            for h in range(2):
                act.activation(bvb[:, h, :], vp[h][:, 0:HALF], ACT.Copy).then_inc(s["bvb_ready"], 1)
            s.wait(act, "bias_in", 32)
            with act.Fori(0, B) as b:
                with act.Fori(0, BPB) as j:
                    it = b * BPB + j
                    s.wait(act, "var_ready", it + 1)
                    act.activation(sd[:, :], mv[:, :, 1], ACT.Sqrt, bias=eps[:, :]).then_inc(s["std_ready"], 1)
                    s.wait(act, "v_done", it * 2 * TPB)
                    s.wait(act, "xs_ready", it * KC)
                    for c in range(KC):
                        r = rows(c)
                        s.wait(act, "tr_done", it * KC + c + 1)
                        act.activation(xm[0:r, c, :], tp[c % 2][0:r, :], ACT.Identity,
                                       bias=modv[0:r, bass.ds(b, 1), SHIFT_A, c:c + 1].rearrange("p a b -> p (a b)"),
                                       scale=modv[0:r, bass.ds(b, 1), SCALE_A, c:c + 1].rearrange("p a b -> p (a b)")
                                       ).then_inc(s["xm_ready"], 1)
                    for m in range(QKT):
                        s.wait(act, "qk_done", it * QKT + m + 1)
                        k, extra = m // RING, int(m % RING == (QKT // 2) % RING)
                        stores = it * (QKT // RING + extra) + k + int(extra and m > QKT // 2)
                        outs.wait(act, f"out_hi{m % RING}", stores * 16)
                        act.activation(oh[:, m % RING, :], qk[m % RING][:, :], ACT.Identity,
                                       bias=bqk[:, m:m + 1]).then_inc(s["hi_ready"], 1)

        @block.tensor
        def _(pe):
            s.give(pe, "v_done", "tr_done", "qk_done")
            s.wait(pe, "ones_ready", 1)
            s.wait(pe, "bias_in", 32)
            for h in range(2):
                last = pe.matmul(vp[h][:, 0:HALF], ones[:, :], bvr[:, h * HALF:(h + 1) * HALF], start=True, stop=True)
            last.then_inc(s["bvb_mm"], 1)
            s.wait(pe, "wv_in", 32)
            s.wait(pe, "wl_ready", KC)
            s.wait(pe, "bvb_ready", 2)
            with pe.Fori(0, NBLK) as it:
                s.wait(pe, "xn_ready", it + 1)
                for c in range(KC):
                    if c < KC - 1:
                        s.wait(pe, "xm_ready", it * KC + (max(0, c - 1) if c < KC - 2 else KC - 2))
                    for t in range(TPB):
                        last = pe.transpose(tp[c % 2][0:rows(c), t * P:(t + 1) * P], xn[:, t, c * P:c * P + rows(c)], ident[:, :])
                    last.then_inc(s["tr_done"], 1)
                s.wait(pe, "xm_ready", it * KC + KC)
                for t in range(TPB):
                    for h in range(2):
                        s.wait(pe, "v_ready", it * 2 * TPB + max(0, 2 * t + h - 1))
                        for c in range(KC):
                            last = pe.matmul(vp[h][:, 0:HALF], xm[0:rows(c), c, t * P:(t + 1) * P],
                                             wv[0:rows(c), c, h * HALF:(h + 1) * HALF], start=(c == 0), stop=(c == KC - 1))
                        last.then_inc(s["v_done"], 1)
                s.wait(pe, "xs_ready", it * KC + KC)
                for m in range(QKT):
                    s.wait(pe, "lo_ready", it * QKT + max(0, m - RING + 1))
                    for c in range(KC):
                        for n, (w, xx) in enumerate(((wh, xh), (wh, xl), (wl, xh))):
                            last = pe.matmul(qk[m % RING][:, :], w[0:rows(c), c, m * P:(m + 1) * P], xx[0:rows(c), c, :],
                                             start=(c == 0 and n == 0), stop=(c == KC - 1 and n == 2))
                    last.then_inc(s["qk_done"], 1)

        @block.vector
        def _(dve):
            s.give(dve, "xs_ready", "v_ready", "lo_ready")
            dve.memset(ones[:, :], 1.0).then_inc(s["ones_ready"], 1)
            dve.memset(eps[:, :], LN_EPS)
            for c in range(KC):
                s.wait(dve, "wh_ready", c + 1)
                ins = dve.tensor_tensor(wl[0:rows(c), c, :], stage[0:rows(c), :], wh[0:rows(c), c, :].bitcast(F32), ALU.subtract)
                ins.then_inc(s["wl_ready"], 1)
                s.wait(dve, "wl_ready", c + 1)
                dve.sem_inc(s["w_free"], 1)
            s.wait(dve, "bvb_ready", 2)
            with dve.Fori(0, B) as b:
                with dve.Fori(0, BPB) as j:
                    it = b * BPB + j
                    ch = Chain(dve, s["chain"], it * 2)
                    s.wait(dve, "x_in", it * 16 + 16)
                    for t in range(TPB):
                        for h in range(2):
                            last = dve.bn_stats(st[:, t, h, :], x[:, t, h * HALF:(h + 1) * HALF])
                    last.then_inc(s["st_ready"], 1)
                    dve.drain()
                    for t in range(TPB):
                        last = dve.bn_aggr(mv[:, t, :], st[:, t, :, :].rearrange("p a b -> p (a b)"))
                    last.then_inc(s["var_ready"], 1)
                    s.wait(dve, "std_ready", it + 1)
                    ch.do(dve.reciprocal(rs[:, :], sd[:, :]))
                    s.wait(dve, "tr_done", it * KC)
                    for t in range(TPB):
                        last = dve.tensor_scalar(xn[:, t, :], x[:, t, :], mv[:, t, 0:1], rs[:, t:t + 1], ALU.subtract, ALU.mult)
                    last.then_inc(s["xn_ready"], 1)
                    s.wait(dve, "xn_ready", it + 1)
                    dve.sem_inc(s["x_used"], 1)
                    s.wait(dve, "qk_done", it * QKT)
                    for c in range(KC):
                        r = rows(c)
                        s.wait(dve, "xm_ready", it * KC + c + 1)
                        last = dve.tensor_copy(xh[0:r, c, :], xm[0:r, c, :])
                    ch.do(last)
                    for c in range(KC):
                        r = rows(c)
                        dve.tensor_tensor(xl[0:r, c, :], xm[0:r, c, :], xh[0:r, c, :].bitcast(F32), ALU.subtract).then_inc(s["xs_ready"], 1)
                    for t in range(TPB):
                        for h in range(2):
                            s.wait(dve, "v_done", it * 2 * TPB + 2 * t + h + 1)
                            dve.tensor_tensor(
                                V[:, bass.ds(b * H + h * (H // 2), H // 2), bass.ds(j * TPB + t, 1), :].rearrange("p h a d -> p h (a d)"),
                                vp[h][:, 0:HALF].rearrange("p (h d) -> p h d", d=HD),
                                bvb[:, h, :].rearrange("p (h d) -> p h d", d=HD), ALU.add).then_inc(s["v_ready"], 1)
                    for m in range(QKT):
                        s.wait(dve, "hi_ready", it * QKT + m + 1)
                        k, extra = m // RING, int(m % RING == (QKT // 2) % RING)
                        stores = it * (QKT // RING + extra) + k + int(extra and m > QKT // 2)
                        outs.wait(dve, f"out_lo{m % RING}", stores * 16)
                        dve.scalar_tensor_tensor(out=ol[:, m % RING, :], in0=qk[m % RING][:, :], scalar=bqk[:, m:m + 1],
                                                 in1=oh[:, m % RING, :].bitcast(F32), op0=ALU.add, op1=ALU.subtract
                                                 ).then_inc(s["lo_ready"], 1)


QB = 1024
NQB = T // QB
SLOTS = NQB * KT
STK = 3 * HD
VW = 64
MAXW = 512
NMAX = KT * (T // MAXW)
MAX_FROM, MAX_PER = 5, 3
SCALE = float(HD) ** -0.5


def max_slots():
    plan, k = [[] for _ in range(SLOTS)], 0
    for s in range(MAX_FROM, SLOTS):
        plan[s] = list(range(k, min(NMAX, k + MAX_PER)))
        k = min(NMAX, k + MAX_PER)
    assert k == NMAX
    return plan


PLAN = max_slots()
LAST_MAX = max(s for s in range(SLOTS) if PLAN[s])
ROW_SLOT = LAST_MAX + 1
O_SLOT = KT + 3
EXTRA = 3


def attention(nc, io, g):
    V = g["V"]
    with ExitStack() as ctx:
        sb = lambda name, shape, dt=F32: ctx.enter_context(nc.sbuf_tensor(name, shape, dt))
        sem = lambda name: ctx.enter_context(nc.semaphore("b_" + name))
        psum = lambda name, shape: ctx.enter_context(nc.psum_tensor(name, shape, F32))
        ident = g["ident"]
        q = [sb(f"q_stack{u}", [P, T], F32R) for u in range(2)]
        k = [sb(f"k_stack{u}", [P, T], F32R) for u in range(2)]
        vst = [sb(f"v_stat{u}", [P, KT, VW]) for u in range(2)]
        pr = [sb(f"probs{i}", [P, QB]) for i in range(4)]
        mxp = sb("max_parts", [P, KT, T // MAXW])
        mx = sb("max_q", [P, KT])
        nm = sb("neg_max", [P, 2, KT])
        nmr = sb("neg_max_r", [P, 2, KT], F32R)
        nmT = sb("neg_maxT", [2 * KT, P], F32R)
        oT = [sb(f"outT{i}", [P, 512]) for i in range(NQB)]
        rc = sb("recip_sum", [P, 2, KT // NQB // 2])
        ob = [sb(f"out_tok{u}", [P, KT, HD]) for u in range(2)]
        sc = [psum(f"scoresT{i}", [P, QB]) for i in range(2)]
        shared = [psum(f"shared{i}", [P, 512]) for i in range(2)]
        av = [psum(f"av{i}", [P, 512]) for i in range(NQB)]
        stack_in = [sem(f"stack_in{u}") for u in range(2)]
        row_in = [sem(f"row_in{u}") for u in range(2)]
        ones_ready, sc_done, exp_done, av_done, half_done = (sem(x) for x in ("ones_ready", "sc_done", "exp_done", "av_done", "half_done"))
        use_done, use_free, nm_ready, nmT_ready, oT_ready, v_ready, v_init, ob_ready, rc_done, chain = (
            sem(x) for x in ("use_done", "use_free", "nm_ready", "nmT_ready", "oT_ready", "v_ready", "v_init", "ob_ready", "rc_done", "chain"))
        out_st = [sem(f"out_st{u}") for u in range(2)]
        USES0, USES = NMAX + 1, NMAX + EXTRA
        EXP_CREDIT, AV_CREDIT, USE_CREDIT, OT_CREDIT, OUT_CREDIT = 2, 4, 2, 1, 16
        block = ctx.enter_context(nc.Block())

        def bank(base, u, j):
            return (base + USES * u + j) % 2

        @block.sync
        def _(sp):
            def load_stacks(n, u):
                r = bass.ds(n * HD, HD)
                for dst, parts in ((q[u], ("q_hi", "q_hi", "q_lo")), (k[u], ("k_hi", "k_lo", "k_hi"))):
                    for i, part in enumerate(parts):
                        sp.dma_start(dst[i * HD:(i + 1) * HD, :].bitcast(F32), g[part][r, :]).then_inc(stack_in[u], 16)

            def max_row(n, u):
                sp.wait_ge(nmT_ready, n + 1)
                for part in range(2):
                    sp.dma_start(q[u][STK + part:STK + part + 1, :].bitcast(F32),
                                 nmT[part * KT:(part + 1) * KT, :].bitcast(F32)).then_inc(row_in[u], 16)

            for u in range(2):
                sp.sem_inc(out_st[u], OUT_CREDIT)
            sp.wait_ge(ones_ready, 2)
            load_stacks(0, 0)
            max_row(0, 0)

            def load_next(n, u):
                if not isinstance(n, int):
                    sp.wait_ge(sc_done, n * SLOTS)
                load_stacks(n + 1, 1 - u)

            def store(n, u):
                sp.wait_ge(ob_ready, (n + 1) * NQB)
                dst = g["attn_scratch"][bass.ds((n // H) * T, T), bass.ds((n % H) * HD, HD)].rearrange("(t p) d -> p t d", p=P)
                sp.dma_start(dst, ob[u][:, :, :]).then_inc(out_st[u], 16)

            load_next(0, 0)
            max_row(1, 1)
            with sp.Fori(0, NH // 2 - 1) as i:
                for n, u in ((2 * i + 1, 1), (2 * i + 2, 0)):
                    load_next(n, u)
                    store(n - 1, 1 - u)
                    max_row(n + 1, 1 - u)
            store(NH - 2, 0)
            store(NH - 1, 1)
            for u in range(2):
                sp.wait_ge(out_st[u], 16 * NH // 2 + OUT_CREDIT)

        @block.gpsimd
        def _(pool):
            for u in range(2):
                pool.memset(vst[u][:, :, :], 0.0).then_inc(v_init, 1)
                pool.wait_ge(v_init, 2 * u + 1)
                pool.memset(vst[u][:, :, HD:HD + 1], 1.0).then_inc(v_init, 1)
            pool.wait_ge(v_init, 4)
            pool.tensor_copy(vst[0][:, :, 0:HD], V[:, 0, :, :]).then_inc(v_ready, 1)

            with pool.Fori(0, B) as b:
                with pool.Fori(0, H // 2) as hp:
                    for u in range(2):
                        h = hp * 2 + u
                        n = b * H + h
                        pool.wait_ge(av_done, n * SLOTS + AV_CREDIT)
                        nxt = n + 1 if u == 0 else (n + 1) % NH
                        pool.tensor_copy(vst[1 - u][:, :, 0:HD], V[:, bass.ds(nxt, 1), :, :].rearrange("p a t d -> p (a t) d")
                                         ).then_inc(v_ready, 1)

        @block.scalar
        def _(act):
            act.sem_inc(exp_done, EXP_CREDIT)

            def head(n, u):
                for s in range(SLOTS):
                    act.wait_ge(sc_done, n * SLOTS + s + 1)
                    act.wait_ge(av_done, n * SLOTS + s + 1)
                    act.activation(pr[s % 4][:, :], sc[s % 2][:, :], ACT.Exp, scale=SCALE).then_inc(exp_done, 1)

            with act.Fori(0, NH // 2) as i:
                head(2 * i, 0)
                head(2 * i + 1, 1)

        @block.tensor
        def _(pe):
            pe.sem_inc(av_done, AV_CREDIT)

            def scores(n, u, s):
                pe.wait_ge(exp_done, n * SLOTS + s - 1 + EXP_CREDIT)
                qb, m = s // KT, s % KT
                for x in range(2):
                    last = pe.matmul(sc[s % 2][:, x * 512:(x + 1) * 512], k[u][0:STK + 2, m * P:(m + 1) * P],
                                     q[u][0:STK + 2, qb * QB + x * 512:qb * QB + (x + 1) * 512], start=True, stop=True)
                last.then_inc(sc_done, 1)

            def one_max(u, kk, use, bk):
                pe.wait_ge(use_free, use + 1)
                qt, kc = kk // (T // MAXW), kk % (T // MAXW)
                pe.matmul(shared[bk][:, :], q[u][0:STK, qt * P:(qt + 1) * P],
                          k[u][0:STK, kc * MAXW:(kc + 1) * MAXW], start=True, stop=True).then_inc(use_done, 1)

            pe.wait_ge(stack_in[0], 96)
            for kk in range(NMAX):
                one_max(0, kk, kk, kk % 2)
            pe.wait_ge(nm_ready, 1)
            pe.wait_ge(use_free, NMAX + 1)
            pe.transpose(shared[NMAX % 2][0:2 * KT, 0:P], nm[:, :, :].rearrange("p a t -> p (a t)"), ident[:, :]).then_inc(use_done, 1)
            pe.wait_ge(row_in[0], 32)
            scores(0, 0, 0)

            def head(n, u, half, has_next):
                base = USES0 + n * USES
                j = 0
                pe.wait_ge(v_ready, n + 1)
                for s in range(SLOTS):
                    if s + 1 < SLOTS:
                        scores(n, u, s + 1)
                    elif has_next:
                        pe.wait_ge(row_in[1 - u], 32 * (half + 1 + u))
                        scores(n + 1, 1 - u, 0)
                    if has_next and PLAN[s]:
                        if s == MAX_FROM:
                            pe.wait_ge(stack_in[1 - u], 96 * (half + 1 + u))
                        for kk in PLAN[s]:
                            one_max(1 - u, kk, base + j, bank(USES0, u, j))
                            j += 1
                    if has_next and s == ROW_SLOT:
                        pe.wait_ge(nm_ready, n + 2)
                        pe.wait_ge(use_free, base + j + 1)
                        pe.transpose(shared[bank(USES0, u, j)][0:2 * KT, 0:P], nm[:, :, :].rearrange("p a t -> p (a t)"),
                                     ident[:, :]).then_inc(use_done, 1)
                        j += 1
                    if s == O_SLOT:
                        j = out_transposes(n, u, base, j, 0)
                    qb, m = s // KT, s % KT
                    if m == 0:
                        pe.wait_ge(oT_ready, n * NQB + OT_CREDIT)
                    pe.wait_ge(exp_done, n * SLOTS + s + 1 + EXP_CREDIT)
                    for x in range(2):
                        last = pe.matmul(av[qb][x * VW:(x + 1) * VW, :], vst[u][:, m, :], pr[s % 4][:, x * 512:(x + 1) * 512],
                                         start=(m == 0), stop=(m == KT - 1))
                    last.then_inc(av_done, 1)
                return out_transposes(n, u, base, j, 1)

            def out_transposes(n, u, base, j, qb):
                pe.wait_ge(oT_ready, n * NQB + qb + 1 + OT_CREDIT)
                pe.wait_ge(use_free, base + j + 1)
                for t in range(4):
                    last = pe.transpose(shared[bank(USES0, u, j)][:, t * P:(t + 1) * P], oT[qb][:, t * P:(t + 1) * P], ident[:, :])
                last.then_inc(use_done, 1)
                return j + 1

            with pe.Fori(0, NH // 2 - 1) as i:
                assert head(2 * i, 0, i, True) == USES
                head(2 * i + 1, 1, i, True)
            head(NH - 2, 0, NH // 2 - 1, True)
            head(NH - 1, 1, NH // 2 - 1, False)

        @block.vector
        def _(dve):
            for u in range(2):
                dve.memset(k[u][96:STK + 2, :].bitcast(F32), 1.0).then_inc(ones_ready, 1)
            dve.sem_inc(use_free, USE_CREDIT)
            dve.sem_inc(oT_ready, OT_CREDIT)

            def one_max(n_use, kk, bk):
                dve.wait_ge(use_done, n_use + 1)
                qt, kc = kk // (T // MAXW), kk % (T // MAXW)
                dve.tensor_reduce(mxp[:, qt, kc:kc + 1], shared[bk][:, :], op=ALU.max, axis=AX.X).then_inc(use_free, 1)

            def neg_max(n, n_use):
                dve.wait_ge(use_free, n_use + USE_CREDIT)
                c = Chain(dve, chain, 3 * n)
                c.do(dve.tensor_reduce(mx[:, :], mxp[:, :, :], op=ALU.max, axis=AX.X))
                c.do(dve.tensor_scalar(nmr[:, 0, :], mx[:, :], -1.0, None, ALU.mult))
                c.do(dve.scalar_tensor_tensor(out=nmr[:, 1, :], in0=mx[:, :], scalar=-1.0, in1=nmr[:, 0, :].bitcast(F32),
                                              op0=ALU.mult, op1=ALU.subtract))
                dve.tensor_copy(nm[:, :, :], nmr[:, :, :].bitcast(F32)).then_inc(nm_ready, 1)

            def row_copy(n, n_use, bk, gate):
                dve.wait_ge(use_done, n_use + 1)
                if gate is not None:
                    dve.wait_ge(*gate)
                dve.tensor_copy(nmT[:, :], shared[bk][0:2 * KT, 0:P]).then_inc(nmT_ready, 1)
                dve.wait_ge(nmT_ready, n + 1)
                dve.sem_inc(use_free, 1)

            for kk in range(NMAX):
                one_max(kk, kk, kk % 2)
            neg_max(0, NMAX)
            row_copy(0, NMAX, NMAX % 2, None)

            def evacuate(n, qb):
                dve.wait_ge(av_done, n * SLOTS + (qb + 1) * KT + AV_CREDIT)
                dve.tensor_copy(oT[qb][:, :], av[qb][:, :]).then_inc(oT_ready, 1)

            def normalise(n, u, half, n_use, bk, qb):
                dve.wait_ge(use_done, n_use + 1)
                ps = shared[bk][:, :].rearrange("p (t x c) -> p x t c", x=2, c=VW)
                dve.reciprocal(rc[:, :, :], ps[:, :, :, HD]).then_inc(rc_done, 1)
                dve.wait_ge(rc_done, n * NQB + qb + 1)
                if qb == 0:
                    dve.wait_ge(out_st[u], 16 * half + OUT_CREDIT)
                o = ob[u][:, qb * 8:(qb + 1) * 8, :].rearrange("p (x t) d -> p x t d", x=2)
                for x in range(2):
                    last = dve.tensor_tensor(o[:, x], ps[:, x, :, 0:HD],
                                             rc[:, x, :].rearrange("p (t a) -> p t a", a=1).broadcast_to([P, 4, HD]), ALU.mult)
                last.then_inc(ob_ready, 1)
                dve.wait_ge(ob_ready, n * NQB + qb + 1)
                dve.sem_inc(use_free, 1)

            def head(n, u, half, has_next):
                base = USES0 + n * USES
                j = 0
                for s in range(SLOTS):
                    if s == KT + 1:
                        evacuate(n, 0)
                    if has_next:
                        for kk in PLAN[s]:
                            one_max(base + j, kk, bank(USES0, u, j))
                            j += 1
                        if s == LAST_MAX:
                            neg_max(n + 1, base + j)
                        if s == ROW_SLOT:
                            row_copy(n + 1, base + j, bank(USES0, u, j), (row_in[u], 32 * (half + 1)))
                            j += 1
                    if s == O_SLOT:
                        normalise(n, u, half, base + j, bank(USES0, u, j), 0)
                        j += 1
                evacuate(n, 1)
                normalise(n, u, half, base + j, bank(USES0, u, j), 1)

            with dve.Fori(0, NH // 2 - 1) as i:
                head(2 * i, 0, i, True)
                head(2 * i + 1, 1, i, True)
            head(NH - 2, 0, NH // 2 - 1, True)
            head(NH - 1, 1, NH // 2 - 1, False)


def mlp(nc, io, g, out):
    HR, WR = 3, 3
    with ExitStack() as ctx:
        sb = lambda name, shape, dt=F32: ctx.enter_context(nc.sbuf_tensor(name, shape, dt))
        sem = lambda name: ctx.enter_context(nc.semaphore("c_" + name))
        psum = lambda name, shape: ctx.enter_context(nc.psum_tensor(name, shape, F32))
        ident, modv, UT, URI = g["ident"], g["modv"], g["UT"], g["URI"]
        w1h = sb("w1_hi", [P, KC, HID], F32R)
        w1l = sb("w1_lo", [P, KC, HID], F32R)
        wph = sb("wp_hi", [P, KC, D], F32R)
        wpl = sb("wp_lo", [P, KC, D], F32R)
        w2 = sb("w2_ring", [P, WR, 2, D], F32R)
        xr = sb("x_resid", [P, TPB, D])
        oi = sb("attn_tok", [P, TPB, D])
        xo = sb("x_norm_out", [P, TPB, D])
        fT = sb("featT", [P, KC, BLK])
        fh = sb("featT_hi", [P, KC, BLK], F32R)
        fl = sb("featT_lo", [P, KC, BLK], F32R)
        hb = sb("hid", [P, 2, BLK])
        hh = sb("hid_hi", [P, 2, BLK], F32R)
        hl = sb("hid_lo", [P, 2, BLK], F32R)
        wT = sb("rotT", [RD, BLK])
        uri = sb("URI_cur", [P, KC, RD])
        bp, b2, b1 = sb("b_proj", [P, KC]), sb("b_fc2", [P, KC]), sb("b_fc1", [P, FT])
        gb = sb("gated_bias", [P, B, 2, KC])
        eps = sb("eps_c", [P, 1])
        st, mv = sb("st_c", [P, TPB, 2, 6]), sb("mv_c", [P, TPB, 2])
        sd, rs = sb("sd_c", [P, TPB]), sb("rs_c", [P, TPB])
        acc = psum("acc", [P, KC, 512])
        hp = [psum(f"hid_ps{i}", [P, BLK]) for i in range(HR)]
        names = ("w1_hi w1_lo wp_in wp_in2 wp_hi wp_lo bias_in bias_ready o_in x_in o_tr o_hi o_lo p_done p_ready b_done x2_ready "
                 "st_ready var_ready std_ready xn_ready tr_done xm_ready xs_ready h_done g_ready hh_ready hs_ready y_done y_ready b2_done x3_ready "
                 "t3_done x3T_ready uri_ready w_done wT_ready r_done xo_ready chain stage_free")
        s = Counts(sem, names.split(), ("y_done", "xo_ready", "g_ready", "hs_ready", "o_tr", "w_done"))
        st_out = Counts(sem, ["out_st"], ["out_st"], credit=16)
        w1_in = [sem(f"w1_in{i}") for i in range(2)]
        w2_in = [sem(f"w2_in{i}") for i in range(WR)]
        stages = (xr, oi)
        xv = io["x"].rearrange("b (k t p) d -> (b k) p t d", p=P, t=TPB)
        ov = out.rearrange("b (k t p) d -> (b k) p t d", p=P, t=TPB)
        av = g["attn_scratch"].rearrange("(k t p) d -> k p t d", p=P, t=TPB)
        block = ctx.enter_context(nc.Block())

        def flat(ap):
            return ap.rearrange("p t d -> p (t d)")

        @block.sync
        def _(sp):
            load_columns(sp, bp[:, :], io["L0_cond_b_proj"], s["bias_in"])
            load_columns(sp, b2[:, :], io["L0_cond_b_fc2"], s["bias_in"])
            sp.dma_start(b1[:, :], io["L0_cond_b_fc1"].rearrange("(f p) -> p f", p=P)).then_inc(s["bias_in"], 16)
            for c in range(KC):
                r = rows(c)
                if c >= 2:
                    s.wait(sp, "stage_free", c - 1)
                sp.dma_start(flat(stages[c % 2][0:r, :, :]), io["L0_cond_w_fc1"][c * P:c * P + r, :]).then_inc(w1_in[c % 2], 16)
                if c == 1:
                    for k in range(4):
                        sp.dma_start(xo[:, k, :], io["L0_cond_w_proj"][k * P:(k + 1) * P, :]).then_inc(s["wp_in"], 16)
            s.wait(sp, "wp_lo", 1)
            sp.dma_start(xo[0:rows(4), 0, :], io["L0_cond_w_proj"][4 * P:D, :]).then_inc(s["wp_in2"], 16)
            s.wait(sp, "stage_free", KC)
            with sp.Fori(0, NBLK) as it:
                s.wait(sp, "o_tr", it * KC)
                sp.dma_start(oi[:, :, :], av[bass.ds(it, 1)].rearrange("a p t d -> p (a t) d")).then_inc(s["o_in"], 16)
                for f in range(FT):
                    s.wait(sp, "y_done", it * FT + max(0, f - WR + 1))
                    sp.dma_start(w2[:, f % WR, :, :].bitcast(F32), g["w2_split"][:, f, :, :]).then_inc(w2_in[f % WR], 16)

        @block.gpsimd
        def _(pool):
            with pool.Fori(0, NBLK) as it:
                s.wait(pool, "w_done", it)
                pool.tensor_copy(uri[:, :, :], URI[:, bass.ds(it // BPB, 1), :, :].rearrange("p a c d -> p (a c) d")).then_inc(s["uri_ready"], 1)

        @block.scalar
        def _(act):
            s.give(act, "g_ready")
            st_out.give(act, "out_st")
            for c in range(KC):
                r = rows(c)
                act.wait_ge(w1_in[c % 2], 16 * (c // 2 + 1))
                act.activation(w1h[0:r, c, :], flat(stages[c % 2][0:r, :, :]), ACT.Copy).then_inc(s["w1_hi"], 1)
            for c in range(KC):
                r = rows(c)
                s.wait(act, "wp_in", 64) if c < 4 else s.wait(act, "wp_in2", 16)
                act.activation(wph[0:r, c, :], xo[0:r, c % 4, :], ACT.Copy).then_inc(s["wp_hi"], 1)
            s.wait(act, "bias_ready", 1)
            s.wait(act, "stage_free", KC)
            with act.Fori(0, NBLK) as it:
                b = bass.ds(it // BPB, 1)

                s.wait(act, "xo_ready", it * TPB)
                act.dma_start(xr[:, :, :], xv[bass.ds(it, 1)].rearrange("a p t d -> p (a t) d")).then_inc(s["x_in"], 16)

                def column(sec, r, c):
                    return modv[0:r, b, sec, c:c + 1].rearrange("p a b -> p (a b)")

                def gated(k, r, c):
                    return gb[0:r, b, k, c:c + 1].rearrange("p a b -> p (a b)")

                for c in range(KC):
                    r = rows(c)
                    s.wait(act, "o_tr", it * KC + c + 1)
                    act.activation(fh[0:r, c, :], acc[0:r, c, :], ACT.Copy).then_inc(s["o_hi"], 1)
                for m in range(KC):
                    r = rows(m)
                    s.wait(act, "p_done", it * KC + m + 1)
                    act.activation(fT[0:r, m, :], hp[m % HR][0:r, :], ACT.Identity, bias=gated(0, r, m),
                                   scale=column(GATE_A, r, m)).then_inc(s["p_ready"], 1)
                s.wait(act, "var_ready", it + 1)
                act.activation(sd[:, :], mv[:, :, 1], ACT.Sqrt, bias=eps[:, :]).then_inc(s["std_ready"], 1)
                for c in range(KC):
                    r = rows(c)
                    s.wait(act, "tr_done", it * KC + c + 1)
                    act.activation(fT[0:r, c, :], acc[0:r, c, :], ACT.Identity, bias=column(SHIFT_F, r, c),
                                   scale=column(SCALE_F, r, c)).then_inc(s["xm_ready"], 1)
                for f in range(FT):
                    s.wait(act, "h_done", it * FT + f + 1)
                    s.wait(act, "hs_ready", it * FT + max(0, f - 1))
                    act.activation(hb[:, f % 2, :], hp[f % HR][:, :], ACT.Gelu_apprx_tanh, bias=b1[:, f:f + 1]).then_inc(s["g_ready"], 1)
                s.wait(act, "y_done", it * FT + FT)
                for m in range(KC):
                    r = rows(m)
                    act.activation(fT[0:r, m, :], acc[0:r, m, :], ACT.Identity, bias=gated(1, r, m),
                                   scale=column(GATE_F, r, m)).then_inc(s["y_ready"], 1)
                for c in range(KC):
                    r = rows(c)
                    s.wait(act, "t3_done", it * KC + c + 1)
                    act.activation(fT[0:r, c, :], acc[0:r, c, :], ACT.Copy).then_inc(s["x3T_ready"], 1)
                s.wait(act, "w_done", it + 1)
                act.activation(wT[:, :], hp[0][0:RD, :], ACT.Copy).then_inc(s["wT_ready"], 1)
                s.wait(act, "xo_ready", it * TPB + TPB)
                act.dma_start(ov[bass.ds(it, 1)].rearrange("a p t d -> p (a t) d"), xo[:, :, :]).then_inc(st_out["out_st"], 16)
            st_out.wait(act, "out_st", 16 * NBLK)

        @block.tensor
        def _(pe):
            s.give(pe, "y_done", "o_tr", "w_done")
            s.wait(pe, "wp_lo", KC)
            s.wait(pe, "w1_lo", KC)

            def to_features(src, c, done):
                for t in range(TPB):
                    last = pe.transpose(acc[0:rows(c), c, t * P:(t + 1) * P], src[:, t, c * P:c * P + rows(c)], ident[:, :])
                last.then_inc(done, 1)

            def to_tokens(t, done):
                for c in range(KC):
                    r = rows(c)
                    bk, col = divmod((t % 2) * 1024 + c * P, 512)
                    last = pe.transpose(acc[:, bk, col:col + r], fT[0:r, c, t * P:(t + 1) * P], ident[0:r, 0:r])
                last.then_inc(done, 1)

            with pe.Fori(0, NBLK) as it:
                s.wait(pe, "o_in", it * 16 + 16)
                s.wait(pe, "xo_ready", it * TPB)
                for c in range(KC):
                    to_features(oi, c, s["o_tr"])
                s.wait(pe, "o_lo", it * KC + KC)
                for m in range(KC):
                    r = rows(m)
                    if m >= HR:
                        s.wait(pe, "p_ready", it * KC + m - HR + 1)
                    for c in range(KC):
                        k = rows(c)
                        for n, (w, xx) in enumerate(((wph, fh), (wph, fl), (wpl, fh))):
                            last = pe.matmul(hp[m % HR][0:r, :], w[0:k, c, m * P:m * P + r], xx[0:k, c, :],
                                             start=(c == 0 and n == 0), stop=(c == KC - 1 and n == 2))
                    last.then_inc(s["p_done"], 1)
                s.wait(pe, "p_ready", it * KC + KC)
                for t in range(TPB):
                    if t >= 2:
                        s.wait(pe, "x2_ready", it * TPB + t - 1)
                    to_tokens(t, s["b_done"])
                s.wait(pe, "xn_ready", it + 1)
                for c in range(KC):
                    to_features(xo, c, s["tr_done"])
                s.wait(pe, "xs_ready", it * KC + KC)

                def hidden(f):
                    s.wait(pe, "g_ready", it * FT + max(0, f - HR + 1))
                    for c in range(KC):
                        k = rows(c)
                        for n, (w, xx) in enumerate(((w1h, fh), (w1h, fl), (w1l, fh))):
                            last = pe.matmul(hp[f % HR][:, :], w[0:k, c, f * P:(f + 1) * P], xx[0:k, c, :],
                                             start=(c == 0 and n == 0), stop=(c == KC - 1 and n == 2))
                    last.then_inc(s["h_done"], 1)

                hidden(0)
                for f in range(FT):
                    if f + 1 < FT:
                        hidden(f + 1)
                    s.wait(pe, "hs_ready", it * FT + f + 1)
                    pe.wait_ge(w2_in[f % WR], it * (16 * FT // WR) + 16 * (f // WR + 1))
                    for m in range(KC):
                        r = rows(m)
                        for n, (part, xx) in enumerate(((0, hh), (0, hl), (1, hh))):
                            last = pe.matmul(acc[0:r, m, :], w2[:, f % WR, part, m * P:m * P + r], xx[:, f % 2, :],
                                             start=(f == 0 and n == 0), stop=(f == FT - 1 and n == 2))
                    last.then_inc(s["y_done"], 1)
                s.wait(pe, "y_ready", it * KC + KC)
                for t in range(TPB):
                    if t >= 2:
                        s.wait(pe, "x3_ready", it * TPB + t - 1)
                    to_tokens(t, s["b2_done"])
                s.wait(pe, "x3_ready", it * TPB + TPB)
                for c in range(KC):
                    to_features(xr, c, s["t3_done"])
                s.wait(pe, "x3T_ready", it * KC + KC)
                s.wait(pe, "uri_ready", it + 1)
                for c in range(KC):
                    k = rows(c)
                    last = pe.matmul(hp[0][0:RD, :], uri[0:k, c, :], fT[0:k, c, :], start=(c == 0), stop=(c == KC - 1))
                last.then_inc(s["w_done"], 1)
                s.wait(pe, "wT_ready", it + 1)
                for t in range(TPB):
                    if t >= 2:
                        s.wait(pe, "xo_ready", it * TPB + t - 1)
                    for h in range(2):
                        last = pe.matmul(acc[:, 2 * (t % 2) + h, 0:HALF], wT[:, t * P:(t + 1) * P], UT[:, h * HALF:(h + 1) * HALF],
                                         start=True, stop=True)
                    last.then_inc(s["r_done"], 1)

        @block.vector
        def _(dve):
            s.give(dve, "xo_ready", "hs_ready")
            dve.memset(eps[:, :], LN_EPS)
            for c in range(KC):
                r = rows(c)
                s.wait(dve, "w1_hi", c + 1)
                dve.tensor_tensor(w1l[0:r, c, :], flat(stages[c % 2][0:r, :, :]), w1h[0:r, c, :].bitcast(F32), ALU.subtract).then_inc(s["w1_lo"], 1)
                s.wait(dve, "w1_lo", c + 1)
                dve.sem_inc(s["stage_free"], 1)
            for c in range(KC):
                r = rows(c)
                s.wait(dve, "wp_hi", c + 1)
                dve.tensor_tensor(wpl[0:r, c, :], xo[0:r, c % 4, :], wph[0:r, c, :].bitcast(F32), ALU.subtract).then_inc(s["wp_lo"], 1)
            s.wait(dve, "bias_in", 80)
            for r, c0, c1 in ((P, 0, KC - 1), (rows(KC - 1), KC - 1, KC)):
                for b in range(B):
                    for k, (sec, bias) in enumerate(((GATE_A, bp), (GATE_F, b2))):
                        last = dve.tensor_tensor(gb[0:r, b, k, c0:c1], modv[0:r, b, sec, c0:c1], bias[0:r, c0:c1], ALU.mult)
            last.then_inc(s["bias_ready"], 1)
            s.wait(dve, "wp_lo", KC)
            with dve.Fori(0, NBLK) as it:
                ch = Chain(dve, s["chain"], it * 2)

                def add_tokens(t, done, x_done):
                    s.wait(dve, done, it * TPB + t + 1)
                    pair = acc[:, :, :].rearrange("p a b -> p (a b)")[:, (t % 2) * 1024:(t % 2) * 1024 + D]
                    dve.tensor_tensor(xr[:, t, :], pair, xr[:, t, :], ALU.add).then_inc(s[x_done], 1)

                for c in range(KC):
                    r = rows(c)
                    s.wait(dve, "o_hi", it * KC + c + 1)
                    dve.tensor_tensor(fl[0:r, c, :], acc[0:r, c, :], fh[0:r, c, :].bitcast(F32), ALU.subtract).then_inc(s["o_lo"], 1)
                s.wait(dve, "x_in", it * 16 + 16)
                for t in range(TPB):
                    add_tokens(t, "b_done", "x2_ready")
                s.wait(dve, "x2_ready", it * TPB + TPB)
                for t in range(TPB):
                    for h in range(2):
                        last = dve.bn_stats(st[:, t, h, :], xr[:, t, h * HALF:(h + 1) * HALF])
                last.then_inc(s["st_ready"], 1)
                dve.drain()
                for t in range(TPB):
                    last = dve.bn_aggr(mv[:, t, :], st[:, t, :, :].rearrange("p a b -> p (a b)"))
                last.then_inc(s["var_ready"], 1)
                s.wait(dve, "std_ready", it + 1)
                ch.do(dve.reciprocal(rs[:, :], sd[:, :]))
                st_out.wait(dve, "out_st", it * 16)
                for t in range(TPB):
                    last = dve.tensor_scalar(xo[:, t, :], xr[:, t, :], mv[:, t, 0:1], rs[:, t:t + 1], ALU.subtract, ALU.mult)
                last.then_inc(s["xn_ready"], 1)
                for c in range(KC):
                    r = rows(c)
                    s.wait(dve, "xm_ready", it * KC + c + 1)
                    last = dve.tensor_copy(fh[0:r, c, :], fT[0:r, c, :])
                ch.do(last)
                for c in range(KC):
                    r = rows(c)
                    dve.tensor_tensor(fl[0:r, c, :], fT[0:r, c, :], fh[0:r, c, :].bitcast(F32), ALU.subtract).then_inc(s["xs_ready"], 1)
                for f in range(FT):
                    s.wait(dve, "g_ready", it * FT + f + 1)
                    s.wait(dve, "y_done", it * FT + max(0, f - 1))
                    dve.tensor_copy(hh[:, f % 2, :], hb[:, f % 2, :]).then_inc(s["hh_ready"], 1)
                    s.wait(dve, "hh_ready", it * FT + f + 1)
                    dve.tensor_tensor(hl[:, f % 2, :], hb[:, f % 2, :], hh[:, f % 2, :].bitcast(F32), ALU.subtract).then_inc(s["hs_ready"], 1)
                for t in range(TPB):
                    add_tokens(t, "b2_done", "x3_ready")
                for t in range(TPB):
                    s.wait(dve, "r_done", it * TPB + t + 1)
                    dve.tensor_tensor(xo[:, t, :].rearrange("p (a b) -> p a b", a=2),
                                      acc[:, 2 * (t % 2):2 * (t % 2) + 2, 0:HALF],
                                      xr[:, t, :].rearrange("p (a b) -> p a b", a=2), ALU.add).then_inc(s["xo_ready"], 1)


def program(nc, io, out, stop=None, dbg=None):
    with ExitStack() as keep:
        keep.enter_context(nc.allow_non_contiguous_dma(reason="short vectors, one value a partition"))
        sb = lambda name, shape, dt=F32: keep.enter_context(nc.sbuf_tensor(name, shape, dt))
        g = {
            "ident": sb("ident", [P, P]),
            "modv": sb("modv", [P, B, SECTIONS, KC]),
            "UT": sb("UT", [RD, D]),
            "URI": sb("URI", [P, B, KC, RD]),
            "w2_split": nc.dram_tensor("w2_split", [P, FT, 2, D], F32, kind="Internal").ap(),
            "skew_scratch": nc.dram_tensor("skew_scratch", [B, SKEW + 2 * RD], F32, kind="Internal").ap(),
            "attn_scratch": nc.dram_tensor("attn_scratch", [B * T, D], F32, kind="Internal").ap(),
        }
        for n in ("q_hi", "q_lo", "k_hi", "k_lo"):
            g[n] = nc.dram_tensor(n + "_scratch", [B * D, T], F32, kind="Internal").ap()
        conditioning(nc, io, g)
        if stop == "cond":
            return dbg(nc, g)
        rotation(nc, io, g)
        if stop == "rot":
            return dbg(nc, g)
        with nc.sbuf_tensor("V_all", [P, NH, KT, HD], F32) as V:
            g["V"] = V
            qkv(nc, io, g)
            if stop == "qkv":
                return dbg(nc, g)
            attention(nc, io, g)
        if stop == "attn":
            return dbg(nc, g)
        mlp(nc, io, g, out)


_INS = ["x", "cond_1152", "L0_cond_w_qkv", "L0_cond_b_qkv", "L0_cond_w_proj", "L0_cond_b_proj", "L0_cond_w_fc1",
        "L0_cond_b_fc1", "L0_cond_w_fc2", "L0_cond_b_fc2", "L0_cond_w_ada", "L0_cond_b_ada", "L1_cond_P",
        "L1_cond_W", "L1_cond_b"]


def kernel(**inputs):
    import numpy as _np
    import concourse.bacc as _bacc
    from concourse import mybir as _mybir
    from concourse.bass_utils import run_bass_kernel_spmd as _run

    nc = _bacc.Bacc("TRN2", target_bir_lowering=False, num_devices=1)
    arrays, io = {}, {}
    for name in _INS:
        a = _np.ascontiguousarray(inputs[name])
        arrays[f"in_{name}"] = a
        io[name] = nc.dram_tensor(f"in_{name}", a.shape, _mybir.dt.from_np(a.dtype), kind="ExternalInput").ap()
    out = nc.dram_tensor("out_0", (B, T, D), _mybir.dt.float32, kind="ExternalOutput").ap()
    program(nc, io, out)
    r = _run(nc, [arrays], core_ids=[0])
    return r.results[0]["out_0"]
```

```python
from contextlib import ExitStack

import concourse.bass as bass
from concourse import mybir

F32 = mybir.dt.float32
F32R = mybir.dt.float32r
ALU = mybir.AluOpType
ACT = mybir.ActivationFunctionType
AX = mybir.AxisListType

P = 128
B, T, D = 2, 2048, 576
H, HD = 16, 36
HID = 4 * D
RD = 64
SKEW = RD * (RD - 1) // 2
BLK = 512
TPB = BLK // P
NBLK = B * T // BLK
BPB = T // BLK
KC = 5
HALF = D // 2
FT = HID // P
NH = B * H
KT = T // P
QKT = 2 * D // P
LN_EPS = 1e-6
SECTIONS = 6
SHIFT_A, SCALE_A, GATE_A, SHIFT_F, SCALE_F, GATE_F = range(SECTIONS)


def rows(c):
    return min(P, D - c * P)


class Chain:

    def __init__(self, eng, sem, base=0):
        self.eng, self.sem, self.base, self.n = eng, sem, base, 0

    def mark(self, ins):
        ins.then_inc(self.sem, 1)
        self.n += 1

    def wait(self):
        self.eng.wait_ge(self.sem, self.base + self.n)

    def do(self, ins):
        self.mark(ins)
        self.wait()


class Counts:

    def __init__(self, sem, names, credited, credit=1):
        self.sems = {n: sem(n) for n in names}
        self.credit = {n: credit * (n in credited) for n in names}

    def __getitem__(self, name):
        return self.sems[name]

    def wait(self, eng, name, count):
        eng.wait_ge(self.sems[name], count + self.credit[name])

    def give(self, eng, *names):
        for n in names:
            eng.sem_inc(self.sems[n], self.credit[n])


def load_chunked(eng, dst, src, sem):
    full = (KC - 1) * P
    eng.dma_start(dst[:, 0:KC - 1, :], src[0:full, :].rearrange("(c p) n -> p c n", p=P)).then_inc(sem, 16)
    eng.dma_start(dst[0:D - full, KC - 1, :], src[full:D, :]).then_inc(sem, 16)


def load_columns(eng, dst, src, sem):
    full = (KC - 1) * P
    eng.dma_start(dst[:, 0:KC - 1], src[0:full].rearrange("(c p) -> p c", p=P)).then_inc(sem, 16)
    eng.dma_start(dst[0:D - full, KC - 1:KC], src[full:D].rearrange("(p a) -> p a", a=1)).then_inc(sem, 16)


def row(v):
    return v.rearrange("(a n) -> a n", a=1)


SQUARINGS, DEGREE = 10, 8
ML = RD + 1


def setup(nc, io, g):
    VT = 16
    VP = SKEW // VT
    PAD = RD
    PIECES = 3
    FP = FT // PIECES
    with ExitStack() as ctx:
        sb = lambda name, shape, dt=F32: ctx.enter_context(nc.sbuf_tensor(name, shape, dt))
        sem = lambda name: ctx.enter_context(nc.semaphore(name))
        psum = lambda name, shape: ctx.enter_context(nc.psum_tensor(name, shape, F32))
        ident, modv = g["ident"], g["modv"]
        G, M, PT, E, step, stepT, X2, one = (g[x] for x in ("G", "M", "UT", "E", "step", "stepT", "X2", "one"))
        half_mask = g["half_mask"]
        wa = sb("w_ada_sb", [P, KC, SECTIONS * D])
        condT = sb("condT", [P, KC, B])
        siluT = sb("siluT", [P, KC, B])
        badaT = sb("badaT", [P, SECTIONS, KC])
        w2 = sb("w2_raw", [P, FT, D])
        w2h = sb("w2_hi", [P, FP, D], F32R)
        w2l = sb("w2_lo", [P, FP, D], F32R)
        Pc = sb("Pc", [P, KC, RD])
        crow = sb("cond_rows", [B, D])
        srow = sb("silu_rows", [B, D])
        selb = sb("sel_batch", [B, B, VP])
        sbc = sb("silu_bcast", [VP, B, D])
        Wv = sb("W_skew", [VP, VT, D])
        junk = sb("junk", [VP, D])
        v = sb("v", [VP, B, VT])
        vT = sb("vT", [B * VT, VP])
        bvT = sb("b_skewT", [B * VT, VP])
        zpad = sb("zpad", [B, PAD])
        Au = sb("A_upper", [RD, B, RD])
        X = sb("X_skew", [RD, B, RD])
        Xn = sb("X_skew_neg", [RD, B, RD])
        E2 = sb("E_pair2", [RD, 2, B, RD])
        ps = psum("ps_ada", [P, SECTIONS, KC, B])
        pA, pB, pC = psum("pA", [P, 2, 512]), psum("pB", [P, 512]), psum("pC", [P, 512])
        cond_in, bada_in, w2_in, p_in, c_in, b_in = (sem(x) for x in ("cond_in", "bada_in", "w2_in", "P_in", "crow_in", "bskew_in"))
        wa_in = [sem(f"wa_in{s}") for s in range(SECTIONS)]
        w_ins = [sem(f"W_in{k}") for k in range(4)]
        silu_ready, ada_ready, mod_done = sem("silu_ready"), sem("ada_ready"), sem("mod_done")
        ident_zero, ident_ready, mask_ready, upper_ready = (sem(x) for x in ("ident_zero", "ident_ready", "mask_ready", "upper_ready"))
        hi_ready, lo_ready, w2_out = sem("w2_hi_ready"), sem("w2_lo_ready"), sem("w2_out")
        v_out, a_in, const_s = sem("v_out"), sem("A_in"), sem("const_chain")
        srow_ready, sbc_mm, sbc_ready, v_ready, vT_mm, vT_ready = (
            sem(x) for x in ("srow_ready", "sbc_mm", "sbc_ready", "v_ready", "vT_mm", "vT_ready"))
        gram_mm, pt_mm, auT_mm, x_ready, e_mm, e_ready, chain_s = (
            sem(x) for x in ("gram_mm", "pt_mm", "auT_mm", "x_ready", "e_mm", "e_ready", "setup_chain"))
        vs = g["skew_scratch"]
        block = ctx.enter_context(nc.Block())

        @block.sync
        def _(sp):
            sp.dma_start(crow[:, :], io["cond_1152"]).then_inc(c_in, 16)
            for k in range(4):
                n = VT // 4
                sp.dma_start(Wv[:, k * n:(k + 1) * n, :],
                             io["L1_cond_W"].rearrange("(t p) k -> p t k", p=VP)[:, k * n:(k + 1) * n, :]).then_inc(w_ins[k], 16)
            load_chunked(sp, Pc[:, :, :], io["L1_cond_P"], p_in)
            for b in range(B):
                sp.dma_start(bvT[b * VT:(b + 1) * VT, :], io["L1_cond_b"].rearrange("(t p) -> t p", p=VP)).then_inc(b_in, 16)
            for b in range(B):
                load_columns(sp, condT[:, :, b], io["cond_1152"][b, :], cond_in)
            bsec = io["L0_cond_b_ada"].rearrange("(s f) -> s f", s=SECTIONS)
            for s in range(SECTIONS):
                load_columns(sp, badaT[:, s, :], bsec[s, :], bada_in)
            for s in range(SECTIONS):
                load_chunked(sp, wa[:, :, s * D:(s + 1) * D], io["L0_cond_w_ada"][:, s * D:(s + 1) * D], wa_in[s])
            sp.dma_start(w2[:, :, :], io["L0_cond_w_fc2"].rearrange("(f p) n -> p f n", p=P)).then_inc(w2_in, 16)
            sp.wait_ge(mask_ready, 1)
            sp.dma_start(vs[:, 0:PAD], zpad[:, :]).then_inc(v_out, 16)
            sp.dma_start(vs[:, PAD + SKEW:PAD + SKEW + PAD], zpad[:, :]).then_inc(v_out, 16)
            sp.wait_ge(vT_ready, 1)
            for b in range(B):
                sp.dma_start(vs[b, PAD:PAD + SKEW].rearrange("(t p) -> t p", p=VP),
                             vT[b * VT:(b + 1) * VT, :]).then_inc(v_out, 16)
            sp.wait_ge(v_out, 64)
            for i in range(RD):
                start = PAD + (RD - 2) * i - i * (i - 1) // 2 - 1
                sp.dma_start(Au[i:i + 1, :, :], vs[:, start:start + RD].rearrange("(a b) c -> a b c", a=1)).then_inc(a_in, 16)
            for k in range(PIECES):
                sp.wait_ge(hi_ready, k + 1)
                sp.wait_ge(lo_ready, k + 1)
                for part, src in enumerate((w2h, w2l)):
                    sp.dma_start(g["w2_split"][:, k * FP:(k + 1) * FP, part, :], src[:, :, :].bitcast(F32)).then_inc(w2_out, 16)
                sp.wait_ge(w2_out, 32 * (k + 1))

        @block.gpsimd
        def _(pool):
            pool.memset(ident[:, :], 0.0).then_inc(ident_zero, 1)
            pool.wait_ge(ident_zero, 1)
            pool.affine_select(out=ident[:, :], in_=ident[:, :], compare_op=ALU.not_equal, fill=1.0,
                               base=0, pattern=[[-1, P]], channel_multiplier=1).then_inc(ident_ready, 1)
            ch = Chain(pool, const_s)
            ch.do(pool.memset(selb[:, :, :], 0.0))
            ch.do(pool.affine_select(out=selb[:, :, :], in_=selb[:, :, :], compare_op=ALU.not_equal, fill=1.0,
                                     base=0, pattern=[[-1, B], [0, VP]], channel_multiplier=1))
            ch.do(pool.memset(M[:, :], 0.0))
            ch.do(pool.memset(X2[:, :, :], 0.0))
            pool.memset(zpad[:, :], 0.0).then_inc(mask_ready, 1)
            ch.do(pool.memset(half_mask[:, :], 1.0))
            ch.do(pool.affine_select(out=half_mask[:, :], in_=half_mask[:, :], compare_op=ALU.not_equal, fill=0.5,
                                     base=0, pattern=[[-1, RD]], channel_multiplier=1))
            ch.do(pool.affine_select(out=half_mask[:, :], in_=half_mask[:, :], compare_op=ALU.is_ge, fill=0.0,
                                     base=0, pattern=[[1, RD]], channel_multiplier=-1))
            for m in (step, stepT):
                ch.do(pool.memset(m[:, :], 0.0))
                ch.do(pool.affine_select(out=m[:, 0:RD], in_=m[:, 0:RD], compare_op=ALU.not_equal, fill=1.0,
                                         base=-1, pattern=[[-1, RD]], channel_multiplier=1))
            ch.do(pool.memset(step[0:1, RD - 1:RD], 1.0))
            pool.memset(one[:, :], 1.0)
            pool.wait_ge(a_in, 16 * RD)
            pool.affine_select(out=Au[:, :, :], in_=Au[:, :, :], compare_op=ALU.is_gt, fill=0.0,
                               base=0, pattern=[[0, B], [1, RD]], channel_multiplier=-1).then_inc(upper_ready, 1)

        @block.scalar
        def _(act):
            act.wait_ge(c_in, 16)
            act.activation(srow[:, :], crow[:, :], ACT.Silu).then_inc(srow_ready, 1)
            act.wait_ge(cond_in, 64)
            for r, c0, c1 in ((P, 0, KC - 1), (rows(KC - 1), KC - 1, KC)):
                act.activation(siluT[0:r, c0:c1, :], condT[0:r, c0:c1, :], ACT.Silu).then_inc(silu_ready, 1)
            for b in range(B):
                for h in range(2):
                    act.wait_ge(sbc_mm, 2 * b + h + 1)
                    act.activation(sbc[:, b, h * HALF:(h + 1) * HALF], pA[0:VP, h, 0:HALF], ACT.Copy).then_inc(sbc_ready, 1)
            act.wait_ge(w2_in, 16)
            for k in range(PIECES):
                if k:
                    act.wait_ge(w2_out, 32 * k)
                act.activation(w2h[:, :, :], w2[:, k * FP:(k + 1) * FP, :], ACT.Copy).then_inc(hi_ready, 1)

        @block.tensor
        def _(pe):
            pe.wait_ge(srow_ready, 1)
            pe.wait_ge(mask_ready, 1)
            for b in range(B):
                for h in range(2):
                    if b:
                        pe.wait_ge(sbc_ready, h + 1)
                    pe.matmul(pA[0:VP, h, 0:HALF], selb[:, b, :], srow[:, h * HALF:(h + 1) * HALF],
                              start=True, stop=True).then_inc(sbc_mm, 1)
            pe.wait_ge(p_in, 32)
            for c in range(KC):
                last = pe.matmul(pB[0:RD, 0:RD], Pc[0:rows(c), c, :], Pc[0:rows(c), c, :], start=(c == 0), stop=(c == KC - 1))
            last.then_inc(gram_mm, 1)
            pe.wait_ge(sbc_ready, 4)
            pe.wait_ge(ident_ready, 1)
            for c in range(KC):
                last = pe.transpose(pA[0:RD, c // 4, (c % 4) * P:(c % 4) * P + rows(c)], Pc[0:rows(c), c, :],
                                    ident[0:rows(c), 0:rows(c)])
            last.then_inc(pt_mm, 1)
            pe.wait_ge(v_ready, 1)
            pe.transpose(pC[0:B * VT, 0:VP], v[:, :, :].rearrange("p b t -> p (b t)"), ident[0:VP, 0:VP]).then_inc(vT_mm, 1)
            pe.wait_ge(silu_ready, 2)
            for s in range(SECTIONS):
                pe.wait_ge(wa_in[s], 32)
                for m in range(KC):
                    for c in range(KC):
                        last = pe.matmul(ps[0:rows(m), s, m, :],
                                         wa[0:rows(c), c, s * D + m * P:s * D + m * P + rows(m)],
                                         siluT[0:rows(c), c, :], start=(c == 0), stop=(c == KC - 1))
            last.then_inc(ada_ready, 1)
            pe.wait_ge(upper_ready, 1)
            for b in range(B):
                last = pe.transpose(pB[0:RD, b * RD:(b + 1) * RD], Au[:, b, :], ident[0:RD, 0:RD])
            last.then_inc(auT_mm, 1)
            pe.wait_ge(x_ready, 1)
            for k in range(DEGREE - 1):
                pe.wait_ge(e_ready, k + 1)
                for b in range(B):
                    pe.matmul(pC[0:RD, b * RD:(b + 1) * RD], Xn[:, b, :], E[:, 0, b, :], start=True, stop=True)
                    last = pe.matmul(pC[0:RD, (B + b) * RD:(B + b + 1) * RD], X[:, b, :], E[:, 1, b, :], start=True, stop=True)
                last.then_inc(e_mm, 1)
            for k in range(SQUARINGS):
                src = (E, E2)[k % 2]
                pe.wait_ge(e_ready, DEGREE + k)
                for b in range(B):
                    pe.matmul(pC[0:RD, b * RD:(b + 1) * RD], src[:, 1, b, :], src[:, 0, b, :], start=True, stop=True)
                    last = pe.matmul(pC[0:RD, (B + b) * RD:(B + b + 1) * RD], src[:, 0, b, :], src[:, 1, b, :], start=True, stop=True)
                last.then_inc(e_mm, 1)

        @block.vector
        def _(dve):
            ch = Chain(dve, chain_s)
            dve.wait_ge(gram_mm, 1)
            dve.wait_ge(mask_ready, 1)
            dve.wait_ge(ident_ready, 1)
            ch.do(dve.tensor_copy(G[:, :], pB[0:RD, 0:RD]))
            dve.tensor_copy(M[:, 0:RD], G[:, :])
            dve.tensor_copy(M[:, ML:ML + RD], ident[0:RD, 0:RD])
            dve.wait_ge(pt_mm, 1)
            dve.tensor_copy(PT[:, :], pA[0:RD, :, :].rearrange("p a b -> p (a b)")[:, 0:D])
            dve.wait_ge(sbc_ready, 4)
            for t in range(VT):
                if t % (VT // 4) == 0:
                    dve.wait_ge(w_ins[t // (VT // 4)], 16)
                for b in range(B):
                    ch.do(dve.tensor_tensor_reduce(out=junk[:, :], in0=Wv[:, t, :], in1=sbc[:, b, :], scale=1.0, scalar=0.0,
                                                   op0=ALU.mult, op1=ALU.add, accum_out=v[:, b, t:t + 1]))
            dve.sem_inc(v_ready, 1)
            dve.wait_ge(b_in, 32)
            dve.wait_ge(vT_mm, 1)
            dve.tensor_tensor(vT[:, :], pC[0:B * VT, 0:VP], bvT[:, :], ALU.add).then_inc(vT_ready, 1)
            dve.wait_ge(bada_in, 32 * SECTIONS)
            dve.wait_ge(ada_ready, 1)
            parts = ((P, 0, KC - 1), (rows(KC - 1), KC - 1, KC))
            for r, c0, c1 in parts:
                for b in range(B):
                    dve.tensor_tensor(modv[0:r, b, :, c0:c1], ps[0:r, :, c0:c1, b], badaT[0:r, :, c0:c1],
                                      ALU.add).then_inc(mod_done, 1)
            dve.wait_ge(mod_done, 4)
            for r, c0, c1 in parts:
                for s in (SCALE_A, SCALE_F):
                    dve.tensor_scalar(modv[0:r, :, s, c0:c1], modv[0:r, :, s, c0:c1], 1.0, None, ALU.add)
            dve.wait_ge(auT_mm, 1)
            ch.do(dve.tensor_tensor(X[:, :, :], Au[:, :, :], pB[0:RD, 0:B * RD].rearrange("p (b c) -> p b c", b=B), ALU.subtract))
            ch.do(dve.tensor_scalar(Xn[:, :, :], X[:, :, :], -1.0 / 2 ** SQUARINGS, None, ALU.mult))
            ch.do(dve.tensor_scalar(X[:, :, :], X[:, :, :], 1.0 / 2 ** SQUARINGS, None, ALU.mult))
            dve.sem_inc(x_ready, 1)
            ch.do(dve.tensor_scalar(E[:, 0, :, :], X[:, :, :], 1.0 / DEGREE, None, ALU.mult))
            dve.tensor_scalar(E[:, 1, :, :], Xn[:, :, :], 1.0 / DEGREE, None, ALU.mult).then_inc(e_ready, 1)
            pairs = pC[0:RD, 0:2 * B * RD].rearrange("p (e b c) -> p e b c", e=2, b=B)
            for k in range(DEGREE - 1):
                dve.wait_ge(e_mm, 1 + k)
                ch.do(dve.tensor_tensor(E2[:, 0, :, :], pairs[:, 0], X[:, :, :], ALU.add))
                ch.do(dve.tensor_tensor(E2[:, 1, :, :], pairs[:, 1], Xn[:, :, :], ALU.add))
                dve.tensor_scalar(E[:, :, :, :], E2[:, :, :, :], 1.0 / (DEGREE - 1 - k), None, ALU.mult).then_inc(e_ready, 1)
            for k in range(SQUARINGS):
                src, dst = ((E, E2), (E2, E))[k % 2]
                dve.wait_ge(e_mm, DEGREE + k)
                dve.wait_ge(e_ready, DEGREE + k)
                dve.scalar_tensor_tensor(out=dst[:, :, :, :], in0=src[:, :, :, :], scalar=2.0, in1=pairs,
                                         op0=ALU.mult, op1=ALU.add).then_inc(e_ready, 1)
            for k in range(PIECES):
                dve.wait_ge(hi_ready, k + 1)
                if k:
                    dve.wait_ge(w2_out, 32 * k)
                dve.tensor_tensor(w2l[:, :, :], w2[:, k * FP:(k + 1) * FP, :],
                                  w2h[:, :, :].bitcast(F32), ALU.subtract).then_inc(lo_ready, 1)


def qkv(nc, io, g):
    V = g["V"]
    RING = 3
    ELIM = RD // NBLK
    with ExitStack() as ctx:
        sb = lambda name, shape, dt=F32: ctx.enter_context(nc.sbuf_tensor(name, shape, dt))
        sem = lambda name: ctx.enter_context(nc.semaphore(name))
        psum = lambda name, shape: ctx.enter_context(nc.psum_tensor(name, shape, F32))
        ident, modv = g["ident"], g["modv"]
        wh = sb("wqk_hi", [P, KC, 2 * D], F32R)
        wl = sb("wqk_lo", [P, KC, 2 * D], F32R)
        wv = sb("wv_sb", [P, KC, D])
        bqk = sb("bqk", [P, QKT])
        ones = sb("ones_row", [1, P])
        bvr = sb("bv_row", [1, D])
        bvb = sb("bv_bcast", [P, 2, HALF])
        eps = sb("eps", [P, 1])
        x = sb("x_blk", [P, TPB, D])
        xn = sb("x_norm", [P, TPB, D])
        stage = xn[:, :, :].rearrange("p t d -> p (t d)")[:, 0:2 * D]
        M, step = g["M"], g["step"]
        piv = sb("pivot", [1, 1])
        st = sb("ln_stats", [P, TPB, 2, 6])
        mv = sb("ln_mv", [P, TPB, 2])
        sd = sb("ln_std", [P, TPB])
        rs = sb("ln_rstd", [P, TPB])
        xm = sb("x_modT", [P, KC, BLK])
        xh = sb("x_modT_hi", [P, KC, BLK], F32R)
        xl = sb("x_modT_lo", [P, KC, BLK], F32R)
        oh = sb("qk_hi_out", [P, RING, BLK], F32R)
        ol = sb("qk_lo_out", [P, RING, BLK], F32R)
        tp = [psum(f"tp{i}", [P, BLK]) for i in range(2)]
        qk = [psum(f"qk{i}", [P, BLK]) for i in range(RING)]
        vp = [psum(f"vp{i}", [P, BLK]) for i in range(2)]
        el = psum("elim_ps", [P, BLK])
        names = ("w_in w_free wh_ready wl_ready wv_in bias_in ones_ready bvb_mm bvb_ready x_in x_used st_ready var_ready std_ready "
                 "xn_ready tr_done xm_ready xs_ready qk_done hi_ready lo_ready v_done v_ready chain elim_chain row_ready elim_mm elim_ready")
        s = Counts(lambda n: sem("a_" + n), names.split(), ("v_done", "xs_ready", "xm_ready", "v_ready", "lo_ready", "tr_done", "qk_done", "elim_ready"))
        rings = range(RING)
        outs = Counts(lambda n: sem("a_" + n), [f"out_{p}{i}" for p in ("hi", "lo") for i in rings],
                      [f"out_{p}{i}" for p in ("hi", "lo") for i in rings], credit=16)
        w_qkv, b_qkv = io["L0_cond_w_qkv"], io["L0_cond_b_qkv"]
        xv = io["x"].rearrange("b (k t p) d -> (b k) p t d", p=P, t=TPB)
        block = ctx.enter_context(nc.Block())

        @block.sync
        def _(sp):
            outs.give(sp, *outs.sems)
            sp.dma_start(bqk[:, :], b_qkv[0:2 * D].rearrange("(m p) -> p m", p=P)).then_inc(s["bias_in"], 16)
            sp.dma_start(bvr[:, :], row(b_qkv[2 * D:3 * D])).then_inc(s["bias_in"], 16)
            for c in range(KC):
                if c:
                    s.wait(sp, "w_free", c)
                sp.dma_start(stage[0:rows(c), :], w_qkv[c * P:c * P + rows(c), 0:2 * D]).then_inc(s["w_in"], 16)
                if c == 0:
                    sp.dma_start(x[:, :, :], xv[0]).then_inc(s["x_in"], 16)
                    load_chunked(sp, wv[:, :, :], w_qkv[:, 2 * D:3 * D], s["wv_in"])
            with sp.Fori(0, B) as b:
                with sp.Fori(0, BPB) as j:
                    it = b * BPB + j
                    for m in range(QKT):
                        if m == 1:
                            s.wait(sp, "x_used", it + 1)
                            sp.dma_start(x[:, :, :], xv[bass.ds((it + 1) % NBLK, 1)].rearrange("a p t d -> p (a t) d")
                                         ).then_inc(s["x_in"], 16)
                        for part, ready, src, out in (("q_hi", "hi_ready", oh, "out_hi"), ("q_lo", "lo_ready", ol, "out_lo")):
                            s.wait(sp, ready, it * QKT + m + 1)
                            f0 = m * P
                            nq = max(0, min(P, D - f0))
                            cols = bass.ds(j * BLK, BLK)
                            pieces = [(0, nq, part, f0)] if nq else []
                            pieces += [(nq, P, part.replace("q", "k"), f0 + nq - D)] if nq < P else []
                            for p0, p1, name, r0 in pieces:
                                sp.dma_start(g[name][bass.ds(b * D + r0, p1 - p0), cols],
                                             src[p0:p1, m % RING, :].bitcast(F32)).then_inc(outs[f"{out}{m % RING}"], 16)
            s.wait(sp, "x_in", 16 * (NBLK + 1))
            for out in ("out_hi", "out_lo"):
                for i in rings:
                    outs.wait(sp, f"{out}{i}", 16 * NBLK * (QKT // RING + (i == (QKT // 2) % RING)))

        @block.scalar
        def _(act):
            s.give(act, "xm_ready")
            for c in range(KC):
                s.wait(act, "w_in", 16 * (c + 1))
                act.activation(wh[0:rows(c), c, :], stage[0:rows(c), :], ACT.Copy).then_inc(s["wh_ready"], 1)
            s.wait(act, "bvb_mm", 1)
            for h in range(2):
                act.activation(bvb[:, h, :], vp[h][:, 0:HALF], ACT.Copy).then_inc(s["bvb_ready"], 1)
            s.wait(act, "bias_in", 32)
            with act.Fori(0, B) as b:
                with act.Fori(0, BPB) as j:
                    it = b * BPB + j
                    s.wait(act, "var_ready", it + 1)
                    act.activation(sd[:, :], mv[:, :, 1], ACT.Sqrt, bias=eps[:, :]).then_inc(s["std_ready"], 1)
                    s.wait(act, "v_done", it * 2 * TPB)
                    s.wait(act, "xs_ready", it * KC)
                    for c in range(KC):
                        r = rows(c)
                        s.wait(act, "tr_done", it * KC + c + 1)
                        act.activation(xm[0:r, c, :], tp[c % 2][0:r, :], ACT.Identity,
                                       bias=modv[0:r, bass.ds(b, 1), SHIFT_A, c:c + 1].rearrange("p a b -> p (a b)"),
                                       scale=modv[0:r, bass.ds(b, 1), SCALE_A, c:c + 1].rearrange("p a b -> p (a b)")
                                       ).then_inc(s["xm_ready"], 1)
                    for m in range(QKT):
                        s.wait(act, "qk_done", it * QKT + m + 1)
                        k, extra = m // RING, int(m % RING == (QKT // 2) % RING)
                        stores = it * (QKT // RING + extra) + k + int(extra and m > QKT // 2)
                        outs.wait(act, f"out_hi{m % RING}", stores * 16)
                        act.activation(oh[:, m % RING, :], qk[m % RING][:, :], ACT.Identity,
                                       bias=bqk[:, m:m + 1]).then_inc(s["hi_ready"], 1)

        @block.tensor
        def _(pe):
            s.give(pe, "v_done", "tr_done", "qk_done")
            s.wait(pe, "ones_ready", 1)
            s.wait(pe, "bias_in", 32)
            for h in range(2):
                last = pe.matmul(vp[h][:, 0:HALF], ones[:, :], bvr[:, h * HALF:(h + 1) * HALF], start=True, stop=True)
            last.then_inc(s["bvb_mm"], 1)
            s.wait(pe, "wv_in", 32)
            s.wait(pe, "wl_ready", KC)
            s.wait(pe, "bvb_ready", 2)
            with pe.Fori(0, NBLK) as it:
                s.wait(pe, "xn_ready", it + 1)
                for c in range(KC):
                    if c < KC - 1:
                        s.wait(pe, "xm_ready", it * KC + (max(0, c - 1) if c < KC - 2 else KC - 2))
                    for t in range(TPB):
                        last = pe.transpose(tp[c % 2][0:rows(c), t * P:(t + 1) * P], xn[:, t, c * P:c * P + rows(c)], ident[:, :])
                    last.then_inc(s["tr_done"], 1)
                s.wait(pe, "xm_ready", it * KC + KC)
                for t in range(TPB):
                    for h in range(2):
                        s.wait(pe, "v_ready", it * 2 * TPB + max(0, 2 * t + h - 1))
                        for c in range(KC):
                            last = pe.matmul(vp[h][:, 0:HALF], xm[0:rows(c), c, t * P:(t + 1) * P],
                                             wv[0:rows(c), c, h * HALF:(h + 1) * HALF], start=(c == 0), stop=(c == KC - 1))
                        last.then_inc(s["v_done"], 1)
                s.wait(pe, "xs_ready", it * KC + KC)
                for m in range(QKT):
                    s.wait(pe, "lo_ready", it * QKT + max(0, m - RING + 1))
                    for c in range(KC):
                        for n, (w, xx) in enumerate(((wh, xh), (wh, xl), (wl, xh))):
                            last = pe.matmul(qk[m % RING][:, :], w[0:rows(c), c, m * P:(m + 1) * P], xx[0:rows(c), c, :],
                                             start=(c == 0 and n == 0), stop=(c == KC - 1 and n == 2))
                    last.then_inc(s["qk_done"], 1)
                    if m:
                        s.wait(pe, "row_ready", it * ELIM + m)
                        pe.matmul(el[:, 0:ML + RD], step[:, :], M[:, 0:ML + RD], start=True, stop=True).then_inc(s["elim_mm"], 1)

        @block.vector
        def _(dve):
            s.give(dve, "xs_ready", "v_ready", "lo_ready", "elim_ready")
            dve.memset(ones[:, :], 1.0).then_inc(s["ones_ready"], 1)
            dve.memset(eps[:, :], LN_EPS)
            for c in range(KC):
                s.wait(dve, "wh_ready", c + 1)
                ins = dve.tensor_tensor(wl[0:rows(c), c, :], stage[0:rows(c), :], wh[0:rows(c), c, :].bitcast(F32), ALU.subtract)
                ins.then_inc(s["wl_ready"], 1)
                s.wait(dve, "wl_ready", c + 1)
                dve.sem_inc(s["w_free"], 1)
            s.wait(dve, "bvb_ready", 2)
            with dve.Fori(0, B) as b:
                with dve.Fori(0, BPB) as j:
                    it = b * BPB + j
                    ch = Chain(dve, s["chain"], it * 2)
                    s.wait(dve, "x_in", it * 16 + 16)
                    for t in range(TPB):
                        for h in range(2):
                            last = dve.bn_stats(st[:, t, h, :], x[:, t, h * HALF:(h + 1) * HALF])
                    last.then_inc(s["st_ready"], 1)
                    dve.drain()
                    for t in range(TPB):
                        last = dve.bn_aggr(mv[:, t, :], st[:, t, :, :].rearrange("p a b -> p (a b)"))
                    last.then_inc(s["var_ready"], 1)
                    s.wait(dve, "std_ready", it + 1)
                    ch.do(dve.reciprocal(rs[:, :], sd[:, :]))
                    s.wait(dve, "tr_done", it * KC)
                    for t in range(TPB):
                        last = dve.tensor_scalar(xn[:, t, :], x[:, t, :], mv[:, t, 0:1], rs[:, t:t + 1], ALU.subtract, ALU.mult)
                    last.then_inc(s["xn_ready"], 1)
                    s.wait(dve, "xn_ready", it + 1)
                    dve.sem_inc(s["x_used"], 1)
                    s.wait(dve, "qk_done", it * QKT)
                    for c in range(KC):
                        r = rows(c)
                        s.wait(dve, "xm_ready", it * KC + c + 1)
                        last = dve.tensor_copy(xh[0:r, c, :], xm[0:r, c, :])
                    ch.do(last)
                    for c in range(KC):
                        r = rows(c)
                        dve.tensor_tensor(xl[0:r, c, :], xm[0:r, c, :], xh[0:r, c, :].bitcast(F32), ALU.subtract).then_inc(s["xs_ready"], 1)
                    for t in range(TPB):
                        for h in range(2):
                            s.wait(dve, "v_done", it * 2 * TPB + 2 * t + h + 1)
                            dve.tensor_tensor(
                                V[:, bass.ds(b * H + h * (H // 2), H // 2), bass.ds(j * TPB + t, 1), :].rearrange("p h a d -> p h (a d)"),
                                vp[h][:, 0:HALF].rearrange("p (h d) -> p h d", d=HD),
                                bvb[:, h, :].rearrange("p (h d) -> p h d", d=HD), ALU.add).then_inc(s["v_ready"], 1)
                    for m in range(QKT):
                        if m:
                            e = Chain(dve, s["elim_chain"], it * ELIM + m - 1)
                            s.wait(dve, "elim_ready", it * ELIM + m - 1)
                            e.do(dve.reciprocal(piv[:, :], M[0:1, 0:1]))
                            dve.tensor_scalar(step[0:1, 0:RD - 1], M[0:1, 1:RD], piv[:, :], -1.0, ALU.mult, ALU.mult
                                              ).then_inc(s["row_ready"], 1)
                        s.wait(dve, "hi_ready", it * QKT + m + 1)
                        k, extra = m // RING, int(m % RING == (QKT // 2) % RING)
                        stores = it * (QKT // RING + extra) + k + int(extra and m > QKT // 2)
                        outs.wait(dve, f"out_lo{m % RING}", stores * 16)
                        dve.scalar_tensor_tensor(out=ol[:, m % RING, :], in0=qk[m % RING][:, :], scalar=bqk[:, m:m + 1],
                                                 in1=oh[:, m % RING, :].bitcast(F32), op0=ALU.add, op1=ALU.subtract
                                                 ).then_inc(s["lo_ready"], 1)
                        if m:
                            s.wait(dve, "elim_mm", it * ELIM + m)
                            dve.tensor_copy(M[:, 0:2 * ML].rearrange("p (a b) -> p a b", a=2)[:, :, 0:RD],
                                            el[0:RD, 1:1 + 2 * RD].rearrange("p (a b) -> p a b", a=2)).then_inc(s["elim_ready"], 1)


QB = 1024
NQB = T // QB
SLOTS = NQB * KT
STK = 3 * HD
VW = 64
MAXW = 512
NMAX = KT * (T // MAXW)
MAX_FROM, MAX_PER = 5, 3
PREV_SLOT = 3
LU_SLOTS = (4, 29)
SCALE = float(HD) ** -0.5


def agenda(prev, nxt):
    plan, k = [[] for _ in range(SLOTS)], 0
    for s in range(MAX_FROM, SLOTS):
        if nxt and k < NMAX:
            plan[s] = [("max", x) for x in range(k, min(NMAX, k + MAX_PER))]
            k += MAX_PER
            row = s + 2
    if nxt:
        plan[row].append(("row", None))
    if prev:
        plan[PREV_SLOT].append(("out", 1))
    plan[O_SLOT].append(("out", 0))
    for l, s in enumerate(LU_SLOTS):
        plan[s].append(("lu", l))
    return plan


O_SLOT = KT + 3
USES = sum(len(p) for p in agenda(True, True))
SHARED = 3
assert USES % SHARED == 0


def attention(nc, io, g):
    V = g["V"]
    with ExitStack() as ctx:
        sb = lambda name, shape, dt=F32: ctx.enter_context(nc.sbuf_tensor(name, shape, dt))
        sem = lambda name: ctx.enter_context(nc.semaphore("b_" + name))
        psum = lambda name, shape: ctx.enter_context(nc.psum_tensor(name, shape, F32))
        ident = g["ident"]
        q = [sb(f"q_stack{u}", [P, T], F32R) for u in range(2)]
        k = [sb(f"k_stack{u}", [P, T], F32R) for u in range(2)]
        vst = [sb(f"v_stat{u}", [P, KT, VW]) for u in range(2)]
        pr = [sb(f"probs{i}", [P, QB]) for i in range(4)]
        mxp = sb("max_parts", [P, KT, T // MAXW])
        mx = sb("max_q", [P, KT])
        nm = sb("neg_max", [P, 2, KT])
        nmr = sb("neg_max_r", [P, 2, KT], F32R)
        nmT = sb("neg_maxT", [2 * KT, P], F32R)
        oT = [sb(f"outT{i}", [P, 512]) for i in range(NQB)]
        rc = sb("recip_sum", [P, 2, KT // NQB // 2])
        ob = [sb(f"out_tok{u}", [P, KT, HD]) for u in range(2)]
        sc = [psum(f"scoresT{i}", [P, QB]) for i in range(2)]
        shared = [psum(f"shared{i}", [P, 512]) for i in range(SHARED)]
        av = psum("av", [P, 512])
        stack_in = [sem(f"stack_in{u}") for u in range(2)]
        row_in = [sem(f"row_in{u}") for u in range(2)]
        ones_ready, sc_done, exp_done, av_done, half_done = (sem(x) for x in ("ones_ready", "sc_done", "exp_done", "av_done", "half_done"))
        use_done, use_free, nm_ready, nmT_ready, oT_ready, v_ready, v_init, ob_ready, rc_done, chain = (
            sem(x) for x in ("use_done", "use_free", "nm_ready", "nmT_ready", "oT_ready", "v_ready", "v_init", "ob_ready", "rc_done", "chain"))
        out_st = [sem(f"out_st{u}") for u in range(2)]
        G, M, E, step, stepT, X2, one, signs, half_mask, UT, URI = (
            g[x] for x in "G M E step stepT X2 one signs half_mask UT URI".split())
        LiT, prod, S, ST, KTm = (sb(x, [RD, RD]) for x in ("LiT", "prod", "Sinv", "SinvT", "correction"))
        dcol = sb("dcol", [RD, 4])
        U1T, U1 = sb("U1T", [RD, D]), sb("U1", [P, KC, RD])
        pivot = sb("lu_pivot", [1, 3])
        pA, pB, pC = sc[0], av, shared[SHARED - 1]
        basis_mm, basis_ready, basis_chain, d_ready, sqrt_ready, lrow_ready, lu_chain = (
            sem(x) for x in ("basis_mm", "basis_ready", "basis_chain", "d_ready", "sqrt_ready", "lrow_ready", "lu_chain"))
        lu_copied = sem("lu_copied")
        BASE = NMAX
        EXP_CREDIT, AV_CREDIT, USE_CREDIT, OT_CREDIT, OUT_CREDIT = 2, 4, SHARED, 1, 16
        block = ctx.enter_context(nc.Block())

        def bank(j):
            return shared[(BASE + j) % SHARED]

        @block.sync
        def _(sp):
            def load_stacks(n, u):
                r = bass.ds(n * HD, HD)
                for dst, parts in ((q[u], ("q_hi", "q_hi", "q_lo")), (k[u], ("k_hi", "k_lo", "k_hi"))):
                    for i, part in enumerate(parts):
                        sp.dma_start(dst[i * HD:(i + 1) * HD, :].bitcast(F32), g[part][r, :]).then_inc(stack_in[u], 16)

            def max_row(n, u):
                sp.wait_ge(nmT_ready, n + 1)
                for part in range(2):
                    sp.dma_start(q[u][STK + part:STK + part + 1, :].bitcast(F32),
                                 nmT[part * KT:(part + 1) * KT, :].bitcast(F32)).then_inc(row_in[u], 16)

            for u in range(2):
                sp.sem_inc(out_st[u], OUT_CREDIT)
            sp.wait_ge(ones_ready, 2)
            load_stacks(0, 0)
            max_row(0, 0)

            def load_next(n, u):
                if not isinstance(n, int):
                    sp.wait_ge(sc_done, n * SLOTS)
                load_stacks(n + 1, 1 - u)

            def store(n, u):
                sp.wait_ge(ob_ready, (n + 1) * NQB)
                dst = g["attn_scratch"][bass.ds((n // H) * T, T), bass.ds((n % H) * HD, HD)].rearrange("(t p) d -> p t d", p=P)
                sp.dma_start(dst, ob[u][:, :, :]).then_inc(out_st[u], 16)

            load_next(0, 0)
            max_row(1, 1)
            with sp.Fori(0, NH // 2 - 1) as i:
                for n, u in ((2 * i + 1, 1), (2 * i + 2, 0)):
                    load_next(n, u)
                    store(n - 1, 1 - u)
                    max_row(n + 1, 1 - u)
            store(NH - 2, 0)
            store(NH - 1, 1)
            for u in range(2):
                sp.wait_ge(out_st[u], 16 * NH // 2 + OUT_CREDIT)

        @block.gpsimd
        def _(pool):
            for u in range(2):
                pool.memset(vst[u][:, :, :], 0.0).then_inc(v_init, 1)
                pool.wait_ge(v_init, 2 * u + 1)
                pool.memset(vst[u][:, :, HD:HD + 1], 1.0).then_inc(v_init, 1)
            pool.wait_ge(v_init, 4)
            pool.tensor_copy(vst[0][:, :, 0:HD], V[:, 0, :, :]).then_inc(v_ready, 1)

            with pool.Fori(0, B) as b:
                with pool.Fori(0, H // 2) as hp:
                    for u in range(2):
                        h = hp * 2 + u
                        n = b * H + h
                        pool.wait_ge(av_done, n * SLOTS + AV_CREDIT)
                        nxt = n + 1 if u == 0 else (n + 1) % NH
                        pool.tensor_copy(vst[1 - u][:, :, 0:HD], V[:, bass.ds(nxt, 1), :, :].rearrange("p a t d -> p (a t) d")
                                         ).then_inc(v_ready, 1)

        @block.scalar
        def _(act):
            act.sem_inc(exp_done, EXP_CREDIT)
            act.sem_inc(oT_ready, OT_CREDIT)
            act.wait_ge(d_ready, 1)
            act.activation(dcol[:, 1:2], dcol[:, 0:1], ACT.Sqrt).then_inc(sqrt_ready, 1)

            def evacuate(n, qb):
                act.wait_ge(av_done, n * SLOTS + (qb + 1) * KT + AV_CREDIT)
                act.activation(oT[qb][:, :], av[:, :], ACT.Copy).then_inc(oT_ready, 1)

            def head(n, prev):
                for s in range(SLOTS):
                    if s == 1 and prev:
                        evacuate(n - 1, 1)
                    if s == KT + 1:
                        evacuate(n, 0)
                    act.wait_ge(sc_done, n * SLOTS + s + 1)
                    act.wait_ge(av_done, n * SLOTS + s + 1)
                    act.activation(pr[s % 4][:, :], sc[s % 2][:, :], ACT.Exp, scale=SCALE).then_inc(exp_done, 1)

            head(0, False)
            group = 3
            with act.Fori(0, (NH - 2) // group) as i:
                for x in range(group):
                    head(group * i + x + 1, True)
            head(NH - 1, True)
            evacuate(NH - 1, 1)

        @block.tensor
        def _(pe):
            pe.sem_inc(av_done, AV_CREDIT)
            pe.transpose(pC[0:RD, 0:RD], M[:, ML:ML + RD], ident[0:RD, 0:RD]).then_inc(basis_mm, 1)
            pe.wait_ge(basis_ready, 1)
            pe.matmul(pB[0:RD, 0:RD], LiT[:, :], G[:, :], start=True, stop=True).then_inc(basis_mm, 1)
            pe.wait_ge(basis_ready, 2)
            pe.transpose(pC[0:RD, 0:RD], S[:, :], ident[0:RD, 0:RD]).then_inc(basis_mm, 1)
            pe.wait_ge(basis_ready, 3)
            for h in range(2):
                last = pe.matmul(pA[0:RD, h * 512:h * 512 + HALF], ST[:, :], UT[:, h * HALF:(h + 1) * HALF], start=True, stop=True)
            last.then_inc(basis_mm, 1)
            pe.wait_ge(basis_ready, 4)
            for c in range(KC):
                last = pe.transpose(pB[0:rows(c), c * RD:(c + 1) * RD], U1T[:, c * P:c * P + rows(c)], ident[0:RD, 0:RD])
            last.then_inc(basis_mm, 1)
            pe.wait_ge(basis_ready, 5)
            for c in range(KC):
                last = pe.matmul(pC[0:RD, 0:RD], U1[0:rows(c), c, :], U1[0:rows(c), c, :], start=(c == 0), stop=(c == KC - 1))
            last.then_inc(basis_mm, 1)
            pe.wait_ge(basis_ready, 6)
            for h in range(2):
                last = pe.matmul(pA[0:RD, h * 512:h * 512 + HALF], KTm[:, :], U1T[:, h * HALF:(h + 1) * HALF], start=True, stop=True)
            last.then_inc(basis_mm, 1)
            pe.wait_ge(basis_ready, 7)
            pe.transpose(pB[0:RD, 0:RD], UT[:, 0:RD], ident[0:RD, 0:RD]).then_inc(basis_mm, 1)

            def scores(n, u, s):
                pe.wait_ge(exp_done, n * SLOTS + s - 1 + EXP_CREDIT)
                qb, m = s // KT, s % KT
                for x in range(2):
                    last = pe.matmul(sc[s % 2][:, x * 512:(x + 1) * 512], k[u][0:STK + 2, m * P:(m + 1) * P],
                                     q[u][0:STK + 2, qb * QB + x * 512:qb * QB + (x + 1) * 512], start=True, stop=True)
                last.then_inc(sc_done, 1)

            def one_max(u, kk, use, bk):
                pe.wait_ge(use_free, use + 1)
                qt, kc = kk // (T // MAXW), kk % (T // MAXW)
                pe.matmul(bk[:, :], q[u][0:STK, qt * P:(qt + 1) * P],
                          k[u][0:STK, kc * MAXW:(kc + 1) * MAXW], start=True, stop=True).then_inc(use_done, 1)

            def max_row(n, use, bk):
                pe.wait_ge(nm_ready, n + 1)
                pe.wait_ge(use_free, use + 1)
                pe.transpose(bk[0:2 * KT, 0:P], nm[:, :, :].rearrange("p a t -> p (a t)"), ident[:, :]).then_inc(use_done, 1)

            def out_half(n, qb, use, bk):
                pe.wait_ge(oT_ready, n * NQB + qb + 1 + OT_CREDIT)
                pe.wait_ge(use_free, use + 1)
                for t in range(4):
                    last = pe.transpose(bk[:, t * P:(t + 1) * P], oT[qb][:, t * P:(t + 1) * P], ident[:, :])
                last.then_inc(use_done, 1)

            def lu_step(i, use, bk):
                pe.wait_ge(lrow_ready, i + 1)
                pe.wait_ge(use_free, use + 1)
                pe.matmul(bk[:, 0:ML], step[:, :], X2[:, 0, :], start=True, stop=True)
                pe.matmul(bk[:, 256:256 + ML], stepT[:, :], X2[:, 1, :], start=True, stop=True).then_inc(use_done, 1)

            pe.wait_ge(stack_in[0], 96)
            for kk in range(NMAX):
                one_max(0, kk, kk, shared[kk % SHARED])
            max_row(0, NMAX, shared[NMAX % SHARED])
            pe.wait_ge(row_in[0], 32)
            pe.wait_ge(lrow_ready, 1)
            scores(0, 0, 0)

            def head(n, u, nth, prev, nxt):
                plan = agenda(prev, nxt)
                base = BASE + n * USES
                j = 0 if prev else 1
                pe.wait_ge(v_ready, n + 1)
                for s in range(SLOTS):
                    def use(kind, x):
                        nonlocal j
                        at, bk = base + j, bank(j)
                        j += 1
                        if kind == "max":
                            if x == 0:
                                pe.wait_ge(stack_in[1 - u], 96 * (nth + 1))
                            one_max(1 - u, x, at, bk)
                        elif kind == "row":
                            max_row(n + 1, at, bk)
                        elif kind == "out":
                            out_half(n - x, x, at, bk)
                        else:
                            lu_step(n * len(LU_SLOTS) + x, at, bk)

                    for item in plan[s][0:1]:
                        use(*item)
                    if s + 1 < SLOTS:
                        scores(n, u, s + 1)
                    elif nxt:
                        pe.wait_ge(row_in[1 - u], 32 * (nth + 1))
                        scores(n + 1, 1 - u, 0)
                    for item in plan[s][1:2]:
                        use(*item)
                    qb, m = s // KT, s % KT
                    if m == 0:
                        pe.wait_ge(oT_ready, n * NQB + qb + OT_CREDIT)
                    pe.wait_ge(exp_done, n * SLOTS + s + 1 + EXP_CREDIT)
                    for x in range(2):
                        last = pe.matmul(av[x * VW:(x + 1) * VW, :], vst[u][:, m, :], pr[s % 4][:, x * 512:(x + 1) * 512],
                                         start=(m == 0), stop=(m == KT - 1))
                    last.then_inc(av_done, 1)
                    for item in plan[s][2:]:
                        use(*item)
                return base + j, bank(j)

            head(0, 0, 0, False, True)
            with pe.Fori(0, NH // 2 - 1) as i:
                head(2 * i + 1, 1, i + 1, True, True)
                head(2 * i + 2, 0, i + 1, True, True)
            at, bk = head(NH - 1, 1, None, True, False)
            out_half(NH - 1, 1, at, bk)
            pe.wait_ge(lrow_ready, RD + 1)
            pe.wait_ge(basis_ready, 8)
            pe.matmul(sc[0][0:RD, 0:1], signs[0:1, 0:RD], one[0:1, 0:1], start=True, stop=True).then_inc(basis_mm, 1)
            pe.wait_ge(basis_ready, 9)
            for b in range(B):
                for c in range(KC):
                    last = pe.matmul(sc[1][0:rows(c), b * 512 + c * RD:b * 512 + (c + 1) * RD], UT[:, c * P:c * P + rows(c)],
                                     E[:, 0, b, :], start=True, stop=True)
            last.then_inc(basis_mm, 1)

        @block.vector
        def _(dve):
            for u in range(2):
                dve.memset(k[u][96:STK + 2, :].bitcast(F32), 1.0).then_inc(ones_ready, 1)
            dve.sem_inc(use_free, USE_CREDIT)
            ch = Chain(dve, basis_chain)
            right = M[:, ML:ML + RD]
            dve.wait_ge(basis_mm, 1)
            dve.tensor_copy(LiT[:, :], pC[0:RD, 0:RD]).then_inc(basis_ready, 1)
            dve.wait_ge(basis_mm, 2)
            ch.do(dve.tensor_tensor(prod[:, :], pB[0:RD, 0:RD], right, ALU.mult))
            dve.tensor_reduce(dcol[:, 0:1], prod[:, :], op=ALU.add, axis=AX.X).then_inc(d_ready, 1)
            dve.wait_ge(sqrt_ready, 1)
            ch.do(dve.reciprocal(dcol[:, 2:3], dcol[:, 1:2]))
            dve.tensor_scalar(S[:, :], right, dcol[:, 2:3], None, ALU.mult).then_inc(basis_ready, 1)
            dve.wait_ge(basis_mm, 3)
            dve.tensor_copy(ST[:, :], pC[0:RD, 0:RD]).then_inc(basis_ready, 1)
            halves = pA[0:RD, :].rearrange("p (a b) -> p a b", a=2)[:, :, 0:HALF]
            dve.wait_ge(basis_mm, 4)
            dve.tensor_copy(U1T[:, :].rearrange("p (a b) -> p a b", a=2), halves).then_inc(basis_ready, 1)
            dve.wait_ge(basis_mm, 5)
            ch.do(dve.tensor_copy(U1[:, 0:KC - 1, :].rearrange("p a b -> p (a b)"), pB[:, 0:(KC - 1) * RD]))
            dve.tensor_copy(U1[0:rows(KC - 1), KC - 1, :], pB[0:rows(KC - 1), (KC - 1) * RD:KC * RD]).then_inc(basis_ready, 1)
            dve.wait_ge(basis_mm, 6)
            ch.do(dve.tensor_tensor(prod[:, :], pC[0:RD, 0:RD], ident[0:RD, 0:RD], ALU.subtract))
            ch.do(dve.tensor_tensor(KTm[:, :], prod[:, :], half_mask[:, :], ALU.mult))
            dve.tensor_tensor(KTm[:, :], ident[0:RD, 0:RD], KTm[:, :], ALU.subtract).then_inc(basis_ready, 1)
            dve.wait_ge(basis_mm, 7)
            dve.tensor_copy(UT[:, :].rearrange("p (a b) -> p a b", a=2), halves).then_inc(basis_ready, 1)
            dve.wait_ge(basis_mm, 8)
            ch.do(dve.tensor_copy(X2[:, 0, 0:RD], pB[0:RD, 0:RD]))
            ch.do(dve.memset(step[0:1, RD - 1:RD], 0.0))
            dve.wait_ge(basis_ready, 7)
            ch.do(dve.tensor_copy(X2[:, 1, 0:RD], UT[:, 0:RD]))

            def lu_rows(i):
                c = Chain(dve, lu_chain, i * 5)
                c.do(dve.tensor_scalar(pivot[:, 0:1], X2[0:1, 0, 0:1], 0.0, 2.0, ALU.is_ge, ALU.mult))
                c.do(dve.tensor_scalar(signs[0:1, bass.ds(i, 1)], pivot[:, 0:1], -1.0, None, ALU.add))
                c.do(dve.scalar_tensor_tensor(out=pivot[:, 1:2], in0=pivot[:, 0:1], scalar=-1.0, in1=X2[0:1, 0, 0:1],
                                              op0=ALU.add, op1=ALU.add))
                c.do(dve.reciprocal(pivot[:, 2:3], pivot[:, 1:2]))
                c.do(dve.tensor_scalar(stepT[0:1, 0:RD - 1], X2[0:1, 0, 1:RD], pivot[:, 2:3], -1.0, ALU.mult, ALU.mult))
                dve.tensor_scalar(step[0:1, 0:RD - 1], X2[0:1, 1, 1:RD], pivot[:, 2:3], -1.0, ALU.mult, ALU.mult).then_inc(lrow_ready, 1)

            def lu_step(i, use, bk):
                dve.wait_ge(use_done, use + 1)
                dve.tensor_copy(X2[:, :, 0:RD], bk[0:RD, :].rearrange("p (a b) -> p a b", a=2)[:, :, 1:ML]).then_inc(lu_copied, 1)
                dve.wait_ge(lu_copied, i + 1)
                dve.sem_inc(use_free, 1)
                lu_rows(i + 1)

            lu_rows(0)

            def one_max(kk, use, bk):
                dve.wait_ge(use_done, use + 1)
                qt, kc = kk // (T // MAXW), kk % (T // MAXW)
                dve.tensor_reduce(mxp[:, qt, kc:kc + 1], bk[:, :], op=ALU.max, axis=AX.X).then_inc(use_free, 1)

            def neg_max(n, uses):
                dve.wait_ge(use_free, uses + USE_CREDIT)
                c = Chain(dve, chain, 3 * n)
                c.do(dve.tensor_reduce(mx[:, :], mxp[:, :, :], op=ALU.max, axis=AX.X))
                c.do(dve.tensor_scalar(nmr[:, 0, :], mx[:, :], -1.0, None, ALU.mult))
                c.do(dve.scalar_tensor_tensor(out=nmr[:, 1, :], in0=mx[:, :], scalar=-1.0, in1=nmr[:, 0, :].bitcast(F32),
                                              op0=ALU.mult, op1=ALU.subtract))
                dve.tensor_copy(nm[:, :, :], nmr[:, :, :].bitcast(F32)).then_inc(nm_ready, 1)

            def row_copy(n, use, bk):
                dve.wait_ge(use_done, use + 1)
                dve.tensor_copy(nmT[:, :], bk[0:2 * KT, 0:P]).then_inc(nmT_ready, 1)
                dve.wait_ge(nmT_ready, n + 1)
                dve.sem_inc(use_free, 1)

            for kk in range(NMAX):
                one_max(kk, kk, shared[kk % SHARED])
            neg_max(0, NMAX)
            row_copy(0, NMAX, shared[NMAX % SHARED])

            def normalise(n, u, nth, qb, use, bk):
                dve.wait_ge(use_done, use + 1)
                ps = bk[:, :].rearrange("p (t x c) -> p x t c", x=2, c=VW)
                dve.reciprocal(rc[:, :, :], ps[:, :, :, HD]).then_inc(rc_done, 1)
                dve.wait_ge(rc_done, n * NQB + qb + 1)
                if qb == 0:
                    dve.wait_ge(out_st[u], 16 * nth + OUT_CREDIT)
                o = ob[u][:, qb * 8:(qb + 1) * 8, :].rearrange("p (x t) d -> p x t d", x=2)
                for x in range(2):
                    last = dve.tensor_tensor(o[:, x], ps[:, x, :, 0:HD],
                                             rc[:, x, :].rearrange("p (t a) -> p t a", a=1).broadcast_to([P, 4, HD]), ALU.mult)
                last.then_inc(ob_ready, 1)
                dve.wait_ge(ob_ready, n * NQB + qb + 1)
                dve.sem_inc(use_free, 1)

            def head(n, u, nth, row_nth, prev, nxt):
                base = BASE + n * USES
                j = 0 if prev else 1
                for items in agenda(prev, nxt):
                    for kind, x in items:
                        at, bk = base + j, bank(j)
                        j += 1
                        if kind == "max":
                            one_max(x, at, bk)
                            if x == NMAX - 1:
                                neg_max(n + 1, base + j)
                        elif kind == "row":
                            dve.wait_ge(row_in[u], 32 * row_nth)
                            row_copy(n + 1, at, bk)
                        elif kind == "out":
                            normalise(n - x, u ^ x, None if x else nth, x, at, bk)
                        else:
                            lu_step(n * len(LU_SLOTS) + x, at, bk)
                return base + j, bank(j)

            head(0, 0, 0, 1, False, True)
            with dve.Fori(0, NH // 2 - 1) as i:
                head(2 * i + 1, 1, i, i + 1, True, True)
                head(2 * i + 2, 0, i + 1, i + 2, True, True)
            at, bk = head(NH - 1, 1, NH // 2 - 1, None, True, False)
            normalise(NH - 1, 1, None, 1, at, bk)
            dve.wait_ge(lu_chain, 5 * (RD + 1))
            dve.sem_inc(basis_ready, 1)
            dve.wait_ge(basis_mm, 9)
            ch.do(dve.tensor_copy(dcol[:, 3:4], sc[0][0:RD, 0:1]))
            dve.tensor_scalar(UT[:, :], UT[:, :], dcol[:, 3:4], -1.0, ALU.mult, ALU.mult).then_inc(basis_ready, 1)
            dve.wait_ge(basis_mm, 10)
            for b in range(B):
                full, r = (KC - 1) * RD, rows(KC - 1)
                dve.memset(URI[r:P, b, KC - 1, :], 0.0)
                dve.tensor_copy(URI[:, b, 0:KC - 1, :].rearrange("p a b -> p (a b)"), sc[1][:, b * 512:b * 512 + full])
                dve.tensor_copy(URI[0:r, b, KC - 1, :], sc[1][0:r, b * 512 + full:b * 512 + full + RD])


def mlp(nc, io, g, out):
    HR, WR = 3, 3
    with ExitStack() as ctx:
        sb = lambda name, shape, dt=F32: ctx.enter_context(nc.sbuf_tensor(name, shape, dt))
        sem = lambda name: ctx.enter_context(nc.semaphore("c_" + name))
        psum = lambda name, shape: ctx.enter_context(nc.psum_tensor(name, shape, F32))
        ident, modv, UT, URI = g["ident"], g["modv"], g["UT"], g["URI"]
        w1h = sb("w1_hi", [P, KC, HID], F32R)
        w1l = sb("w1_lo", [P, KC, HID], F32R)
        wph = sb("wp_hi", [P, KC, D], F32R)
        wpl = sb("wp_lo", [P, KC, D], F32R)
        w2 = sb("w2_ring", [P, WR, 2, D], F32R)
        xr = sb("x_resid", [P, TPB, D])
        oi = sb("attn_tok", [P, TPB, D])
        xo = sb("x_norm_out", [P, TPB, D])
        fT = sb("featT", [P, KC, BLK])
        fh = sb("featT_hi", [P, KC, BLK], F32R)
        fl = sb("featT_lo", [P, KC, BLK], F32R)
        hb = sb("hid", [P, 2, BLK])
        hh = sb("hid_hi", [P, 2, BLK], F32R)
        hl = sb("hid_lo", [P, 2, BLK], F32R)
        wT = sb("rotT", [RD, BLK])
        uri = sb("URI_cur", [P, KC, RD])
        bp, b2, b1 = sb("b_proj", [P, KC]), sb("b_fc2", [P, KC]), sb("b_fc1", [P, FT])
        gb = sb("gated_bias", [P, B, 2, KC])
        eps = sb("eps_c", [P, 1])
        st, mv = sb("st_c", [P, TPB, 2, 6]), sb("mv_c", [P, TPB, 2])
        sd, rs = sb("sd_c", [P, TPB]), sb("rs_c", [P, TPB])
        acc = psum("acc", [P, KC, 512])
        hp = [psum(f"hid_ps{i}", [P, BLK]) for i in range(HR)]
        names = ("w1_hi w1_lo wp_in wp_in2 wp_hi wp_lo bias_in bias_ready o_in x_in o_tr o_hi o_lo p_done p_ready b_done x2_ready "
                 "st_ready var_ready std_ready xn_ready tr_done xm_ready xs_ready h_done g_ready hh_ready hs_ready y_done y_ready b2_done x3_ready "
                 "t3_done x3T_ready uri_ready w_done wT_ready r_done xo_ready chain stage_free")
        s = Counts(sem, names.split(), ("y_done", "xo_ready", "g_ready", "hs_ready", "o_tr", "w_done"))
        st_out = Counts(sem, ["out_st"], ["out_st"], credit=16)
        w1_in = [sem(f"w1_in{i}") for i in range(2)]
        w2_in = [sem(f"w2_in{i}") for i in range(WR)]
        stages = (xr, oi)
        xv = io["x"].rearrange("b (k t p) d -> (b k) p t d", p=P, t=TPB)
        ov = out.rearrange("b (k t p) d -> (b k) p t d", p=P, t=TPB)
        av = g["attn_scratch"].rearrange("(k t p) d -> k p t d", p=P, t=TPB)
        block = ctx.enter_context(nc.Block())

        def flat(ap):
            return ap.rearrange("p t d -> p (t d)")

        @block.sync
        def _(sp):
            load_columns(sp, bp[:, :], io["L0_cond_b_proj"], s["bias_in"])
            load_columns(sp, b2[:, :], io["L0_cond_b_fc2"], s["bias_in"])
            sp.dma_start(b1[:, :], io["L0_cond_b_fc1"].rearrange("(f p) -> p f", p=P)).then_inc(s["bias_in"], 16)
            for c in range(KC):
                r = rows(c)
                if c >= 2:
                    s.wait(sp, "stage_free", c - 1)
                sp.dma_start(flat(stages[c % 2][0:r, :, :]), io["L0_cond_w_fc1"][c * P:c * P + r, :]).then_inc(w1_in[c % 2], 16)
                if c == 1:
                    for k in range(4):
                        sp.dma_start(xo[:, k, :], io["L0_cond_w_proj"][k * P:(k + 1) * P, :]).then_inc(s["wp_in"], 16)
            s.wait(sp, "wp_lo", 1)
            sp.dma_start(xo[0:rows(4), 0, :], io["L0_cond_w_proj"][4 * P:D, :]).then_inc(s["wp_in2"], 16)
            s.wait(sp, "stage_free", KC)
            with sp.Fori(0, NBLK) as it:
                s.wait(sp, "o_tr", it * KC)
                sp.dma_start(oi[:, :, :], av[bass.ds(it, 1)].rearrange("a p t d -> p (a t) d")).then_inc(s["o_in"], 16)
                for f in range(FT):
                    s.wait(sp, "y_done", it * FT + max(0, f - WR + 1))
                    sp.dma_start(w2[:, f % WR, :, :].bitcast(F32), g["w2_split"][:, f, :, :]).then_inc(w2_in[f % WR], 16)

        @block.gpsimd
        def _(pool):
            with pool.Fori(0, NBLK) as it:
                s.wait(pool, "w_done", it)
                pool.tensor_copy(uri[:, :, :], URI[:, bass.ds(it // BPB, 1), :, :].rearrange("p a c d -> p (a c) d")).then_inc(s["uri_ready"], 1)

        @block.scalar
        def _(act):
            s.give(act, "g_ready")
            st_out.give(act, "out_st")
            for c in range(KC):
                r = rows(c)
                act.wait_ge(w1_in[c % 2], 16 * (c // 2 + 1))
                act.activation(w1h[0:r, c, :], flat(stages[c % 2][0:r, :, :]), ACT.Copy).then_inc(s["w1_hi"], 1)
            for c in range(KC):
                r = rows(c)
                s.wait(act, "wp_in", 64) if c < 4 else s.wait(act, "wp_in2", 16)
                act.activation(wph[0:r, c, :], xo[0:r, c % 4, :], ACT.Copy).then_inc(s["wp_hi"], 1)
            s.wait(act, "bias_ready", 1)
            s.wait(act, "stage_free", KC)
            with act.Fori(0, NBLK) as it:
                b = bass.ds(it // BPB, 1)

                s.wait(act, "xo_ready", it * TPB)
                act.dma_start(xr[:, :, :], xv[bass.ds(it, 1)].rearrange("a p t d -> p (a t) d")).then_inc(s["x_in"], 16)

                def column(sec, r, c):
                    return modv[0:r, b, sec, c:c + 1].rearrange("p a b -> p (a b)")

                def gated(k, r, c):
                    return gb[0:r, b, k, c:c + 1].rearrange("p a b -> p (a b)")

                for c in range(KC):
                    r = rows(c)
                    s.wait(act, "o_tr", it * KC + c + 1)
                    act.activation(fh[0:r, c, :], acc[0:r, c, :], ACT.Copy).then_inc(s["o_hi"], 1)
                for m in range(KC):
                    r = rows(m)
                    s.wait(act, "p_done", it * KC + m + 1)
                    act.activation(fT[0:r, m, :], hp[m % HR][0:r, :], ACT.Identity, bias=gated(0, r, m),
                                   scale=column(GATE_A, r, m)).then_inc(s["p_ready"], 1)
                s.wait(act, "var_ready", it + 1)
                act.activation(sd[:, :], mv[:, :, 1], ACT.Sqrt, bias=eps[:, :]).then_inc(s["std_ready"], 1)
                for c in range(KC):
                    r = rows(c)
                    s.wait(act, "tr_done", it * KC + c + 1)
                    act.activation(fT[0:r, c, :], acc[0:r, c, :], ACT.Identity, bias=column(SHIFT_F, r, c),
                                   scale=column(SCALE_F, r, c)).then_inc(s["xm_ready"], 1)
                for f in range(FT):
                    s.wait(act, "h_done", it * FT + f + 1)
                    s.wait(act, "hs_ready", it * FT + max(0, f - 1))
                    act.activation(hb[:, f % 2, :], hp[f % HR][:, :], ACT.Gelu_apprx_tanh, bias=b1[:, f:f + 1]).then_inc(s["g_ready"], 1)
                s.wait(act, "y_done", it * FT + FT)
                for m in range(KC):
                    r = rows(m)
                    act.activation(fT[0:r, m, :], acc[0:r, m, :], ACT.Identity, bias=gated(1, r, m),
                                   scale=column(GATE_F, r, m)).then_inc(s["y_ready"], 1)
                for c in range(KC):
                    r = rows(c)
                    s.wait(act, "t3_done", it * KC + c + 1)
                    act.activation(fT[0:r, c, :], acc[0:r, c, :], ACT.Copy).then_inc(s["x3T_ready"], 1)
                s.wait(act, "w_done", it + 1)
                act.activation(wT[:, :], hp[0][0:RD, :], ACT.Copy).then_inc(s["wT_ready"], 1)
                s.wait(act, "xo_ready", it * TPB + TPB)
                act.dma_start(ov[bass.ds(it, 1)].rearrange("a p t d -> p (a t) d"), xo[:, :, :]).then_inc(st_out["out_st"], 16)
            st_out.wait(act, "out_st", 16 * NBLK)

        @block.tensor
        def _(pe):
            s.give(pe, "y_done", "o_tr", "w_done")
            s.wait(pe, "wp_lo", KC)
            s.wait(pe, "w1_lo", KC)

            def to_features(src, c, done):
                for t in range(TPB):
                    last = pe.transpose(acc[0:rows(c), c, t * P:(t + 1) * P], src[:, t, c * P:c * P + rows(c)], ident[:, :])
                last.then_inc(done, 1)

            def to_tokens(t, done):
                for c in range(KC):
                    r = rows(c)
                    bk, col = divmod((t % 2) * 1024 + c * P, 512)
                    last = pe.transpose(acc[:, bk, col:col + r], fT[0:r, c, t * P:(t + 1) * P], ident[0:r, 0:r])
                last.then_inc(done, 1)

            with pe.Fori(0, NBLK) as it:
                s.wait(pe, "o_in", it * 16 + 16)
                s.wait(pe, "xo_ready", it * TPB)
                for c in range(KC):
                    to_features(oi, c, s["o_tr"])
                s.wait(pe, "o_lo", it * KC + KC)
                for m in range(KC):
                    r = rows(m)
                    if m >= HR:
                        s.wait(pe, "p_ready", it * KC + m - HR + 1)
                    for c in range(KC):
                        k = rows(c)
                        for n, (w, xx) in enumerate(((wph, fh), (wph, fl), (wpl, fh))):
                            last = pe.matmul(hp[m % HR][0:r, :], w[0:k, c, m * P:m * P + r], xx[0:k, c, :],
                                             start=(c == 0 and n == 0), stop=(c == KC - 1 and n == 2))
                    last.then_inc(s["p_done"], 1)
                s.wait(pe, "p_ready", it * KC + KC)
                for t in range(TPB):
                    if t >= 2:
                        s.wait(pe, "x2_ready", it * TPB + t - 1)
                    to_tokens(t, s["b_done"])
                s.wait(pe, "xn_ready", it + 1)
                for c in range(KC):
                    to_features(xo, c, s["tr_done"])
                s.wait(pe, "xs_ready", it * KC + KC)

                def hidden(f):
                    s.wait(pe, "g_ready", it * FT + max(0, f - HR + 1))
                    for c in range(KC):
                        k = rows(c)
                        for n, (w, xx) in enumerate(((w1h, fh), (w1h, fl), (w1l, fh))):
                            last = pe.matmul(hp[f % HR][:, :], w[0:k, c, f * P:(f + 1) * P], xx[0:k, c, :],
                                             start=(c == 0 and n == 0), stop=(c == KC - 1 and n == 2))
                    last.then_inc(s["h_done"], 1)

                hidden(0)
                for f in range(FT):
                    if f + 1 < FT:
                        hidden(f + 1)
                    s.wait(pe, "hs_ready", it * FT + f + 1)
                    pe.wait_ge(w2_in[f % WR], it * (16 * FT // WR) + 16 * (f // WR + 1))
                    for m in range(KC):
                        r = rows(m)
                        for n, (part, xx) in enumerate(((0, hh), (0, hl), (1, hh))):
                            last = pe.matmul(acc[0:r, m, :], w2[:, f % WR, part, m * P:m * P + r], xx[:, f % 2, :],
                                             start=(f == 0 and n == 0), stop=(f == FT - 1 and n == 2))
                    last.then_inc(s["y_done"], 1)
                s.wait(pe, "y_ready", it * KC + KC)
                for t in range(TPB):
                    if t >= 2:
                        s.wait(pe, "x3_ready", it * TPB + t - 1)
                    to_tokens(t, s["b2_done"])
                s.wait(pe, "x3_ready", it * TPB + TPB)
                for c in range(KC):
                    to_features(xr, c, s["t3_done"])
                s.wait(pe, "x3T_ready", it * KC + KC)
                s.wait(pe, "uri_ready", it + 1)
                for c in range(KC):
                    k = rows(c)
                    last = pe.matmul(hp[0][0:RD, :], uri[0:k, c, :], fT[0:k, c, :], start=(c == 0), stop=(c == KC - 1))
                last.then_inc(s["w_done"], 1)
                s.wait(pe, "wT_ready", it + 1)
                for t in range(TPB):
                    if t >= 2:
                        s.wait(pe, "xo_ready", it * TPB + t - 1)
                    for h in range(2):
                        last = pe.matmul(acc[:, 2 * (t % 2) + h, 0:HALF], wT[:, t * P:(t + 1) * P], UT[:, h * HALF:(h + 1) * HALF],
                                         start=True, stop=True)
                    last.then_inc(s["r_done"], 1)

        @block.vector
        def _(dve):
            s.give(dve, "xo_ready", "hs_ready")
            dve.memset(eps[:, :], LN_EPS)
            for c in range(KC):
                r = rows(c)
                s.wait(dve, "w1_hi", c + 1)
                dve.tensor_tensor(w1l[0:r, c, :], flat(stages[c % 2][0:r, :, :]), w1h[0:r, c, :].bitcast(F32), ALU.subtract).then_inc(s["w1_lo"], 1)
                s.wait(dve, "w1_lo", c + 1)
                dve.sem_inc(s["stage_free"], 1)
            for c in range(KC):
                r = rows(c)
                s.wait(dve, "wp_hi", c + 1)
                dve.tensor_tensor(wpl[0:r, c, :], xo[0:r, c % 4, :], wph[0:r, c, :].bitcast(F32), ALU.subtract).then_inc(s["wp_lo"], 1)
            s.wait(dve, "bias_in", 80)
            for r, c0, c1 in ((P, 0, KC - 1), (rows(KC - 1), KC - 1, KC)):
                for b in range(B):
                    for k, (sec, bias) in enumerate(((GATE_A, bp), (GATE_F, b2))):
                        last = dve.tensor_tensor(gb[0:r, b, k, c0:c1], modv[0:r, b, sec, c0:c1], bias[0:r, c0:c1], ALU.mult)
            last.then_inc(s["bias_ready"], 1)
            s.wait(dve, "wp_lo", KC)
            with dve.Fori(0, NBLK) as it:
                ch = Chain(dve, s["chain"], it * 2)

                def add_tokens(t, done, x_done):
                    s.wait(dve, done, it * TPB + t + 1)
                    pair = acc[:, :, :].rearrange("p a b -> p (a b)")[:, (t % 2) * 1024:(t % 2) * 1024 + D]
                    dve.tensor_tensor(xr[:, t, :], pair, xr[:, t, :], ALU.add).then_inc(s[x_done], 1)

                for c in range(KC):
                    r = rows(c)
                    s.wait(dve, "o_hi", it * KC + c + 1)
                    dve.tensor_tensor(fl[0:r, c, :], acc[0:r, c, :], fh[0:r, c, :].bitcast(F32), ALU.subtract).then_inc(s["o_lo"], 1)
                s.wait(dve, "x_in", it * 16 + 16)
                for t in range(TPB):
                    add_tokens(t, "b_done", "x2_ready")
                s.wait(dve, "x2_ready", it * TPB + TPB)
                for t in range(TPB):
                    for h in range(2):
                        last = dve.bn_stats(st[:, t, h, :], xr[:, t, h * HALF:(h + 1) * HALF])
                last.then_inc(s["st_ready"], 1)
                dve.drain()
                for t in range(TPB):
                    last = dve.bn_aggr(mv[:, t, :], st[:, t, :, :].rearrange("p a b -> p (a b)"))
                last.then_inc(s["var_ready"], 1)
                s.wait(dve, "std_ready", it + 1)
                ch.do(dve.reciprocal(rs[:, :], sd[:, :]))
                st_out.wait(dve, "out_st", it * 16)
                for t in range(TPB):
                    last = dve.tensor_scalar(xo[:, t, :], xr[:, t, :], mv[:, t, 0:1], rs[:, t:t + 1], ALU.subtract, ALU.mult)
                last.then_inc(s["xn_ready"], 1)
                for c in range(KC):
                    r = rows(c)
                    s.wait(dve, "xm_ready", it * KC + c + 1)
                    last = dve.tensor_copy(fh[0:r, c, :], fT[0:r, c, :])
                ch.do(last)
                for c in range(KC):
                    r = rows(c)
                    dve.tensor_tensor(fl[0:r, c, :], fT[0:r, c, :], fh[0:r, c, :].bitcast(F32), ALU.subtract).then_inc(s["xs_ready"], 1)
                for f in range(FT):
                    s.wait(dve, "g_ready", it * FT + f + 1)
                    s.wait(dve, "y_done", it * FT + max(0, f - 1))
                    dve.tensor_copy(hh[:, f % 2, :], hb[:, f % 2, :]).then_inc(s["hh_ready"], 1)
                    s.wait(dve, "hh_ready", it * FT + f + 1)
                    dve.tensor_tensor(hl[:, f % 2, :], hb[:, f % 2, :], hh[:, f % 2, :].bitcast(F32), ALU.subtract).then_inc(s["hs_ready"], 1)
                for t in range(TPB):
                    add_tokens(t, "b2_done", "x3_ready")
                for t in range(TPB):
                    s.wait(dve, "r_done", it * TPB + t + 1)
                    dve.tensor_tensor(xo[:, t, :].rearrange("p (a b) -> p a b", a=2),
                                      acc[:, 2 * (t % 2):2 * (t % 2) + 2, 0:HALF],
                                      xr[:, t, :].rearrange("p (a b) -> p a b", a=2), ALU.add).then_inc(s["xo_ready"], 1)


def program(nc, io, out, stop=None, dbg=None):
    with ExitStack() as keep:
        keep.enter_context(nc.allow_non_contiguous_dma(reason="short vectors, one value a partition"))
        sb = lambda name, shape, dt=F32: keep.enter_context(nc.sbuf_tensor(name, shape, dt))
        dram = lambda name, shape: nc.dram_tensor(name, shape, F32, kind="Internal").ap()
        g = {
            "ident": sb("ident", [P, P]),
            "modv": sb("modv", [P, B, SECTIONS, KC]),
            "UT": sb("UT", [RD, D]),
            "URI": sb("URI", [P, B, KC, RD]),
            "w2_split": dram("w2_split", [P, FT, 2, D]),
            "skew_scratch": dram("skew_scratch", [B, SKEW + 2 * RD]),
            "attn_scratch": dram("attn_scratch", [B * T, D]),
        }
        for n in ("q_hi", "q_lo", "k_hi", "k_lo"):
            g[n] = dram(n + "_scratch", [B * D, T])
        with ExitStack() as basis:
            for n, shape in (("E", [RD, 2, B, RD]), ("G", [RD, RD]), ("M", [RD, 2 * ML]), ("step", [RD, P]), ("stepT", [RD, P]),
                             ("X2", [RD, 2, ML]), ("one", [1, 1]), ("signs", [1, RD + 1]), ("half_mask", [RD, RD])):
                g[n] = basis.enter_context(nc.sbuf_tensor("basis_" + n, shape, F32))
            setup(nc, io, g)
            if stop == "setup":
                return dbg(nc, g)
            with nc.sbuf_tensor("V_all", [P, NH, KT, HD], F32) as V:
                g["V"] = V
                qkv(nc, io, g)
                if stop == "qkv":
                    return dbg(nc, g)
                attention(nc, io, g)
        if stop == "attn":
            return dbg(nc, g)
        mlp(nc, io, g, out)


_INS = ["x", "cond_1152", "L0_cond_w_qkv", "L0_cond_b_qkv", "L0_cond_w_proj", "L0_cond_b_proj", "L0_cond_w_fc1",
        "L0_cond_b_fc1", "L0_cond_w_fc2", "L0_cond_b_fc2", "L0_cond_w_ada", "L0_cond_b_ada", "L1_cond_P",
        "L1_cond_W", "L1_cond_b"]


def kernel(**inputs):
    import numpy as _np
    import concourse.bacc as _bacc
    from concourse import mybir as _mybir
    from concourse.bass_utils import run_bass_kernel_spmd as _run

    nc = _bacc.Bacc("TRN2", target_bir_lowering=False, num_devices=1)
    arrays, io = {}, {}
    for name in _INS:
        a = _np.ascontiguousarray(inputs[name])
        arrays[f"in_{name}"] = a
        io[name] = nc.dram_tensor(f"in_{name}", a.shape, _mybir.dt.from_np(a.dtype), kind="ExternalInput").ap()
    out = nc.dram_tensor("out_0", (B, T, D), _mybir.dt.float32, kind="ExternalOutput").ap()
    program(nc, io, out)
    r = _run(nc, [arrays], core_ids=[0])
    return r.results[0]["out_0"]
```

```python
from contextlib import ExitStack

import concourse.bass as bass
from concourse import mybir

F32 = mybir.dt.float32
F32R = mybir.dt.float32r
ALU = mybir.AluOpType
ACT = mybir.ActivationFunctionType
AX = mybir.AxisListType

P = 128
B, T, D = 2, 2048, 576
H, HD = 16, 36
HID = 4 * D
RD = 64
SKEW = RD * (RD - 1) // 2
BLK = 512
TPB = BLK // P
NBLK = B * T // BLK
BPB = T // BLK
KC = 5
HALF = D // 2
FT = HID // P
NH = B * H
KT = T // P
QKT = 2 * D // P
LN_EPS = 1e-6
SECTIONS = 6
SHIFT_A, SCALE_A, GATE_A, SHIFT_F, SCALE_F, GATE_F = range(SECTIONS)


def rows(c):
    return min(P, D - c * P)


class Chain:

    def __init__(self, eng, sem, base=0):
        self.eng, self.sem, self.base, self.n = eng, sem, base, 0

    def mark(self, ins):
        ins.then_inc(self.sem, 1)
        self.n += 1

    def wait(self):
        self.eng.wait_ge(self.sem, self.base + self.n)

    def do(self, ins):
        self.mark(ins)
        self.wait()


class Counts:

    def __init__(self, sem, names, credited, credit=1):
        self.sems = {n: sem(n) for n in names}
        self.credit = {n: credit * (n in credited) for n in names}

    def __getitem__(self, name):
        return self.sems[name]

    def wait(self, eng, name, count):
        eng.wait_ge(self.sems[name], count + self.credit[name])

    def give(self, eng, *names):
        for n in names:
            eng.sem_inc(self.sems[n], self.credit[n])


def load_chunked(eng, dst, src, sem):
    full = (KC - 1) * P
    eng.dma_start(dst[:, 0:KC - 1, :], src[0:full, :].rearrange("(c p) n -> p c n", p=P)).then_inc(sem, 16)
    eng.dma_start(dst[0:D - full, KC - 1, :], src[full:D, :]).then_inc(sem, 16)


def load_columns(eng, dst, src, sem):
    full = (KC - 1) * P
    eng.dma_start(dst[:, 0:KC - 1], src[0:full].rearrange("(c p) -> p c", p=P)).then_inc(sem, 16)
    eng.dma_start(dst[0:D - full, KC - 1:KC], src[full:D].rearrange("(p a) -> p a", a=1)).then_inc(sem, 16)


def row(v):
    return v.rearrange("(a n) -> a n", a=1)


SQUARINGS, DEGREE = 10, 8
ML = RD + 1


def setup(nc, io, g):
    VT = 16
    VP = SKEW // VT
    PAD = RD
    WR = 2
    WP = VT // 4
    with ExitStack() as ctx:
        sb = lambda name, shape, dt=F32: ctx.enter_context(nc.sbuf_tensor(name, shape, dt))
        sem = lambda name: ctx.enter_context(nc.semaphore(name))
        psum = lambda name, shape: ctx.enter_context(nc.psum_tensor(name, shape, F32))
        ident, modv = g["ident"], g["modv"]
        G, M, PT, E, step, stepT, X2, one = (g[x] for x in ("G", "M", "UT", "E", "step", "stepT", "X2", "one"))
        half_mask = g["half_mask"]
        wh, wl, wv = g["wqk_hi"], g["wqk_lo"], g["wv"]
        stage = sb("wqk_raw", [P, 2, 2 * D])
        wa = sb("w_ada_ring", [P, WR, KC, D])
        condT = sb("condT", [P, KC, B])
        siluT = sb("siluT", [P, KC, B])
        badaT = sb("badaT", [P, SECTIONS, KC])
        Pc = sb("Pc", [P, KC, RD])
        crow = sb("cond_rows", [B, D])
        srow = sb("silu_rows", [B, D])
        selb = sb("sel_batch", [B, B, VP])
        sbc = sb("silu_bcast", [VP, B, D])
        Wv = sb("W_skew_ring", [VP, WR, WP, D])
        junk = sb("junk", [VP, D])
        v = sb("v", [VP, B, VT])
        vT = sb("vT", [B * VT, VP])
        bvT = sb("b_skewT", [B * VT, VP])
        zpad = sb("zpad", [B, PAD])
        Au = sb("A_upper", [RD, B, RD])
        X = sb("X_skew", [RD, B, RD])
        Xn = sb("X_skew_neg", [RD, B, RD])
        E2 = sb("E_pair2", [RD, 2, B, RD])
        ps = psum("ps_ada", [P, SECTIONS, KC, B])
        pr = psum("ps_ada_rows", [B, 2, 512])
        ada_rows = (crow, srow)
        pA, pB, pC = psum("pA", [P, 2, 512]), psum("pB", [P, 512]), psum("pC", [P, 512])
        cond_in, bada_in, p_in, c_in, b_in = (sem(x) for x in ("cond_in", "bada_in", "P_in", "crow_in", "bskew_in"))
        wa_in = [sem(f"wa_in{s}") for s in range(WR)]
        w_in = [sem(f"W_in{k}") for k in range(WR)]
        wa_used, w_used, qkv_hi, qkv_lo, wv_in, rows_ready = (
            sem(x) for x in ("wa_used", "W_used", "qkv_hi", "qkv_lo", "wv_in", "ada_rows_ready"))
        stage_in = [sem(f"wqk_in{c}") for c in range(2)]
        silu_ready, mod_done = sem("silu_ready"), sem("mod_done")
        ident_zero, ident_ready, mask_ready, upper_ready = (sem(x) for x in ("ident_zero", "ident_ready", "mask_ready", "upper_ready"))
        v_out, a_in, const_s = sem("v_out"), sem("A_in"), sem("const_chain")
        srow_ready, sbc_mm, sbc_ready, v_ready, vT_mm, vT_ready = (
            sem(x) for x in ("srow_ready", "sbc_mm", "sbc_ready", "v_ready", "vT_mm", "vT_ready"))
        gram_mm, pt_mm, auT_mm, x_ready, e_mm, e_ready, chain_s = (
            sem(x) for x in ("gram_mm", "pt_mm", "auT_mm", "x_ready", "e_mm", "e_ready", "setup_chain"))
        vs = g["skew_scratch"]
        block = ctx.enter_context(nc.Block())

        @block.sync
        def _(sp):
            sp.dma_start(crow[:, :], io["cond_1152"]).then_inc(c_in, 16)

            def load_skew(k):
                sp.dma_start(Wv[:, k % WR, :, :], io["L1_cond_W"].rearrange("(t p) k -> p t k", p=VP)[:, k * WP:(k + 1) * WP, :]
                             ).then_inc(w_in[k % WR], 16)

            def load_qk(c):
                sp.dma_start(stage[0:rows(c), c % 2, :], io["L0_cond_w_qkv"][c * P:c * P + rows(c), 0:2 * D]).then_inc(stage_in[c % 2], 16)

            def load_ada(s):
                load_chunked(sp, wa[:, s % WR, :, :], io["L0_cond_w_ada"][:, s * D:(s + 1) * D], wa_in[s % WR])

            for k in range(WR):
                load_skew(k)
            load_chunked(sp, Pc[:, :, :], io["L1_cond_P"], p_in)
            for b in range(B):
                sp.dma_start(bvT[b * VT:(b + 1) * VT, :], io["L1_cond_b"].rearrange("(t p) -> t p", p=VP)).then_inc(b_in, 16)
            for k in range(WR, VT // WP):
                sp.wait_ge(w_used, k - WR + 1)
                load_skew(k)
            for b in range(B):
                load_columns(sp, condT[:, :, b], io["cond_1152"][b, :], cond_in)
            for c in range(2):
                load_qk(c)
            load_ada(0)
            load_ada(1)
            bsec = io["L0_cond_b_ada"].rearrange("(s f) -> s f", s=SECTIONS)
            for s in range(SECTIONS):
                load_columns(sp, badaT[:, s, :], bsec[s, :], bada_in)
            load_chunked(sp, wv[:, :, :], io["L0_cond_w_qkv"][:, 2 * D:3 * D], wv_in)
            for s in range(WR, SECTIONS):
                sp.wait_ge(wa_used, s - WR + 1)
                load_ada(s)
                if s < KC:
                    sp.wait_ge(qkv_lo, s - 1)
                    load_qk(s)
            sp.wait_ge(wv_in, 32)

        @block.gpsimd
        def _(pool):
            pool.memset(ident[:, :], 0.0).then_inc(ident_zero, 1)
            pool.wait_ge(ident_zero, 1)
            pool.affine_select(out=ident[:, :], in_=ident[:, :], compare_op=ALU.not_equal, fill=1.0,
                               base=0, pattern=[[-1, P]], channel_multiplier=1).then_inc(ident_ready, 1)
            ch = Chain(pool, const_s)
            ch.do(pool.memset(selb[:, :, :], 0.0))
            ch.do(pool.affine_select(out=selb[:, :, :], in_=selb[:, :, :], compare_op=ALU.not_equal, fill=1.0,
                                     base=0, pattern=[[-1, B], [0, VP]], channel_multiplier=1))
            ch.do(pool.memset(M[:, :], 0.0))
            ch.do(pool.memset(X2[:, :, :], 0.0))
            pool.memset(zpad[:, :], 0.0).then_inc(mask_ready, 1)
            ch.do(pool.memset(half_mask[:, :], 1.0))
            ch.do(pool.affine_select(out=half_mask[:, :], in_=half_mask[:, :], compare_op=ALU.not_equal, fill=0.5,
                                     base=0, pattern=[[-1, RD]], channel_multiplier=1))
            ch.do(pool.affine_select(out=half_mask[:, :], in_=half_mask[:, :], compare_op=ALU.is_ge, fill=0.0,
                                     base=0, pattern=[[1, RD]], channel_multiplier=-1))
            for m in (step, stepT):
                ch.do(pool.memset(m[:, :], 0.0))
                ch.do(pool.affine_select(out=m[:, 0:RD], in_=m[:, 0:RD], compare_op=ALU.not_equal, fill=1.0,
                                         base=-1, pattern=[[-1, RD]], channel_multiplier=1))
            ch.do(pool.memset(step[0:1, RD - 1:RD], 1.0))
            pool.memset(one[:, :], 1.0)
            pool.wait_ge(a_in, 8 * RD)
            pool.affine_select(out=Au[:, :, :], in_=Au[:, :, :], compare_op=ALU.is_gt, fill=0.0,
                               base=0, pattern=[[0, B], [1, RD]], channel_multiplier=-1).then_inc(upper_ready, 1)

        @block.scalar
        def _(act):
            act.wait_ge(c_in, 16)
            act.activation(srow[:, :], crow[:, :], ACT.Silu).then_inc(srow_ready, 1)
            act.wait_ge(mask_ready, 1)
            act.dma_start(vs[:, 0:PAD], zpad[:, :]).then_inc(v_out, 16)
            act.dma_start(vs[:, PAD + SKEW:PAD + SKEW + PAD], zpad[:, :]).then_inc(v_out, 16)
            for b in range(B):
                for h in range(2):
                    act.wait_ge(sbc_mm, 2 * b + h + 1)
                    act.activation(sbc[:, b, h * HALF:(h + 1) * HALF], pA[0:VP, h, 0:HALF], ACT.Copy).then_inc(sbc_ready, 1)
            act.wait_ge(cond_in, 64)
            for r, c0, c1 in ((P, 0, KC - 1), (rows(KC - 1), KC - 1, KC)):
                act.activation(siluT[0:r, c0:c1, :], condT[0:r, c0:c1, :], ACT.Silu).then_inc(silu_ready, 1)
            for c in range(KC):
                if c == 2:
                    act.wait_ge(vT_ready, 1)
                    for b in range(B):
                        act.dma_start(vs[b, PAD:PAD + SKEW].rearrange("(t p) -> t p", p=VP),
                                      vT[b * VT:(b + 1) * VT, :]).then_inc(v_out, 16)
                    act.wait_ge(v_out, 64)
                    for i in range(0, RD, 2):
                        start = PAD + (RD - 2) * i - i * (i - 1) // 2 - 1
                        first = vs[:, start:start + RD]
                        pair = bass.AP(tensor=first.tensor, offset=first.offset, ap=[[RD - 2 - i, 2], [SKEW + 2 * PAD, B], [1, RD]])
                        act.dma_start(Au[i:i + 2, :, :], pair).then_inc(a_in, 16)
                act.wait_ge(stage_in[c % 2], 16 * (c // 2 + 1))
                act.activation(wh[0:rows(c), c, :], stage[0:rows(c), c % 2, :], ACT.Copy).then_inc(qkv_hi, 1)

        @block.tensor
        def _(pe):
            pe.wait_ge(srow_ready, 1)
            pe.wait_ge(mask_ready, 1)
            for b in range(B):
                for h in range(2):
                    if b:
                        pe.wait_ge(sbc_ready, h + 1)
                    pe.matmul(pA[0:VP, h, 0:HALF], selb[:, b, :], srow[:, h * HALF:(h + 1) * HALF],
                              start=True, stop=True).then_inc(sbc_mm, 1)
            pe.wait_ge(p_in, 32)
            for c in range(KC):
                last = pe.matmul(pB[0:RD, 0:RD], Pc[0:rows(c), c, :], Pc[0:rows(c), c, :], start=(c == 0), stop=(c == KC - 1))
            last.then_inc(gram_mm, 1)
            pe.wait_ge(sbc_ready, 4)
            pe.wait_ge(ident_ready, 1)
            for c in range(KC):
                last = pe.transpose(pA[0:RD, c // 4, (c % 4) * P:(c % 4) * P + rows(c)], Pc[0:rows(c), c, :],
                                    ident[0:rows(c), 0:rows(c)])
            last.then_inc(pt_mm, 1)
            pe.wait_ge(v_ready, 1)
            pe.transpose(pC[0:B * VT, 0:VP], v[:, :, :].rearrange("p b t -> p (b t)"), ident[0:VP, 0:VP]).then_inc(vT_mm, 1)
            def ada_columns(s):
                pe.wait_ge(rows_ready, s + 1)
                for m in range(KC):
                    last = pe.transpose(ps[0:rows(m), s, m, :], ada_rows[s % 2][:, m * P:m * P + rows(m)], ident[0:B, 0:B])
                return last

            def ada_chunk(s, c):
                if c == 0:
                    if s:
                        ada_columns(s - 1)
                    pe.wait_ge(wa_in[s % WR], 32 * (s // WR + 1))
                for h in range(2):
                    last = pe.matmul(pr[:, h, 0:HALF], siluT[0:rows(c), c, :], wa[0:rows(c), s % WR, c, h * HALF:(h + 1) * HALF],
                                     start=(c == 0), stop=(c == KC - 1))
                if c == KC - 1:
                    last.then_inc(wa_used, 1)

            beside = {first + c: (s, c) for s, first in ((4, 5), (5, 11)) for c in range(KC)}

            pe.wait_ge(silu_ready, 2)
            for x in range(4):
                for c in range(KC):
                    ada_chunk(x, c)
            pe.wait_ge(upper_ready, 1)
            for b in range(B):
                last = pe.transpose(pB[0:RD, b * RD:(b + 1) * RD], Au[:, b, :], ident[0:RD, 0:RD])
            last.then_inc(auT_mm, 1)
            pe.wait_ge(x_ready, 1)
            for k in range(DEGREE - 1):
                pe.wait_ge(e_ready, k + 1)
                for b in range(B):
                    pe.matmul(pC[0:RD, b * RD:(b + 1) * RD], Xn[:, b, :], E[:, 0, b, :], start=True, stop=True)
                    last = pe.matmul(pC[0:RD, (B + b) * RD:(B + b + 1) * RD], X[:, b, :], E[:, 1, b, :], start=True, stop=True)
                last.then_inc(e_mm, 1)
                if k in beside:
                    ada_chunk(*beside[k])
            for k in range(SQUARINGS):
                src = (E, E2)[k % 2]
                pe.wait_ge(e_ready, DEGREE + k)
                for b in range(B):
                    pe.matmul(pC[0:RD, b * RD:(b + 1) * RD], src[:, 1, b, :], src[:, 0, b, :], start=True, stop=True)
                    last = pe.matmul(pC[0:RD, (B + b) * RD:(B + b + 1) * RD], src[:, 0, b, :], src[:, 1, b, :], start=True, stop=True)
                last.then_inc(e_mm, 1)
                if k + DEGREE - 1 in beside:
                    ada_chunk(*beside[k + DEGREE - 1])
            ada_columns(SECTIONS - 1).then_inc(e_mm, 1)

        @block.vector
        def _(dve):
            ch = Chain(dve, chain_s)
            dve.wait_ge(sbc_ready, 4)
            for t in range(VT):
                if t % WP == 0:
                    dve.wait_ge(w_in[t // WP % WR], 16 * (t // WP // WR + 1))
                for b in range(B):
                    ch.do(dve.tensor_tensor_reduce(out=junk[:, :], in0=Wv[:, t // WP % WR, t % WP, :], in1=sbc[:, b, :], scale=1.0,
                                                   scalar=0.0, op0=ALU.mult, op1=ALU.add, accum_out=v[:, b, t:t + 1]))
                if t % WP == WP - 1:
                    dve.sem_inc(w_used, 1)
            dve.sem_inc(v_ready, 1)
            dve.wait_ge(gram_mm, 1)
            dve.wait_ge(mask_ready, 1)
            dve.wait_ge(ident_ready, 1)
            ch.do(dve.tensor_copy(G[:, :], pB[0:RD, 0:RD]))
            dve.tensor_copy(M[:, 0:RD], G[:, :])
            dve.tensor_copy(M[:, ML:ML + RD], ident[0:RD, 0:RD])
            dve.wait_ge(pt_mm, 1)
            dve.tensor_copy(PT[:, 0:D], pA[0:RD, :, :].rearrange("p a b -> p (a b)")[:, 0:D])
            dve.wait_ge(b_in, 32)
            dve.wait_ge(vT_mm, 1)
            dve.tensor_tensor(vT[:, :], pC[0:B * VT, 0:VP], bvT[:, :], ALU.add).then_inc(vT_ready, 1)
            def ada_to_rows(s):
                dve.wait_ge(wa_used, s + 1)
                dve.tensor_copy(ada_rows[s % 2][:, :].rearrange("p (a b) -> p a b", a=2), pr[:, :, 0:HALF]).then_inc(rows_ready, 1)

            for c in range(KC):
                r = rows(c)
                for x in {2: (0, 1), 3: (2,), 4: (3,)}.get(c, ()):
                    ada_to_rows(x)
                dve.wait_ge(qkv_hi, c + 1)
                dve.tensor_tensor(wl[0:r, c, :], stage[0:r, c % 2, :], wh[0:r, c, :].bitcast(F32), ALU.subtract).then_inc(qkv_lo, 1)
            dve.wait_ge(auT_mm, 1)
            ch.do(dve.tensor_tensor(X[:, :, :], Au[:, :, :], pB[0:RD, 0:B * RD].rearrange("p (b c) -> p b c", b=B), ALU.subtract))
            ch.do(dve.tensor_scalar(Xn[:, :, :], X[:, :, :], -1.0 / 2 ** SQUARINGS, None, ALU.mult))
            ch.do(dve.tensor_scalar(X[:, :, :], X[:, :, :], 1.0 / 2 ** SQUARINGS, None, ALU.mult))
            dve.sem_inc(x_ready, 1)
            ch.do(dve.tensor_scalar(E[:, 0, :, :], X[:, :, :], 1.0 / DEGREE, None, ALU.mult))
            dve.tensor_scalar(E[:, 1, :, :], Xn[:, :, :], 1.0 / DEGREE, None, ALU.mult).then_inc(e_ready, 1)
            pairs = pC[0:RD, 0:2 * B * RD].rearrange("p (e b c) -> p e b c", e=2, b=B)
            for k in range(DEGREE - 1):
                dve.wait_ge(e_mm, 1 + k)
                ch.do(dve.tensor_tensor(E2[:, 0, :, :], pairs[:, 0], X[:, :, :], ALU.add))
                ch.do(dve.tensor_tensor(E2[:, 1, :, :], pairs[:, 1], Xn[:, :, :], ALU.add))
                dve.tensor_scalar(E[:, :, :, :], E2[:, :, :, :], 1.0 / (DEGREE - 1 - k), None, ALU.mult).then_inc(e_ready, 1)
            for k in range(SQUARINGS):
                src, dst = ((E, E2), (E2, E))[k % 2]
                if k == 4:
                    ada_to_rows(4)
                dve.wait_ge(e_mm, DEGREE + k)
                dve.wait_ge(e_ready, DEGREE + k)
                dve.scalar_tensor_tensor(out=dst[:, :, :, :], in0=src[:, :, :, :], scalar=2.0, in1=pairs,
                                         op0=ALU.mult, op1=ALU.add).then_inc(e_ready, 1)
            ada_to_rows(5)
            dve.wait_ge(bada_in, 32 * SECTIONS)
            dve.wait_ge(e_mm, DEGREE + SQUARINGS)
            parts = ((P, 0, KC - 1), (rows(KC - 1), KC - 1, KC))
            for r, c0, c1 in parts:
                for b in range(B):
                    dve.tensor_tensor(modv[0:r, b, :, c0:c1], ps[0:r, :, c0:c1, b], badaT[0:r, :, c0:c1],
                                      ALU.add).then_inc(mod_done, 1)
            dve.wait_ge(mod_done, 4)
            for r, c0, c1 in parts:
                for s in (SCALE_A, SCALE_F):
                    dve.tensor_scalar(modv[0:r, :, s, c0:c1], modv[0:r, :, s, c0:c1], 1.0, None, ALU.add)


def qkv(nc, io, g):
    V = g["V"]
    MOD_AFTER = {4: (0, 1), 5: (2, 3), 6: (4,)}
    RING = 3
    ELIM = RD // NBLK
    with ExitStack() as ctx:
        sb = lambda name, shape, dt=F32: ctx.enter_context(nc.sbuf_tensor(name, shape, dt))
        sem = lambda name: ctx.enter_context(nc.semaphore(name))
        psum = lambda name, shape: ctx.enter_context(nc.psum_tensor(name, shape, F32))
        ident, modv = g["ident"], g["modv"]
        wh, wl, wv = g["wqk_hi"], g["wqk_lo"], g["wv"]
        bqk = sb("bqk", [P, QKT])
        ones = sb("ones_row", [1, P])
        bvr = sb("bv_row", [1, D])
        bvb = sb("bv_bcast", [P, 2, HALF])
        eps = sb("eps", [P, 1])
        x = sb("x_blk", [P, TPB, D])
        xn = sb("x_norm", [P, TPB, KC * P])
        M, step = g["M"], g["step"]
        piv = sb("pivot", [1, 1])
        st = sb("ln_stats", [P, TPB, 2, 6])
        mv = sb("ln_mv", [P, TPB, 2])
        sd = sb("ln_std", [P, TPB])
        rs = sb("ln_rstd", [P, TPB])
        xm = sb("x_modT", [P, KC, BLK])
        xh = sb("x_modT_hi", [P, KC, BLK], F32R)
        xl = sb("x_modT_lo", [P, KC, BLK], F32R)
        oh = sb("qk_hi_out", [P, RING, BLK], F32R)
        ol = sb("qk_lo_out", [P, RING, BLK], F32R)
        tp = [psum(f"tp{i}", [P, BLK]) for i in range(2)]
        qk = [psum(f"qk{i}", [P, BLK]) for i in range(RING)]
        vp = [psum(f"vp{i}", [P, BLK]) for i in range(2)]
        el = psum("elim_ps", [P, BLK])
        names = ("bias_in ones_ready stack_in bvb_mm bvb_ready x_in x_used st_ready var_ready std_ready "
                 "xn_ready tr_done xm_ready xs_ready qk_done hi_ready lo_ready v_done v_ready chain elim_chain row_ready elim_mm elim_ready")
        s = Counts(lambda n: sem("a_" + n), names.split(), ("v_done", "xs_ready", "xm_ready", "v_ready", "lo_ready", "tr_done", "qk_done", "elim_ready"))
        rings = range(RING)
        outs = Counts(lambda n: sem("a_" + n), [f"out_{p}{i}" for p in ("hi", "lo") for i in rings],
                      [f"out_{p}{i}" for p in ("hi", "lo") for i in rings], credit=16)
        w_qkv, b_qkv = io["L0_cond_w_qkv"], io["L0_cond_b_qkv"]
        xv = io["x"].rearrange("b (k t p) d -> (b k) p t d", p=P, t=TPB)
        block = ctx.enter_context(nc.Block())

        @block.sync
        def _(sp):
            outs.give(sp, *outs.sems)
            sp.dma_start(bqk[:, :], b_qkv[0:2 * D].rearrange("(m p) -> p m", p=P)).then_inc(s["bias_in"], 16)
            sp.dma_start(bvr[:, :], row(b_qkv[2 * D:3 * D])).then_inc(s["bias_in"], 16)
            sp.dma_start(x[:, :, :], xv[0]).then_inc(s["x_in"], 16)
            tail = rows(KC - 1)
            sp.dma_start(wh[tail:P, KC - 1, :].bitcast(F32), wl[0:tail, KC - 1, :].bitcast(F32)).then_inc(s["stack_in"], 16)
            sp.dma_start(modv[tail:P, :, :, KC - 1], modv[0:tail, :, :, KC - 1]).then_inc(s["stack_in"], 16)
            s.wait(sp, "x_used", 1)
            sp.dma_start(x[:, :, :], xv[1]).then_inc(s["x_in"], 16)

            def iteration(it, nxt):
                for m in range(QKT):
                    for part, ready, src, out in (("q_hi", "hi_ready", oh, "out_hi"), ("q_lo", "lo_ready", ol, "out_lo")):
                        s.wait(sp, ready, it * QKT + m + 1)
                        f0 = m * P
                        nq = max(0, min(P, D - f0))
                        cols = bass.ds((it % BPB) * BLK, BLK)
                        pieces = [(0, nq, part, f0)] if nq else []
                        pieces += [(nq, P, part.replace("q", "k"), f0 + nq - D)] if nq < P else []
                        for p0, p1, name, r0 in pieces:
                            sp.dma_start(g[name][bass.ds((it // BPB) * D + r0, p1 - p0), cols],
                                         src[p0:p1, m % RING, :].bitcast(F32)).then_inc(outs[f"{out}{m % RING}"], 16)
                    if m == 2 and nxt:
                        s.wait(sp, "x_used", it + 2)
                        sp.dma_start(x[:, :, :], xv[bass.ds((it + 2) % NBLK, 1)].rearrange("a p t d -> p (a t) d")
                                     ).then_inc(s["x_in"], 16)

            with sp.Fori(0, NBLK - 1) as it:
                iteration(it, True)
            iteration(NBLK - 1, False)
            s.wait(sp, "x_in", 16 * (NBLK + 1))
            for out in ("out_hi", "out_lo"):
                for i in rings:
                    outs.wait(sp, f"{out}{i}", 16 * NBLK * (QKT // RING + (i == (QKT // 2) % RING)))

        @block.scalar
        def _(act):
            s.give(act, "xm_ready")
            s.wait(act, "bvb_mm", 1)
            for h in range(2):
                act.activation(bvb[:, h, :], vp[h][:, 0:HALF], ACT.Copy).then_inc(s["bvb_ready"], 1)
            s.wait(act, "bias_in", 32)
            s.wait(act, "stack_in", 32)

            def root(n):
                s.wait(act, "var_ready", n + 1)
                act.activation(sd[:, :], mv[:, :, 1], ACT.Sqrt, bias=eps[:, :]).then_inc(s["std_ready"], 1)

            def modulate(n, c):
                if c == 0:
                    s.wait(act, "v_done", n * 2 * TPB)
                    s.wait(act, "xs_ready", n * KC)
                s.wait(act, "tr_done", n * KC + c + 1)
                act.activation(xm[:, c, :], tp[c % 2][:, :], ACT.Identity,
                               bias=modv[:, bass.ds(n // BPB, 1), SHIFT_A, c:c + 1].rearrange("p a b -> p (a b)"),
                               scale=modv[:, bass.ds(n // BPB, 1), SCALE_A, c:c + 1].rearrange("p a b -> p (a b)")
                               ).then_inc(s["xm_ready"], 1)

            def iteration(it, nxt):
                if nxt:
                    root(it + 1)
                for m in range(QKT):
                    s.wait(act, "qk_done", it * QKT + m + 1)
                    k, extra = m // RING, int(m % RING == (QKT // 2) % RING)
                    stores = it * (QKT // RING + extra) + k + int(extra and m > QKT // 2)
                    outs.wait(act, f"out_hi{m % RING}", stores * 16)
                    act.activation(oh[:, m % RING, :], qk[m % RING][:, :], ACT.Identity,
                                   bias=bqk[:, m:m + 1]).then_inc(s["hi_ready"], 1)
                    if nxt:
                        for c in MOD_AFTER.get(m, ()):
                            modulate(it + 1, c)

            root(0)
            for c in range(KC):
                modulate(0, c)
            with act.Fori(0, NBLK - 1) as it:
                iteration(it, True)
            iteration(NBLK - 1, False)

        @block.tensor
        def _(pe):
            s.give(pe, "v_done", "tr_done", "qk_done")
            s.wait(pe, "ones_ready", 1)
            s.wait(pe, "bias_in", 32)
            for h in range(2):
                last = pe.matmul(vp[h][:, 0:HALF], ones[:, :], bvr[:, h * HALF:(h + 1) * HALF], start=True, stop=True)
            last.then_inc(s["bvb_mm"], 1)
            s.wait(pe, "bvb_ready", 2)

            def transposes(n, c):
                s.wait(pe, "xm_ready", n * KC + max(0, c - 1))
                for t in range(TPB):
                    last = pe.transpose(tp[c % 2][:, t * P:(t + 1) * P], xn[:, t, c * P:(c + 1) * P], ident[:, :])
                last.then_inc(s["tr_done"], 1)

            def iteration(it, nxt):
                s.wait(pe, "xm_ready", it * KC + KC)
                for t in range(TPB):
                    for h in range(2):
                        s.wait(pe, "v_ready", it * 2 * TPB + max(0, 2 * t + h - 1))
                        for c in range(KC):
                            last = pe.matmul(vp[h][:, 0:HALF], xm[0:rows(c), c, t * P:(t + 1) * P],
                                             wv[0:rows(c), c, h * HALF:(h + 1) * HALF], start=(c == 0), stop=(c == KC - 1))
                        last.then_inc(s["v_done"], 1)
                s.wait(pe, "xs_ready", it * KC + KC)
                for m in range(QKT):
                    s.wait(pe, "lo_ready", it * QKT + max(0, m - RING + 1))
                    cols = slice(m * P, (m + 1) * P)
                    passes = split_passes(lambda c, k: wh[0:k, c, cols], lambda c, k: wl[0:k, c, cols],
                                          lambda c, k: xh[0:k, c, :], lambda c, k: xl[0:k, c, :])
                    for n, (w, xx) in enumerate(passes):
                        last = pe.matmul(qk[m % RING][:, :], w, xx, start=(n == 0), stop=(n == len(passes) - 1))
                    last.then_inc(s["qk_done"], 1)
                    if m:
                        s.wait(pe, "row_ready", it * ELIM + m)
                        pe.matmul(el[:, 0:ML + RD], step[:, :], M[:, 0:ML + RD], start=True, stop=True).then_inc(s["elim_mm"], 1)
                    if nxt:
                        if m == min(MOD_AFTER):
                            s.wait(pe, "xn_ready", it + 2)
                        for c in MOD_AFTER.get(m, ()):
                            transposes(it + 1, c)

            s.wait(pe, "stack_in", 32)
            s.wait(pe, "xn_ready", 1)
            for c in range(KC):
                transposes(0, c)
            with pe.Fori(0, NBLK - 1) as it:
                iteration(it, True)
            iteration(NBLK - 1, False)

        @block.vector
        def _(dve):
            s.give(dve, "xs_ready", "v_ready", "lo_ready", "elim_ready")
            dve.memset(ones[:, :], 1.0).then_inc(s["ones_ready"], 1)
            dve.memset(eps[:, :], LN_EPS)
            s.wait(dve, "bvb_ready", 2)

            def stats(n, t):
                if t == 0:
                    s.wait(dve, "x_in", n * 16 + 16)
                for h in range(2):
                    last = dve.bn_stats(st[:, t, h, :], x[:, t, h * HALF:(h + 1) * HALF])
                if t == TPB - 1:
                    last.then_inc(s["st_ready"], 1)

            def normalise(n):
                dve.drain()
                for t in range(TPB):
                    last = dve.bn_aggr(mv[:, t, :], st[:, t, :, :].rearrange("p a b -> p (a b)"))
                last.then_inc(s["var_ready"], 1)
                s.wait(dve, "std_ready", n + 1)
                Chain(dve, s["chain"], n * 2).do(dve.reciprocal(rs[:, :], sd[:, :]))
                s.wait(dve, "tr_done", n * KC)
                for t in range(TPB):
                    for c0, c1, at in ((0, D, 0), (D - rows(KC - 1), D, D)):
                        last = dve.tensor_scalar(xn[:, t, at:at + c1 - c0], x[:, t, c0:c1], mv[:, t, 0:1], rs[:, t:t + 1],
                                                 ALU.subtract, ALU.mult)
                last.then_inc(s["xn_ready"], 1)
                s.wait(dve, "xn_ready", n + 1)
                dve.sem_inc(s["x_used"], 1)

            def iteration(it, nxt):
                s.wait(dve, "qk_done", it * QKT)
                for c in range(KC):
                    s.wait(dve, "xm_ready", it * KC + c + 1)
                    last = dve.tensor_copy(xh[:, c, :], xm[:, c, :])
                Chain(dve, s["chain"], it * 2 + 1).do(last)
                for c in range(KC):
                    r = rows(c)
                    dve.tensor_tensor(xl[0:r, c, :], xm[0:r, c, :], xh[0:r, c, :].bitcast(F32), ALU.subtract).then_inc(s["xs_ready"], 1)
                for t in range(TPB):
                    for h in range(2):
                        s.wait(dve, "v_done", it * 2 * TPB + 2 * t + h + 1)
                        dve.tensor_tensor(
                            V[:, bass.ds((it // BPB) * H + h * (H // 2), H // 2), bass.ds((it % BPB) * TPB + t, 1), :].rearrange("p h a d -> p h (a d)"),
                            vp[h][:, 0:HALF].rearrange("p (h d) -> p h d", d=HD),
                            bvb[:, h, :].rearrange("p (h d) -> p h d", d=HD), ALU.add).then_inc(s["v_ready"], 1)
                    if nxt:
                        stats(it + 1, t)
                if nxt:
                    normalise(it + 1)
                for m in range(QKT):
                    if m:
                        e = Chain(dve, s["elim_chain"], it * ELIM + m - 1)
                        s.wait(dve, "elim_ready", it * ELIM + m - 1)
                        e.do(dve.reciprocal(piv[:, :], M[0:1, 0:1]))
                        dve.tensor_scalar(step[0:1, 0:RD - 1], M[0:1, 1:RD], piv[:, :], -1.0, ALU.mult, ALU.mult
                                          ).then_inc(s["row_ready"], 1)
                    s.wait(dve, "hi_ready", it * QKT + m + 1)
                    k, extra = m // RING, int(m % RING == (QKT // 2) % RING)
                    stores = it * (QKT // RING + extra) + k + int(extra and m > QKT // 2)
                    outs.wait(dve, f"out_lo{m % RING}", stores * 16)
                    dve.scalar_tensor_tensor(out=ol[:, m % RING, :], in0=qk[m % RING][:, :], scalar=bqk[:, m:m + 1],
                                             in1=oh[:, m % RING, :].bitcast(F32), op0=ALU.add, op1=ALU.subtract
                                             ).then_inc(s["lo_ready"], 1)
                    if m:
                        s.wait(dve, "elim_mm", it * ELIM + m)
                        dve.tensor_copy(M[:, 0:2 * ML].rearrange("p (a b) -> p a b", a=2)[:, :, 0:RD],
                                        el[0:RD, 1:1 + 2 * RD].rearrange("p (a b) -> p a b", a=2)).then_inc(s["elim_ready"], 1)

            for t in range(TPB):
                stats(0, t)
            normalise(0)
            with dve.Fori(0, NBLK - 1) as it:
                iteration(it, True)
            iteration(NBLK - 1, False)


QB = 1024
NQB = T // QB
SLOTS = NQB * KT
STK = 3 * HD
VW = 64
MAXW = 512
NMAX = KT * (T // MAXW)
MAX_FROM, MAX_PER = 5, 3
PREV_SLOT = 3
LU_SLOTS = (4, 29)
SCALE = float(HD) ** -0.5


def agenda(prev, nxt):
    plan, k = [[] for _ in range(SLOTS)], 0
    for s in range(MAX_FROM, SLOTS):
        if nxt and k < NMAX:
            plan[s] = [("max", x) for x in range(k, min(NMAX, k + MAX_PER))]
            k += MAX_PER
            row = s + 2
    if nxt:
        plan[row].append(("row", None))
    if prev:
        plan[PREV_SLOT].append(("out", 1))
    plan[O_SLOT].append(("out", 0))
    for l, s in enumerate(LU_SLOTS):
        plan[s].append(("lu", l))
    return plan


O_SLOT = KT + 3
USES = sum(len(p) for p in agenda(True, True))
SHARED = 3
assert USES % SHARED == 0


SPLITS = NH // 2
WIDTHS = {"w1": D * HID // SPLITS // P, "w2": D * HID // SPLITS // P, "wp": D * D // SPLITS // P}


def weight_part(w, i, n):
    return w.rearrange("a b -> (a b)").rearrange("(s p e) -> s p e", p=P, e=n)[bass.ds(i, 1)].rearrange("a p e -> p (a e)")


def attention(nc, io, g):
    V = g["V"]
    with ExitStack() as ctx:
        sb = lambda name, shape, dt=F32: ctx.enter_context(nc.sbuf_tensor(name, shape, dt))
        sem = lambda name: ctx.enter_context(nc.semaphore("b_" + name))
        psum = lambda name, shape: ctx.enter_context(nc.psum_tensor(name, shape, F32))
        ident = g["ident"]
        q = [sb(f"q_stack{u}", [P, T], F32R) for u in range(2)]
        k = [sb(f"k_stack{u}", [P, T], F32R) for u in range(2)]
        vst = [sb(f"v_stat{u}", [P, KT, VW]) for u in range(2)]
        pr = [sb(f"probs{i}", [P, QB]) for i in range(4)]
        mxp = sb("max_parts", [P, KT, T // MAXW])
        mx = sb("max_q", [P, KT])
        nm = sb("neg_max", [P, 2, KT])
        nmr = sb("neg_max_r", [P, 2, KT], F32R)
        nmT = sb("neg_maxT", [2 * KT, P], F32R)
        oT = [sb(f"outT{i}", [P, 512]) for i in range(NQB)]
        rc = sb("recip_sum", [P, 2, KT // NQB // 2])
        ob = [sb(f"out_tok{u}", [P, KT, HD]) for u in range(2)]
        sc = [psum(f"scoresT{i}", [P, QB]) for i in range(2)]
        shared = [psum(f"shared{i}", [P, 512]) for i in range(SHARED)]
        av = psum("av", [P, 512])
        stack_in = [sem(f"stack_in{u}") for u in range(2)]
        row_in = [sem(f"row_in{u}") for u in range(2)]
        ones_ready, sc_done, exp_done, av_done, half_done = (sem(x) for x in ("ones_ready", "sc_done", "exp_done", "av_done", "half_done"))
        use_done, use_free, nm_ready, nmT_ready, oT_ready, v_ready, v_init, ob_ready, rc_done, chain = (
            sem(x) for x in ("use_done", "use_free", "nm_ready", "nmT_ready", "oT_ready", "v_ready", "v_init", "ob_ready", "rc_done", "chain"))
        out_st = [sem(f"out_st{u}") for u in range(2)]
        WS = sum(WIDTHS.values())
        wraw, whi, wlo = sb("w_part", [P, WS]), sb("w_part_hi", [P, WS], F32R), sb("w_part_lo", [P, WS], F32R)
        w_in, whi_ready, wlo_ready, w_out = (sem(x) for x in ("w_in", "whi_ready", "wlo_ready", "w_out"))
        raw = {"w1": io["L0_cond_w_fc1"], "w2": io["L0_cond_w_fc2"], "wp": io["L0_cond_w_proj"]}
        G, M, E, step, stepT, X2, one, signs, half_mask, UT, URI = (
            g[x] for x in "G M E step stepT X2 one signs half_mask UT URI".split())
        LiT, prod, S, ST, KTm = (sb(x, [RD, RD]) for x in ("LiT", "prod", "Sinv", "SinvT", "correction"))
        dcol = sb("dcol", [RD, 4])
        U1T, U1 = sb("U1T", [RD, D]), sb("U1", [P, KC, RD])
        pivot = sb("lu_pivot", [1, 3])
        pA, pB, pC = sc[0], av, shared[SHARED - 1]
        basis_mm, basis_ready, basis_chain, d_ready, sqrt_ready, lrow_ready, lu_chain = (
            sem(x) for x in ("basis_mm", "basis_ready", "basis_chain", "d_ready", "sqrt_ready", "lrow_ready", "lu_chain"))
        lu_copied = sem("lu_copied")
        BASE = NMAX
        EXP_CREDIT, AV_CREDIT, USE_CREDIT, OT_CREDIT, OUT_CREDIT = 2, 4, SHARED, 1, 16
        block = ctx.enter_context(nc.Block())

        def bank(j):
            return shared[(BASE + j) % SHARED]

        @block.sync
        def _(sp):
            def load_stacks(n, u):
                r = bass.ds(n * HD, HD)
                for dst, parts in ((q[u], ("q_hi", "q_hi", "q_lo")), (k[u], ("k_hi", "k_lo", "k_hi"))):
                    for i, part in enumerate(parts):
                        sp.dma_start(dst[i * HD:(i + 1) * HD, :].bitcast(F32), g[part][r, :]).then_inc(stack_in[u], 16)

            def max_row(n, u):
                sp.wait_ge(nmT_ready, n + 1)
                for part in range(2):
                    sp.dma_start(q[u][STK + part:STK + part + 1, :].bitcast(F32),
                                 nmT[part * KT:(part + 1) * KT, :].bitcast(F32)).then_inc(row_in[u], 16)

            for u in range(2):
                sp.sem_inc(out_st[u], OUT_CREDIT)
            sp.sem_inc(w_out, OUT_CREDIT)
            sp.wait_ge(ones_ready, 2)
            load_stacks(0, 0)
            max_row(0, 0)

            def load_next(n, u):
                if not isinstance(n, int):
                    sp.wait_ge(sc_done, n * SLOTS)
                load_stacks(n + 1, 1 - u)

            def store(n, u):
                sp.wait_ge(ob_ready, (n + 1) * NQB)
                dst = g["attn_scratch"][bass.ds((n // H) * T, T), bass.ds((n % H) * HD, HD)].rearrange("(t p) d -> p t d", p=P)
                sp.dma_start(dst, ob[u][:, :, :]).then_inc(out_st[u], 16)

            def load_weights(i):
                if not isinstance(i, int):
                    sp.wait_ge(wlo_ready, i)
                at = 0
                for name, n in WIDTHS.items():
                    sp.dma_start(wraw[:, at:at + n], weight_part(raw[name], i, n)).then_inc(w_in, 16)
                    at += n

            def store_weights(i):
                sp.wait_ge(whi_ready, i + 1)
                sp.wait_ge(wlo_ready, i + 1)
                at = 0
                for name, n in WIDTHS.items():
                    for part, src in (("_hi", whi), ("_lo", wlo)):
                        sp.dma_start(weight_part(g[name + part], i, n), src[:, at:at + n].bitcast(F32)).then_inc(w_out, 16)
                    at += n

            load_next(0, 0)
            load_weights(0)
            max_row(1, 1)
            with sp.Fori(0, NH // 2 - 1) as i:
                for n, u in ((2 * i + 1, 1), (2 * i + 2, 0)):
                    load_next(n, u)
                    store(n - 1, 1 - u)
                    max_row(n + 1, 1 - u)
                store_weights(i)
                load_weights(i + 1)
            store_weights(SPLITS - 1)
            store(NH - 2, 0)
            store(NH - 1, 1)
            for u in range(2):
                sp.wait_ge(out_st[u], 16 * NH // 2 + OUT_CREDIT)
            sp.wait_ge(w_out, 96 * SPLITS + OUT_CREDIT)

        @block.gpsimd
        def _(pool):
            for u in range(2):
                pool.memset(vst[u][:, :, :], 0.0).then_inc(v_init, 1)
                pool.wait_ge(v_init, 2 * u + 1)
                pool.memset(vst[u][:, :, HD:HD + 1], 1.0).then_inc(v_init, 1)
            pool.wait_ge(v_init, 4)
            pool.tensor_copy(vst[0][:, :, 0:HD], V[:, 0, :, :]).then_inc(v_ready, 1)

            with pool.Fori(0, NH // 2) as i:
                for u in range(2):
                    n = 2 * i + u
                    pool.wait_ge(av_done, n * SLOTS + AV_CREDIT)
                    if u:
                        pool.wait_ge(w_in, 48 * i + 48)
                        pool.wait_ge(w_out, 96 * i + OUT_CREDIT)
                    nxt = n + 1 if u == 0 else (n + 1) % NH
                    pool.tensor_copy(vst[1 - u][:, :, 0:HD], V[:, bass.ds(nxt, 1), :, :].rearrange("p a t d -> p (a t) d")
                                     ).then_inc(v_ready, 1)
                pool.tensor_copy(whi[:, :], wraw[:, :]).then_inc(whi_ready, 1)
                pool.wait_ge(whi_ready, i + 1)
                pool.tensor_tensor(wlo[:, :], wraw[:, :], whi[:, :].bitcast(F32), ALU.subtract).then_inc(wlo_ready, 1)

        @block.scalar
        def _(act):
            act.sem_inc(exp_done, EXP_CREDIT)
            act.sem_inc(oT_ready, OT_CREDIT)
            act.wait_ge(d_ready, 1)
            act.activation(dcol[:, 1:2], dcol[:, 0:1], ACT.Sqrt).then_inc(sqrt_ready, 1)

            def evacuate(n, qb):
                act.wait_ge(av_done, n * SLOTS + (qb + 1) * KT + AV_CREDIT)
                act.activation(oT[qb][:, :], av[:, :], ACT.Copy).then_inc(oT_ready, 1)

            def head(n, prev):
                for s in range(SLOTS):
                    if s == 1 and prev:
                        evacuate(n - 1, 1)
                    if s == KT + 1:
                        evacuate(n, 0)
                    act.wait_ge(sc_done, n * SLOTS + s + 1)
                    act.wait_ge(av_done, n * SLOTS + s + 1)
                    act.activation(pr[s % 4][:, :], sc[s % 2][:, :], ACT.Exp, scale=SCALE).then_inc(exp_done, 1)

            head(0, False)
            group = 3
            with act.Fori(0, (NH - 2) // group) as i:
                for x in range(group):
                    head(group * i + x + 1, True)
            head(NH - 1, True)
            evacuate(NH - 1, 1)

        @block.tensor
        def _(pe):
            pe.sem_inc(av_done, AV_CREDIT)
            pe.transpose(pC[0:RD, 0:RD], M[:, ML:ML + RD], ident[0:RD, 0:RD]).then_inc(basis_mm, 1)
            pe.wait_ge(basis_ready, 1)
            pe.matmul(pB[0:RD, 0:RD], LiT[:, :], G[:, :], start=True, stop=True).then_inc(basis_mm, 1)
            pe.wait_ge(basis_ready, 2)
            pe.transpose(pC[0:RD, 0:RD], S[:, :], ident[0:RD, 0:RD]).then_inc(basis_mm, 1)
            pe.wait_ge(basis_ready, 3)
            for h in range(2):
                last = pe.matmul(pA[0:RD, h * 512:h * 512 + HALF], ST[:, :], UT[:, h * HALF:(h + 1) * HALF], start=True, stop=True)
            last.then_inc(basis_mm, 1)
            pe.wait_ge(basis_ready, 4)
            for c in range(KC):
                last = pe.transpose(pB[0:rows(c), c * RD:(c + 1) * RD], U1T[:, c * P:c * P + rows(c)], ident[0:RD, 0:RD])
            last.then_inc(basis_mm, 1)
            pe.wait_ge(basis_ready, 5)
            for c in range(KC):
                last = pe.matmul(pC[0:RD, 0:RD], U1[0:rows(c), c, :], U1[0:rows(c), c, :], start=(c == 0), stop=(c == KC - 1))
            last.then_inc(basis_mm, 1)
            pe.wait_ge(basis_ready, 6)
            for h in range(2):
                last = pe.matmul(pA[0:RD, h * 512:h * 512 + HALF], KTm[:, :], U1T[:, h * HALF:(h + 1) * HALF], start=True, stop=True)
            last.then_inc(basis_mm, 1)
            pe.wait_ge(basis_ready, 7)
            pe.transpose(pB[0:RD, 0:RD], UT[:, 0:RD], ident[0:RD, 0:RD]).then_inc(basis_mm, 1)

            def scores(n, u, s):
                pe.wait_ge(exp_done, n * SLOTS + s - 1 + EXP_CREDIT)
                qb, m = s // KT, s % KT
                for x in range(2):
                    last = pe.matmul(sc[s % 2][:, x * 512:(x + 1) * 512], k[u][0:STK + 2, m * P:(m + 1) * P],
                                     q[u][0:STK + 2, qb * QB + x * 512:qb * QB + (x + 1) * 512], start=True, stop=True)
                last.then_inc(sc_done, 1)

            def one_max(u, kk, use, bk):
                pe.wait_ge(use_free, use + 1)
                qt, kc = kk // (T // MAXW), kk % (T // MAXW)
                pe.matmul(bk[:, :], q[u][0:STK, qt * P:(qt + 1) * P],
                          k[u][0:STK, kc * MAXW:(kc + 1) * MAXW], start=True, stop=True).then_inc(use_done, 1)

            def max_row(n, use, bk):
                pe.wait_ge(nm_ready, n + 1)
                pe.wait_ge(use_free, use + 1)
                pe.transpose(bk[0:2 * KT, 0:P], nm[:, :, :].rearrange("p a t -> p (a t)"), ident[:, :]).then_inc(use_done, 1)

            def out_half(n, qb, use, bk):
                pe.wait_ge(oT_ready, n * NQB + qb + 1 + OT_CREDIT)
                pe.wait_ge(use_free, use + 1)
                for t in range(4):
                    last = pe.transpose(bk[:, t * P:(t + 1) * P], oT[qb][:, t * P:(t + 1) * P], ident[:, :])
                last.then_inc(use_done, 1)

            def lu_step(i, use, bk):
                pe.wait_ge(lrow_ready, i + 1)
                pe.wait_ge(use_free, use + 1)
                pe.matmul(bk[:, 0:ML], step[:, :], X2[:, 0, :], start=True, stop=True)
                pe.matmul(bk[:, 256:256 + ML], stepT[:, :], X2[:, 1, :], start=True, stop=True).then_inc(use_done, 1)

            pe.wait_ge(stack_in[0], 96)
            for kk in range(NMAX):
                one_max(0, kk, kk, shared[kk % SHARED])
            max_row(0, NMAX, shared[NMAX % SHARED])
            pe.wait_ge(row_in[0], 32)
            pe.wait_ge(lrow_ready, 1)
            scores(0, 0, 0)

            def head(n, u, nth, prev, nxt):
                plan = agenda(prev, nxt)
                base = BASE + n * USES
                j = 0 if prev else 1
                pe.wait_ge(v_ready, n + 1)
                for s in range(SLOTS):
                    def use(kind, x):
                        nonlocal j
                        at, bk = base + j, bank(j)
                        j += 1
                        if kind == "max":
                            if x == 0:
                                pe.wait_ge(stack_in[1 - u], 96 * (nth + 1))
                            one_max(1 - u, x, at, bk)
                        elif kind == "row":
                            max_row(n + 1, at, bk)
                        elif kind == "out":
                            out_half(n - x, x, at, bk)
                        else:
                            lu_step(n * len(LU_SLOTS) + x, at, bk)

                    for item in plan[s][0:1]:
                        use(*item)
                    if s + 1 < SLOTS:
                        scores(n, u, s + 1)
                    elif nxt:
                        pe.wait_ge(row_in[1 - u], 32 * (nth + 1))
                        scores(n + 1, 1 - u, 0)
                    for item in plan[s][1:2]:
                        use(*item)
                    qb, m = s // KT, s % KT
                    if m == 0:
                        pe.wait_ge(oT_ready, n * NQB + qb + OT_CREDIT)
                    pe.wait_ge(exp_done, n * SLOTS + s + 1 + EXP_CREDIT)
                    for x in range(2):
                        last = pe.matmul(av[x * VW:(x + 1) * VW, :], vst[u][:, m, :], pr[s % 4][:, x * 512:(x + 1) * 512],
                                         start=(m == 0), stop=(m == KT - 1))
                    last.then_inc(av_done, 1)
                    for item in plan[s][2:]:
                        use(*item)
                return base + j, bank(j)

            head(0, 0, 0, False, True)
            with pe.Fori(0, NH // 2 - 1) as i:
                head(2 * i + 1, 1, i + 1, True, True)
                head(2 * i + 2, 0, i + 1, True, True)
            at, bk = head(NH - 1, 1, None, True, False)
            out_half(NH - 1, 1, at, bk)
            pe.wait_ge(lrow_ready, RD + 1)
            pe.wait_ge(basis_ready, 8)
            pe.matmul(sc[0][0:RD, 0:1], signs[0:1, 0:RD], one[0:1, 0:1], start=True, stop=True).then_inc(basis_mm, 1)
            pe.wait_ge(basis_ready, 9)
            for b in range(B):
                for c in range(KC):
                    last = pe.matmul(sc[1][0:rows(c), b * 512 + c * RD:b * 512 + (c + 1) * RD], UT[:, c * P:c * P + rows(c)],
                                     E[:, 0, b, :], start=True, stop=True)
            last.then_inc(basis_mm, 1)

        @block.vector
        def _(dve):
            for u in range(2):
                dve.memset(k[u][96:STK + 2, :].bitcast(F32), 1.0).then_inc(ones_ready, 1)
            dve.sem_inc(use_free, USE_CREDIT)
            ch = Chain(dve, basis_chain)
            right = M[:, ML:ML + RD]
            dve.wait_ge(basis_mm, 1)
            dve.tensor_copy(LiT[:, :], pC[0:RD, 0:RD]).then_inc(basis_ready, 1)
            dve.wait_ge(basis_mm, 2)
            ch.do(dve.tensor_tensor(prod[:, :], pB[0:RD, 0:RD], right, ALU.mult))
            dve.tensor_reduce(dcol[:, 0:1], prod[:, :], op=ALU.add, axis=AX.X).then_inc(d_ready, 1)
            dve.wait_ge(sqrt_ready, 1)
            ch.do(dve.reciprocal(dcol[:, 2:3], dcol[:, 1:2]))
            dve.tensor_scalar(S[:, :], right, dcol[:, 2:3], None, ALU.mult).then_inc(basis_ready, 1)
            dve.wait_ge(basis_mm, 3)
            dve.tensor_copy(ST[:, :], pC[0:RD, 0:RD]).then_inc(basis_ready, 1)
            halves = pA[0:RD, :].rearrange("p (a b) -> p a b", a=2)[:, :, 0:HALF]
            dve.wait_ge(basis_mm, 4)
            dve.tensor_copy(U1T[:, :].rearrange("p (a b) -> p a b", a=2), halves).then_inc(basis_ready, 1)
            dve.wait_ge(basis_mm, 5)
            ch.do(dve.tensor_copy(U1[:, 0:KC - 1, :].rearrange("p a b -> p (a b)"), pB[:, 0:(KC - 1) * RD]))
            dve.tensor_copy(U1[0:rows(KC - 1), KC - 1, :], pB[0:rows(KC - 1), (KC - 1) * RD:KC * RD]).then_inc(basis_ready, 1)
            dve.wait_ge(basis_mm, 6)
            ch.do(dve.tensor_tensor(prod[:, :], pC[0:RD, 0:RD], ident[0:RD, 0:RD], ALU.subtract))
            ch.do(dve.tensor_tensor(KTm[:, :], prod[:, :], half_mask[:, :], ALU.mult))
            dve.tensor_tensor(KTm[:, :], ident[0:RD, 0:RD], KTm[:, :], ALU.subtract).then_inc(basis_ready, 1)
            dve.wait_ge(basis_mm, 7)
            dve.tensor_copy(UT[:, 0:D].rearrange("p (a b) -> p a b", a=2), halves).then_inc(basis_ready, 1)
            dve.wait_ge(basis_mm, 8)
            ch.do(dve.tensor_copy(X2[:, 0, 0:RD], pB[0:RD, 0:RD]))
            ch.do(dve.memset(step[0:1, RD - 1:RD], 0.0))
            dve.wait_ge(basis_ready, 7)
            ch.do(dve.tensor_copy(X2[:, 1, 0:RD], UT[:, 0:RD]))

            def lu_rows(i):
                c = Chain(dve, lu_chain, i * 5)
                c.do(dve.tensor_scalar(pivot[:, 0:1], X2[0:1, 0, 0:1], 0.0, 2.0, ALU.is_ge, ALU.mult))
                c.do(dve.tensor_scalar(signs[0:1, bass.ds(i, 1)], pivot[:, 0:1], -1.0, None, ALU.add))
                c.do(dve.scalar_tensor_tensor(out=pivot[:, 1:2], in0=pivot[:, 0:1], scalar=-1.0, in1=X2[0:1, 0, 0:1],
                                              op0=ALU.add, op1=ALU.add))
                c.do(dve.reciprocal(pivot[:, 2:3], pivot[:, 1:2]))
                c.do(dve.tensor_scalar(stepT[0:1, 0:RD - 1], X2[0:1, 0, 1:RD], pivot[:, 2:3], -1.0, ALU.mult, ALU.mult))
                dve.tensor_scalar(step[0:1, 0:RD - 1], X2[0:1, 1, 1:RD], pivot[:, 2:3], -1.0, ALU.mult, ALU.mult).then_inc(lrow_ready, 1)

            def lu_step(i, use, bk):
                dve.wait_ge(use_done, use + 1)
                dve.tensor_copy(X2[:, :, 0:RD], bk[0:RD, :].rearrange("p (a b) -> p a b", a=2)[:, :, 1:ML]).then_inc(lu_copied, 1)
                dve.wait_ge(lu_copied, i + 1)
                dve.sem_inc(use_free, 1)
                lu_rows(i + 1)

            lu_rows(0)

            def one_max(kk, use, bk):
                dve.wait_ge(use_done, use + 1)
                qt, kc = kk // (T // MAXW), kk % (T // MAXW)
                dve.tensor_reduce(mxp[:, qt, kc:kc + 1], bk[:, :], op=ALU.max, axis=AX.X).then_inc(use_free, 1)

            def neg_max(n, uses):
                dve.wait_ge(use_free, uses + USE_CREDIT)
                c = Chain(dve, chain, 3 * n)
                c.do(dve.tensor_reduce(mx[:, :], mxp[:, :, :], op=ALU.max, axis=AX.X))
                c.do(dve.tensor_scalar(nmr[:, 0, :], mx[:, :], -1.0, None, ALU.mult))
                c.do(dve.scalar_tensor_tensor(out=nmr[:, 1, :], in0=mx[:, :], scalar=-1.0, in1=nmr[:, 0, :].bitcast(F32),
                                              op0=ALU.mult, op1=ALU.subtract))
                dve.tensor_copy(nm[:, :, :], nmr[:, :, :].bitcast(F32)).then_inc(nm_ready, 1)

            def row_copy(n, use, bk):
                dve.wait_ge(use_done, use + 1)
                dve.tensor_copy(nmT[:, :], bk[0:2 * KT, 0:P]).then_inc(nmT_ready, 1)
                dve.wait_ge(nmT_ready, n + 1)
                dve.sem_inc(use_free, 1)

            for kk in range(NMAX):
                one_max(kk, kk, shared[kk % SHARED])
            neg_max(0, NMAX)
            row_copy(0, NMAX, shared[NMAX % SHARED])

            def normalise(n, u, nth, qb, use, bk):
                dve.wait_ge(use_done, use + 1)
                ps = bk[:, :].rearrange("p (t x c) -> p x t c", x=2, c=VW)
                dve.reciprocal(rc[:, :, :], ps[:, :, :, HD]).then_inc(rc_done, 1)
                dve.wait_ge(rc_done, n * NQB + qb + 1)
                if qb == 0:
                    dve.wait_ge(out_st[u], 16 * nth + OUT_CREDIT)
                o = ob[u][:, qb * 8:(qb + 1) * 8, :].rearrange("p (x t) d -> p x t d", x=2)
                for x in range(2):
                    last = dve.tensor_tensor(o[:, x], ps[:, x, :, 0:HD],
                                             rc[:, x, :].rearrange("p (t a) -> p t a", a=1).broadcast_to([P, 4, HD]), ALU.mult)
                last.then_inc(ob_ready, 1)
                dve.wait_ge(ob_ready, n * NQB + qb + 1)
                dve.sem_inc(use_free, 1)

            def head(n, u, nth, row_nth, prev, nxt):
                base = BASE + n * USES
                j = 0 if prev else 1
                for items in agenda(prev, nxt):
                    for kind, x in items:
                        at, bk = base + j, bank(j)
                        j += 1
                        if kind == "max":
                            one_max(x, at, bk)
                            if x == NMAX - 1:
                                neg_max(n + 1, base + j)
                        elif kind == "row":
                            dve.wait_ge(row_in[u], 32 * row_nth)
                            row_copy(n + 1, at, bk)
                        elif kind == "out":
                            normalise(n - x, u ^ x, None if x else nth, x, at, bk)
                        else:
                            lu_step(n * len(LU_SLOTS) + x, at, bk)
                return base + j, bank(j)

            head(0, 0, 0, 1, False, True)
            with dve.Fori(0, NH // 2 - 1) as i:
                head(2 * i + 1, 1, i, i + 1, True, True)
                head(2 * i + 2, 0, i + 1, i + 2, True, True)
            at, bk = head(NH - 1, 1, NH // 2 - 1, None, True, False)
            normalise(NH - 1, 1, None, 1, at, bk)
            dve.wait_ge(lu_chain, 5 * (RD + 1))
            dve.sem_inc(basis_ready, 1)
            dve.wait_ge(basis_mm, 9)
            ch.do(dve.tensor_copy(dcol[:, 3:4], sc[0][0:RD, 0:1]))
            dve.tensor_scalar(UT[:, 0:D], UT[:, 0:D], dcol[:, 3:4], -1.0, ALU.mult, ALU.mult).then_inc(basis_ready, 1)
            dve.wait_ge(basis_mm, 10)
            for b in range(B):
                full, r = (KC - 1) * RD, rows(KC - 1)
                dve.memset(URI[r:P, b, KC - 1, :], 0.0)
                dve.tensor_copy(URI[:, b, 0:KC - 1, :].rearrange("p a b -> p (a b)"), sc[1][:, b * 512:b * 512 + full])
                dve.tensor_copy(URI[0:r, b, KC - 1, :], sc[1][0:r, b * 512 + full:b * 512 + full + RD])


def load_parts(eng, dst_hi, dst_lo, hi, lo, sem):
    full = (KC - 1) * P
    eng.dma_start(dst_hi[:, 0:KC - 1, :].bitcast(F32), hi[0:full, :].rearrange("(c p) n -> p c n", p=P)).then_inc(sem, 16)
    eng.dma_start(dst_hi[0:RD, KC - 1, :].bitcast(F32), hi[full:D, :]).then_inc(sem, 16)
    eng.dma_start(dst_hi[RD:P, KC - 1, :].bitcast(F32), lo[full:D, :]).then_inc(sem, 16)
    if dst_lo is not None:
        eng.dma_start(dst_lo[:, :, :].bitcast(F32), lo[0:full, :].rearrange("(c p) n -> p c n", p=P)).then_inc(sem, 16)


def split_passes(w_hi, w_lo, x_hi, x_lo):
    passes = []
    for c in range(KC - 1):
        passes += [(w_hi(c, P), x_hi(c, P)), (w_hi(c, P), x_lo(c, P)), (w_lo(c, P), x_hi(c, P))]
    c = KC - 1
    return passes + [(w_hi(c, P), x_hi(c, P)), (w_hi(c, rows(c)), x_lo(c, rows(c)))]


def projection(nc, io, g):
    HR = 3
    with ExitStack() as ctx:
        sb = lambda name, shape, dt=F32: ctx.enter_context(nc.sbuf_tensor(name, shape, dt))
        sem = lambda name: ctx.enter_context(nc.semaphore("c_" + name))
        psum = lambda name, shape: ctx.enter_context(nc.psum_tensor(name, shape, F32))
        ident, modv, w1h = g["ident"], g["modv"], g["w1h"]
        wph = sb("wp_hi", [P, KC, D], F32R)
        wpl = sb("wp_lo", [P, KC - 1, D], F32R)
        oi = sb("attn_tok", [P, TPB, KC * P])
        oh = sb("attnT_hi", [P, KC, BLK], F32R)
        ol = sb("attnT_lo", [P, KC, BLK], F32R)
        pT = sb("projT", [P, KC, BLK])
        xr = sb("x_resid", [P, TPB, D])
        xn = sb("x_norm_c", [P, TPB, D])
        xm = sb("x_modT_c", [P, KC, BLK])
        xh = sb("x_modT_hi_c", [P, KC, BLK], F32R)
        xl = sb("x_modT_lo_c", [P, KC, BLK], F32R)
        x2 = sb("x2T_out", [P, KC, BLK])
        bp, b2 = sb("b_proj", [P, KC]), sb("b_fc2", [P, KC])
        gb = sb("gated_bias", [P, B, 2, KC])
        eps = sb("eps_c", [P, 1])
        st, mv = sb("st_c", [P, TPB, 2, 6]), sb("mv_c", [P, TPB, 2])
        sd, rs = sb("sd_c", [P, TPB]), sb("rs_c", [P, TPB])
        hp = [psum(f"proj_ps{i}", [P, BLK]) for i in range(HR)]
        tp = [psum(f"trans_ps{i}", [P, BLK]) for i in range(KC)]
        names = ("w1_in wp_in bias_in bias_ready o_in x_in o_tr o_hi o_lo p_done p_ready b_done x2_ready r_tr r_ready "
                 "st_ready var_ready std_ready xn_ready n_tr xm_ready hi_ready xs_ready chain")
        s = Counts(sem, names.split(), ("r_ready", "p_ready", "xm_ready", "n_tr", "xs_ready", "p_done"))
        outs = Counts(sem, ["out_s", "out_r"], ["out_s", "out_r"], credit=16)
        xv = io["x"].rearrange("b (k t p) d -> (b k) p t d", p=P, t=TPB)
        av = g["attn_scratch"].rearrange("(k t p) d -> k p t d", p=P, t=TPB)
        full, tail = KC - 1, rows(KC - 1)
        block = ctx.enter_context(nc.Block())

        def columns(tile, it, k):
            return lambda c, r: tile[0:r, bass.ds(it // BPB, 1), k, c:c + 1].rearrange("p a b -> p (a b)")

        @block.sync
        def _(sp):
            def load_attention(it):
                src = av[bass.ds(it, 1)].rearrange("a p t d -> p (a t) d")
                sp.dma_start(oi[:, :, 0:D], src).then_inc(s["o_in"], 16)
                sp.dma_start(oi[:, :, D:KC * P], src[:, :, full * P:D]).then_inc(s["o_in"], 16)

            def load_x(it):
                sp.dma_start(xr[:, :, :], xv[bass.ds(it, 1)].rearrange("a p t d -> p (a t) d")).then_inc(s["x_in"], 16)

            def store_feature_major(name, it, src, done):
                dst = g[name][bass.ds(it, 1)].rearrange("a p c n -> p (a c) n")
                sp.dma_start(dst[:, 0:full, :], src[:, 0:full, :]).then_inc(outs[done], 16)
                sp.dma_start(dst[0:tail, full, :], src[0:tail, full, :]).then_inc(outs[done], 16)
                return dst

            def store_split(it):
                s.wait(sp, "xs_ready", it * KC + KC)
                dst = store_feature_major("xs_hi", it, xh[:, :, :].bitcast(F32), "out_s")
                sp.dma_start(dst[tail:P, full, :], xh[0:tail, full, :].bitcast(F32)).then_inc(outs["out_s"], 16)
                store_feature_major("xs_lo", it, xl[:, :, :].bitcast(F32), "out_s")

            outs.give(sp, *outs.sems)
            load_attention(0)
            load_parts(sp, wph, wpl, g["wp_hi"], g["wp_lo"], s["wp_in"])
            load_columns(sp, bp[:, :], io["L0_cond_b_proj"], s["bias_in"])
            load_columns(sp, b2[:, :], io["L0_cond_b_fc2"], s["bias_in"])
            load_x(0)
            load_parts(sp, w1h, None, g["w1_hi"], g["w1_lo"], s["w1_in"])

            def iteration(it, prev, nxt):
                if prev:
                    s.wait(sp, "r_tr", it * KC)
                    s.wait(sp, "xn_ready", it)
                    load_x(it)
                if nxt:
                    s.wait(sp, "o_tr", it * KC + KC)
                    load_attention(it + 1)
                if prev:
                    store_split(it - 1)
                s.wait(sp, "r_ready", it * KC + KC)
                store_feature_major("x2T", it, x2, "out_r")

            iteration(0, False, True)
            with sp.Fori(0, NBLK - 2) as i:
                iteration(i + 1, True, True)
            iteration(NBLK - 1, True, False)
            store_split(NBLK - 1)
            outs.wait(sp, "out_s", 80 * NBLK)
            outs.wait(sp, "out_r", 32 * NBLK)
            s.wait(sp, "w1_in", 48)

        @block.scalar
        def _(act):
            s.give(act, "p_ready", "xm_ready", "r_ready")

            def attention_hi(it):
                for c in range(KC):
                    if c == 0:
                        s.wait(act, "p_done", it * KC)
                    s.wait(act, "o_tr", it * KC + c + 1)
                    act.activation(oh[:, c, :], tp[c][:, :], ACT.Copy).then_inc(s["o_hi"], 1)

            attention_hi(0)
            s.wait(act, "bias_ready", 1)

            def gated(it, m):
                r = rows(m)
                s.wait(act, "p_done", it * KC + m + 1)
                act.activation(pT[0:r, m, :], hp[m % HR][0:r, :], ACT.Identity, bias=columns(gb, it, 0)(m, r),
                               scale=columns(modv, it, GATE_A)(m, r)).then_inc(s["p_ready"], 1)

            def modulate(it):
                s.wait(act, "xs_ready", it * KC)
                for c in range(KC):
                    r = rows(c)
                    s.wait(act, "n_tr", it * KC + c + 1)
                    act.activation(xm[0:r, c, :], tp[c][0:r, :], ACT.Identity, bias=columns(modv, it, SHIFT_F)(c, r),
                                   scale=columns(modv, it, SCALE_F)(c, r)).then_inc(s["xm_ready"], 1)

            def iteration(it, prev, nxt):
                for m in range(KC):
                    if m == SPLIT_AT and prev:
                        modulate(it - 1)
                    gated(it, m)
                if nxt:
                    attention_hi(it + 1)
                outs.wait(act, "out_r", it * 32)
                for c in range(KC):
                    r = rows(c)
                    s.wait(act, "r_tr", it * KC + c + 1)
                    act.activation(x2[0:r, c, :], tp[c][0:r, :], ACT.Identity, bias=columns(gb, it, 1)(c, r)
                                   ).then_inc(s["r_ready"], 1)
                s.wait(act, "var_ready", it + 1)
                act.activation(sd[:, :], mv[:, :, 1], ACT.Sqrt, bias=eps[:, :]).then_inc(s["std_ready"], 1)

            iteration(0, False, True)
            with act.Fori(0, NBLK - 2) as i:
                iteration(i + 1, True, True)
            iteration(NBLK - 1, True, False)
            modulate(NBLK - 1)

        @block.tensor
        def _(pe):
            s.give(pe, "n_tr", "p_done")

            def transposes(src, c, r, done):
                for t in range(TPB):
                    last = pe.transpose(tp[c][0:r, t * P:(t + 1) * P], src[:, t, c * P:c * P + r], ident[:, :])
                last.then_inc(s[done], 1)

            def attention_transposes(it):
                s.wait(pe, "o_in", 32 * it + 32)
                for c in range(KC):
                    s.wait(pe, "xm_ready", (it - 2) * KC + c + 1)
                    transposes(oi, c, P, "o_tr")

            def norm_transposes(it):
                s.wait(pe, "xn_ready", it + 1)
                for c in range(KC):
                    if c < full:
                        s.wait(pe, "r_ready", it * KC + (c + 1 if c < full - 1 else KC))
                    transposes(xn, c, rows(c), "n_tr")

            def first_transposes(it):
                s.wait(pe, "o_in", 32 * it + 32)
                for c in range(KC):
                    transposes(oi, c, P, "o_tr")

            first_transposes(0)
            s.wait(pe, "wp_in", 64)

            def iteration(it, prev, nxt):
                s.wait(pe, "o_lo", it * KC + KC)
                for m in range(KC):
                    if m == SPLIT_AT and prev:
                        norm_transposes(it - 1)
                    r = rows(m)
                    s.wait(pe, "p_ready", it * KC + max(0, m - HR + 1) if m >= HR or not prev else it * KC)
                    cols = slice(m * P, m * P + r)
                    passes = split_passes(lambda c, k: wph[0:k, c, cols], lambda c, k: wpl[0:k, c, cols],
                                          lambda c, k: oh[0:k, c, :], lambda c, k: ol[0:k, c, :])
                    for n, (w, xx) in enumerate(passes):
                        last = pe.matmul(hp[m % HR][0:r, :], w, xx, start=(n == 0), stop=(n == len(passes) - 1))
                    last.then_inc(s["p_done"], 1)
                if nxt:
                    if prev:
                        attention_transposes(it + 1)
                    else:
                        first_transposes(it + 1)
                s.wait(pe, "p_ready", it * KC + KC)
                for t in range(TPB):
                    if nxt:
                        s.wait(pe, "o_lo", it * KC + KC + t + 1)
                    else:
                        s.wait(pe, "xm_ready", it * KC - KC + t + 1)
                    for c in range(full):
                        last = pe.transpose(tp[t][:, c * P:(c + 1) * P], pT[:, c, t * P:(t + 1) * P], ident[:, :])
                    last.then_inc(s["b_done"], 1)
                if nxt:
                    s.wait(pe, "o_lo", it * KC + 2 * KC)
                else:
                    s.wait(pe, "xm_ready", it * KC)
                for t in range(TPB):
                    last = pe.transpose(tp[full][:, t * P:(t + 1) * P], pT[:, full, t * P:(t + 1) * P], ident[:, :])
                last.then_inc(s["b_done"], 1)
                s.wait(pe, "x2_ready", it * KC + KC)
                for c in range(KC):
                    transposes(xr, c, rows(c), "r_tr")

            iteration(0, False, True)
            with pe.Fori(0, NBLK - 2) as i:
                iteration(i + 1, True, True)
            iteration(NBLK - 1, True, False)
            norm_transposes(NBLK - 1)

        @block.vector
        def _(dve):
            s.give(dve, "xs_ready")
            dve.memset(eps[:, :], LN_EPS)
            dve.memset(pT[tail:P, full, :], 0.0)

            def attention_lo(it):
                for c in range(KC):
                    r = rows(c)
                    s.wait(dve, "o_hi", it * KC + c + 1)
                    dve.tensor_tensor(ol[0:r, c, :], tp[c][0:r, :], oh[0:r, c, :].bitcast(F32), ALU.subtract).then_inc(s["o_lo"], 1)

            s.wait(dve, "bias_in", 64)
            for r, c0, c1 in ((P, 0, full), (tail, full, KC)):
                for b in range(B):
                    for k, (sec, bias) in enumerate(((GATE_A, bp), (GATE_F, b2))):
                        last = dve.tensor_tensor(gb[0:r, b, k, c0:c1], modv[0:r, b, sec, c0:c1], bias[0:r, c0:c1], ALU.mult)
            last.then_inc(s["bias_ready"], 1)
            attention_lo(0)

            def normalise(it):
                ch = Chain(dve, s["chain"], it * 2)
                s.wait(dve, "std_ready", it + 1)
                ch.do(dve.reciprocal(rs[:, :], sd[:, :]))
                s.wait(dve, "n_tr", it * KC)
                for t in range(TPB):
                    last = dve.tensor_scalar(xn[:, t, :], xr[:, t, :], mv[:, t, 0:1], rs[:, t:t + 1], ALU.subtract, ALU.mult)
                last.then_inc(s["xn_ready"], 1)
                outs.wait(dve, "out_s", it * 80)
                for c in range(KC):
                    r = rows(c)
                    s.wait(dve, "xm_ready", it * KC + c + 1)
                    last = dve.tensor_copy(xh[0:r, c, :], xm[0:r, c, :])
                ch.do(last)
                for c in range(KC):
                    r = rows(c)
                    dve.tensor_tensor(xl[0:r, c, :], xm[0:r, c, :], xh[0:r, c, :].bitcast(F32), ALU.subtract).then_inc(s["xs_ready"], 1)

            def iteration(it, prev, nxt):
                if prev:
                    normalise(it - 1)
                if nxt:
                    attention_lo(it + 1)
                s.wait(dve, "x_in", it * 16 + 16)
                for t in range(TPB):
                    s.wait(dve, "b_done", it * KC + t + 1)
                    dve.tensor_tensor(xr[:, t, 0:full * P], tp[t][:, :], xr[:, t, 0:full * P], ALU.add).then_inc(s["x2_ready"], 1)
                s.wait(dve, "b_done", it * KC + KC)
                dve.tensor_tensor(xr[:, :, full * P:D], tp[full][:, :].rearrange("p (t c) -> p t c", t=TPB)[:, :, 0:tail],
                                  xr[:, :, full * P:D], ALU.add).then_inc(s["x2_ready"], 1)
                s.wait(dve, "x2_ready", it * KC + KC)
                for t in range(TPB):
                    for h in range(2):
                        last = dve.bn_stats(st[:, t, h, :], xr[:, t, h * HALF:(h + 1) * HALF])
                last.then_inc(s["st_ready"], 1)
                dve.drain()
                for t in range(TPB):
                    last = dve.bn_aggr(mv[:, t, :], st[:, t, :, :].rearrange("p a b -> p (a b)"))
                last.then_inc(s["var_ready"], 1)

            iteration(0, False, True)
            with dve.Fori(0, NBLK - 2) as i:
                iteration(i + 1, True, True)
            iteration(NBLK - 1, True, False)
            normalise(NBLK - 1)


SPLIT_AT = 3


def mlp(nc, io, g, out):
    HR, WR = 2, 3
    W1P = 3
    ROT_AT, ADD_AT, OUT_AT = 1, 3, 9
    with ExitStack() as ctx:
        sb = lambda name, shape, dt=F32: ctx.enter_context(nc.sbuf_tensor(name, shape, dt))
        sem = lambda name: ctx.enter_context(nc.semaphore("d_" + name))
        psum = lambda name, shape: ctx.enter_context(nc.psum_tensor(name, shape, F32))
        ident, modv, UT, URI, w1h = g["ident"], g["modv"], g["UT"], g["URI"], g["w1h"]
        w1l = sb("w1_lo", [P, KC - 1, HID], F32R)
        w2 = sb("w2_ring", [P, WR, 2 * D], F32R)
        fold = sb("fold", [P, RD])
        tail_sum = sb("tail_sum", [P, BLK])
        xh = sb("mlp_x_hi", [P, 2, KC, BLK], F32R)
        xl = sb("mlp_x_lo", [P, 2, KC, BLK], F32R)
        x3 = sb("residT", [P, 2, KC, BLK])
        oT = sb("outT", [P, KC, BLK])
        hb = sb("hid", [P, 2, BLK])
        hh = sb("hid_hi", [P, 2, BLK], F32R)
        hl = sb("hid_lo", [P, 2, BLK], F32R)
        xo = sb("out_tok", [P, TPB, D])
        wT = sb("rotT", [RD, BLK])
        uri = sb("URI_cur", [P, KC, RD])
        gate = sb("gate_cur", [P, KC])
        b1 = sb("b_fc1", [P, FT])
        acc = psum("acc", [P, KC, 512])
        hp = [psum(f"hid_ps{i}", [P, BLK]) for i in range(HR)]
        side = psum("side_ps", [P, BLK])
        names = ("copy_ready fold_done b1_in x_in x2_in h_done g_ready hh_ready hs_ready y_done x3_ready cur_ready w_done wT_ready "
                 "r_done o_ready t_done xo_ready")
        s = Counts(sem, names.split(), ("g_ready", "hs_ready", "y_done", "w_done", "xo_ready"))
        st_out = Counts(sem, ["out_st"], ["out_st"], credit=16)
        w2_in = [sem(f"w2_in{i}") for i in range(WR)]
        w1_in = [sem(f"w1_in{i}") for i in range(FT // W1P)]
        ov = out.rearrange("b (k t p) d -> (b k) p t d", p=P, t=TPB)
        full, tail = KC - 1, rows(KC - 1)
        block = ctx.enter_context(nc.Block())

        def slot(tile, n, c, r):
            return tile[0:r, bass.ds(n % 2, 1), c, :].rearrange("p a n -> p (a n)")

        @block.sync
        def _(sp):
            def load_block(n):
                dst = lambda tile: tile[:, bass.ds(n % 2, 1), :, :].rearrange("p a c n -> p (a c) n")
                src = lambda name: g[name][bass.ds(n, 1)].rearrange("a p c n -> p (a c) n")
                sp.dma_start(dst(xh).bitcast(F32), src("xs_hi")).then_inc(s["x_in"], 16)
                sp.dma_start(dst(xl)[:, 0:full, :].bitcast(F32), src("xs_lo")[:, 0:full, :]).then_inc(s["x_in"], 16)
                sp.dma_start(dst(xl)[0:tail, full:KC, :].bitcast(F32), src("xs_lo")[0:tail, full:KC, :]).then_inc(s["x_in"], 16)

            def load_residual(n):
                dst = x3[:, bass.ds(n % 2, 1), :, :].rearrange("p a c n -> p (a c) n")
                src = g["x2T"][bass.ds(n, 1)].rearrange("a p c n -> p (a c) n")
                sp.dma_start(dst[:, 0:full, :], src[:, 0:full, :]).then_inc(s["x2_in"], 16)
                sp.dma_start(dst[0:tail, full:KC, :], src[0:tail, full:KC, :]).then_inc(s["x2_in"], 16)

            def load_w1(k):
                cols = slice(k * W1P * P, (k + 1) * W1P * P)
                sp.dma_start(w1l[:, :, cols].bitcast(F32), g["w1_lo"][0:full * P, cols].rearrange("(c p) n -> p c n", p=P)
                             ).then_inc(w1_in[k], 16)

            sp.dma_start(b1[:, :], io["L0_cond_b_fc1"].rearrange("(f p) -> p f", p=P)).then_inc(s["b1_in"], 16)
            load_w1(0)
            load_block(0)
            st_out.give(sp, "out_st")

            def store(n):
                s.wait(sp, "xo_ready", n * KC + KC)
                sp.dma_start(ov[bass.ds(n, 1)].rearrange("a p t d -> p (a t) d"), xo[:, :, :]).then_inc(st_out["out_st"], 16)

            def stage(n, prev, nxt):
                for f in range(FT):
                    s.wait(sp, "y_done", n * FT + max(0, f - WR + 1))
                    for name, c0, c1, at in (("w2_hi", 0, D, 0), ("w2_lo", full * P, D, D), ("w2_lo", 0, full * P, D + tail)):
                        sp.dma_start(w2[:, f % WR, at:at + c1 - c0].bitcast(F32), g[name][f * P:(f + 1) * P, c0:c1]
                                     ).then_inc(w2_in[f % WR], 16)
                    if not prev:
                        if f % 2 == 0 and f // 2 + 1 < FT // W1P:
                            load_w1(f // 2 + 1)
                        if f == WR:
                            load_residual(0)
                    if f == OUT_AT + KC - 1 and nxt:
                        if prev:
                            s.wait(sp, "o_ready", n * KC)
                        s.wait(sp, "x2_in", n * 32 + 32)
                        s.wait(sp, "h_done", n * FT + 1)
                        load_block(n + 1)
                        load_residual(n + 1)
                if prev:
                    store(n - 1)

            stage(0, False, True)
            with sp.Fori(0, NBLK - 2) as i:
                stage(i + 1, True, True)
            stage(NBLK - 1, True, False)
            store(NBLK - 1)
            st_out.wait(sp, "out_st", 16 * NBLK)

        @block.gpsimd
        def _(pool):
            with pool.Fori(0, NBLK) as n:
                s.wait(pool, "w_done", n)
                pool.tensor_copy(gate[:, 0:full], modv[:, bass.ds(n // BPB, 1), GATE_F, 0:full].rearrange("p a c -> p (a c)"))
                pool.tensor_copy(gate[0:tail, full:KC], modv[0:tail, bass.ds(n // BPB, 1), GATE_F, full:KC].rearrange("p a c -> p (a c)"))
                pool.tensor_copy(uri[:, :, :], URI[:, bass.ds(n // BPB, 1), :, :].rearrange("p a c d -> p (a c) d")
                                 ).then_inc(s["cur_ready"], 1)

        @block.scalar
        def _(act):
            s.give(act, "xo_ready", "g_ready")
            s.wait(act, "b1_in", 16)

            def gelu(n, f):
                s.wait(act, "h_done", n * FT + f + 1)
                if f or not isinstance(n, int):
                    s.wait(act, "hs_ready", n * FT + f - 1)
                act.activation(hb[:, f % 2, :], hp[f % HR][:, :], ACT.Gelu_apprx_tanh, bias=b1[:, f:f + 1]).then_inc(s["g_ready"], 1)

            def rear(r, f):
                if f == ROT_AT:
                    s.wait(act, "w_done", r + 1)
                    act.activation(wT[:, :], side[0:RD, :], ACT.Copy).then_inc(s["wT_ready"], 1)
                if f == OUT_AT:
                    st_out.wait(act, "out_st", 16 * r)
                if OUT_AT <= f < OUT_AT + full:
                    t = f - OUT_AT
                    s.wait(act, "t_done", r * KC + t + 1)
                    act.activation(xo[:, t, 0:full * P], side[:, :], ACT.Copy).then_inc(s["xo_ready"], 1)
                if f == OUT_AT + full:
                    s.wait(act, "t_done", r * KC + KC)
                    act.activation(xo[:, :, full * P:D], side[:, :].rearrange("p (t c) -> p t c", t=TPB)[:, :, 0:tail], ACT.Copy
                                   ).then_inc(s["xo_ready"], 1)

            def stage(n, prev, nxt):
                for f in range(FT):
                    if f + 1 < FT:
                        gelu(n, f + 1)
                    elif nxt:
                        gelu(n + 1, 0)
                    if prev:
                        rear(n - 1, f)

            gelu(0, 0)
            stage(0, False, True)
            with act.Fori(0, NBLK - 2) as i:
                stage(i + 1, True, True)
            stage(NBLK - 1, True, False)
            for f in range(FT):
                rear(NBLK - 1, f)

        @block.tensor
        def _(pe):
            s.give(pe, "y_done", "w_done")

            def hidden(n, f, first=False):
                if f == 0:
                    s.wait(pe, "x_in", n * 48 + 48)
                if first and f % W1P == 0:
                    pe.wait_ge(w1_in[f // W1P], 16)
                if f or not first:
                    s.wait(pe, "g_ready", n * FT + f - HR + 1)
                cols = slice(f * P, (f + 1) * P)
                passes = split_passes(lambda c, k: w1h[0:k, c, cols], lambda c, k: w1l[0:k, c, cols],
                                      lambda c, k: slot(xh, n, c, k), lambda c, k: slot(xl, n, c, k))
                for x, (w, xx) in enumerate(passes):
                    last = pe.matmul(hp[f % HR][:, :], w, xx, start=(x == 0), stop=(x == len(passes) - 1))
                last.then_inc(s["h_done"], 1)

            def rear(r, f):
                if f == 0:
                    s.wait(pe, "xo_ready", r * KC)
                    s.wait(pe, "copy_ready", r + 1)
                    pe.matmul(side[0:tail, :], fold[:, :], tail_sum[:, :], start=True, stop=True).then_inc(s["fold_done"], 1)
                if f == ROT_AT:
                    s.wait(pe, "cur_ready", r + 1)
                    s.wait(pe, "x3_ready", r * KC + KC)
                    for c in range(KC):
                        last = pe.matmul(side[0:RD, :], uri[:, c, :], slot(x3, r, c, P), start=(c == 0), stop=(c == KC - 1))
                    last.then_inc(s["w_done"], 1)
                if ADD_AT <= f < ADD_AT + KC:
                    c = f - ADD_AT
                    if c == 0:
                        s.wait(pe, "wT_ready", r + 1)
                    else:
                        s.wait(pe, "o_ready", r * KC + c)
                    pe.matmul(side[:, :], UT[:, c * P:(c + 1) * P], wT[:, :], start=True, stop=True).then_inc(s["r_done"], 1)
                if OUT_AT <= f < OUT_AT + full:
                    t = f - OUT_AT
                    if t == 0:
                        s.wait(pe, "o_ready", r * KC + KC)
                    else:
                        s.wait(pe, "xo_ready", r * KC + t)
                    for c in range(full):
                        last = pe.transpose(side[:, c * P:(c + 1) * P], oT[:, c, t * P:(t + 1) * P], ident[:, :])
                    last.then_inc(s["t_done"], 1)
                if f == OUT_AT + full:
                    s.wait(pe, "xo_ready", r * KC + full)
                    for t in range(TPB):
                        last = pe.transpose(side[:, t * P:(t + 1) * P], oT[:, full, t * P:(t + 1) * P], ident[:, :])
                    last.then_inc(s["t_done"], 1)

            def stage(n, prev, nxt):
                for f in range(FT):
                    if f + 1 < FT:
                        hidden(n, f + 1, first=not prev)
                    elif nxt:
                        hidden(n + 1, 0)
                    if prev:
                        if f == 0:
                            s.wait(pe, "x3_ready", n * KC - 1)
                        rear(n - 1, f)
                    s.wait(pe, "hs_ready", n * FT + f + 1)
                    pe.wait_ge(w2_in[f % WR], n * (48 * FT // WR) + 48 * (f // WR + 1))
                    for m in range(KC):
                        cols, low = m * P, D + tail + m * P
                        passes = ((cols, P, hh), (cols, P, hl), (low, P, hh)) if m < full else ((cols, P, hh), (cols, tail, hl))
                        if m == full and f == FT - 1:
                            passes = passes[::-1]
                        for x, (c0, r, xx) in enumerate(passes):
                            last = pe.matmul(acc[0:r, m, :], w2[:, f % WR, c0:c0 + r], xx[:, f % 2, :],
                                             start=(f == 0 and x == 0), stop=(f == FT - 1 and x == len(passes) - 1))
                    last.then_inc(s["y_done"], 1)

            hidden(0, 0, first=True)
            stage(0, False, True)
            with pe.Fori(0, NBLK - 2) as i:
                stage(i + 1, True, True)
            stage(NBLK - 1, True, False)
            for f in range(FT):
                rear(NBLK - 1, f)

        @block.vector
        def _(dve):
            s.give(dve, "hs_ready")
            dve.memset(x3[tail:P, :, full, :], 0.0)
            dve.memset(oT[tail:P, full, :], 0.0)
            dve.memset(UT[:, D:KC * P], 0.0)
            dve.tensor_tensor(fold[:, :], ident[:, 0:RD], ident[:, RD:P], ALU.add)

            def split(n, f):
                s.wait(dve, "g_ready", n * FT + f + 1)
                if f or not isinstance(n, int):
                    s.wait(dve, "y_done", n * FT + f - 1)
                dve.tensor_copy(hh[:, f % 2, :], hb[:, f % 2, :]).then_inc(s["hh_ready"], 1)
                s.wait(dve, "hh_ready", n * FT + f + 1)
                dve.tensor_tensor(hl[:, f % 2, :], hb[:, f % 2, :], hh[:, f % 2, :].bitcast(F32), ALU.subtract).then_inc(s["hs_ready"], 1)

            def residual(n):
                s.wait(dve, "cur_ready", n + 1)
                s.wait(dve, "x2_in", n * 32 + 32)
                s.wait(dve, "y_done", n * FT + FT)
                for c in range(full):
                    x = slot(x3, n, c, P)
                    dve.scalar_tensor_tensor(out=x, in0=acc[:, c, :], scalar=gate[:, c:c + 1], in1=x,
                                             op0=ALU.mult, op1=ALU.add).then_inc(s["x3_ready"], 1)
                dve.tensor_copy(tail_sum[:, :], acc[:, full, :]).then_inc(s["copy_ready"], 1)

            def rear(r, f):
                if f == 0:
                    s.wait(dve, "fold_done", r + 1)
                    x = slot(x3, r, full, tail)
                    dve.scalar_tensor_tensor(out=x, in0=side[0:tail, :], scalar=gate[0:tail, full:KC], in1=x,
                                             op0=ALU.mult, op1=ALU.add).then_inc(s["x3_ready"], 1)
                if ADD_AT <= f < ADD_AT + KC:
                    c = f - ADD_AT
                    k = rows(c)
                    s.wait(dve, "r_done", r * KC + c + 1)
                    dve.tensor_tensor(oT[0:k, c, :], side[0:k, :], slot(x3, r, c, k), ALU.add).then_inc(s["o_ready"], 1)

            def stage(n, prev, nxt):
                if prev:
                    residual(n - 1)
                for f in range(FT):
                    if f + 1 < FT:
                        split(n, f + 1)
                    elif nxt:
                        split(n + 1, 0)
                    if prev:
                        rear(n - 1, f)

            split(0, 0)
            stage(0, False, True)
            with dve.Fori(0, NBLK - 2) as i:
                stage(i + 1, True, True)
            stage(NBLK - 1, True, False)
            residual(NBLK - 1)
            for f in range(FT):
                rear(NBLK - 1, f)


def program(nc, io, out, stop=None, dbg=None):
    with ExitStack() as keep:
        keep.enter_context(nc.allow_non_contiguous_dma(reason="short vectors, one value a partition"))
        sb = lambda name, shape, dt=F32: keep.enter_context(nc.sbuf_tensor(name, shape, dt))
        dram = lambda name, shape: nc.dram_tensor(name, shape, F32, kind="Internal").ap()
        g = {
            "ident": sb("ident", [P, P]),
            "modv": sb("modv", [P, B, SECTIONS, KC]),
            "UT": sb("UT", [RD, KC * P]),
            "URI": sb("URI", [P, B, KC, RD]),
            "w1_hi": dram("w1_hi_scratch", [D, HID]), "w1_lo": dram("w1_lo_scratch", [D, HID]),
            "w2_hi": dram("w2_hi_scratch", [HID, D]), "w2_lo": dram("w2_lo_scratch", [HID, D]),
            "wp_hi": dram("wp_hi_scratch", [D, D]), "wp_lo": dram("wp_lo_scratch", [D, D]),
            "xs_hi": dram("xs_hi_scratch", [NBLK, P, KC, BLK]), "xs_lo": dram("xs_lo_scratch", [NBLK, P, KC, BLK]),
            "x2T": dram("x2T_scratch", [NBLK, P, KC, BLK]),
            "skew_scratch": dram("skew_scratch", [B, SKEW + 2 * RD]),
            "attn_scratch": dram("attn_scratch", [B * T, D]),
        }
        for n in ("q_hi", "q_lo", "k_hi", "k_lo"):
            g[n] = dram(n + "_scratch", [B * D, T])
        with ExitStack() as basis:
            for n, shape in (("E", [RD, 2, B, RD]), ("G", [RD, RD]), ("M", [RD, 2 * ML]), ("step", [RD, P]), ("stepT", [RD, P]),
                             ("X2", [RD, 2, ML]), ("one", [1, 1]), ("signs", [1, RD + 1]), ("half_mask", [RD, RD])):
                g[n] = basis.enter_context(nc.sbuf_tensor("basis_" + n, shape, F32))
            with nc.sbuf_tensor("V_all", [P, NH, KT, HD], F32) as V:
                g["V"] = V
                with ExitStack() as weights:
                    for n, shape, dt in (("wqk_hi", [P, KC, 2 * D], F32R), ("wqk_lo", [P, KC, 2 * D], F32R), ("wv", [P, KC, D], F32)):
                        g[n] = weights.enter_context(nc.sbuf_tensor(n, shape, dt))
                    setup(nc, io, g)
                    if stop == "setup":
                        return dbg(nc, g)
                    qkv(nc, io, g)
                if stop == "qkv":
                    return dbg(nc, g)
                attention(nc, io, g)
        if stop == "attn":
            return dbg(nc, g)
        with nc.sbuf_tensor("w1_hi", [P, KC, HID], F32R) as w1h:
            g["w1h"] = w1h
            projection(nc, io, g)
            if stop == "proj":
                return dbg(nc, g)
            mlp(nc, io, g, out)


_INS = ["x", "cond_1152", "L0_cond_w_qkv", "L0_cond_b_qkv", "L0_cond_w_proj", "L0_cond_b_proj", "L0_cond_w_fc1",
        "L0_cond_b_fc1", "L0_cond_w_fc2", "L0_cond_b_fc2", "L0_cond_w_ada", "L0_cond_b_ada", "L1_cond_P",
        "L1_cond_W", "L1_cond_b"]


def kernel(**inputs):
    import numpy as _np
    import concourse.bacc as _bacc
    from concourse import mybir as _mybir
    from concourse.bass_utils import run_bass_kernel_spmd as _run

    nc = _bacc.Bacc("TRN2", target_bir_lowering=False, num_devices=1)
    arrays, io = {}, {}
    for name in _INS:
        a = _np.ascontiguousarray(inputs[name])
        arrays[f"in_{name}"] = a
        io[name] = nc.dram_tensor(f"in_{name}", a.shape, _mybir.dt.from_np(a.dtype), kind="ExternalInput").ap()
    out = nc.dram_tensor("out_0", (B, T, D), _mybir.dt.float32, kind="ExternalOutput").ap()
    program(nc, io, out)
    r = _run(nc, [arrays], core_ids=[0])
    return r.results[0]["out_0"]
```
